# Optimizing a Trainium2 kernel written in Bass

```python
import numpy as np
import jax
import jax.numpy as jnp

def _softmax(x, axis=-1):
    return jax.nn.softmax(x, axis=axis)

def _gelu(x):
    return jax.nn.gelu(x, approximate=True)

def _silu(x):
    return jax.nn.silu(x)

def _sigmoid(x):
    return jax.nn.sigmoid(x)

def _layernorm(x, axis=-1, eps=1e-05):
    m = jnp.mean(x, axis=axis, keepdims=True)
    v = jnp.var(x, axis=axis, keepdims=True)
    return (x - m) / jnp.sqrt(v + eps)

def _scatter_add(tgt, idx, src, axis=0):
    return tgt.at[idx].add(src)

def _segment_sum(src, seg, n):
    return jax.ops.segment_sum(src, seg, n)
kernel_name = 'mk_metaformer_d2_conv_nchw512_r4_7f288f'

def setup_inputs(seed: int=0):
    np.random.seed(seed)
    _w = jnp.asarray

    def _rec_inputs():
        import jax
        import jax.numpy as jnp
        _gk = jax.random.key(seed)
        x = -0.0003929 + 0.9999 * jax.random.normal(jax.random.fold_in(_gk, 1), (8, 128, 16, 16), jnp.float32)
        return x
    x = _rec_inputs()

    def _L0_conv_setup():
        import jax, jax.numpy as jnp
        import numpy as np
        DIM = 16
        EPS = 1e-15
        BN_EPS = 1e-05

        def _conv(x, w, groups=1):
            return jax.lax.conv_general_dilated(x, w, window_strides=(1, 1), padding='SAME', feature_group_count=groups, dimension_numbers=('NCHW', 'OIHW', 'NCHW'))
        key = jax.random.key(seed)
        ks = jax.random.split(key, 5)
        B, Cin, H, W = (8, 128, 16, 16)
        total_dim = 128
        C3 = 3 * total_dim
        x = jax.random.normal(ks[0], (B, Cin, H, W), dtype=jnp.float32)
        w_qkv = jax.random.normal(ks[1], (C3, Cin, 1, 1), dtype=jnp.float32) * 0.02
        w_dw = jax.random.normal(ks[2], (C3, 1, 5, 5), dtype=jnp.float32) * 0.02
        w_pw = jax.random.normal(ks[3], (C3, C3 // (3 * DIM), 1, 1), dtype=jnp.float32) * 0.02
        w_proj = jax.random.normal(ks[4], (128, 2 * total_dim, 1, 1), dtype=jnp.float32) * 0.02
        bn_gamma = jnp.ones((128,), jnp.float32)
        bn_beta = jnp.zeros((128,), jnp.float32)
        bn_mean = jnp.zeros((128,), jnp.float32)
        bn_var = jnp.ones((128,), jnp.float32)
        return {'x': x, 'w_qkv': w_qkv, 'w_dw': w_dw, 'w_pw': w_pw, 'w_proj': w_proj, 'bn_gamma': bn_gamma, 'bn_beta': bn_beta, 'bn_mean': bn_mean, 'bn_var': bn_var}
    _L0_conv_all = _L0_conv_setup()
    _L0_conv_in = {k: v for k, v in _L0_conv_all.items() if k in ('w_qkv', 'w_dw', 'w_pw', 'w_proj', 'bn_gamma', 'bn_beta', 'bn_mean', 'bn_var')}
    del _L0_conv_all

    def _L0_ffn_setup():
        import jax, jax.numpy as jnp
        import numpy as np
        E = 8
        TOP_K = 2
        H = 128
        DFF = 512
        B, S = (4, 512)
        key = jax.random.key(seed)
        k0, k1, k2, k3 = jax.random.split(key, 4)
        return {'hidden_states': jax.random.normal(k0, (B, S, H), jnp.float32), 'gate_w': jax.random.normal(k1, (E, H), jnp.float32) * 0.01, 'w1': jax.random.normal(k2, (E, H, DFF), jnp.float32) * (1.0 / np.sqrt(H)), 'b1': jnp.zeros((E, DFF), jnp.float32), 'w2': jax.random.normal(k3, (E, DFF, H), jnp.float32) * (1.0 / np.sqrt(DFF)), 'b2': jnp.zeros((E, H), jnp.float32)}
    _L0_ffn_all = _L0_ffn_setup()
    _L0_ffn_in = {k: v for k, v in _L0_ffn_all.items() if k in ('gate_w', 'w1', 'b1', 'w2', 'b2')}
    del _L0_ffn_all

    def _L1_conv_setup():
        import jax, jax.numpy as jnp
        import numpy as np
        EMBED_DIM = 128
        B, H, W = (2, 16, 16)

        def _conv1x1(x, w, b):
            return jnp.einsum('bchw,dc->bdhw', x, w) + b[None, :, None, None]
        key = jax.random.key(seed)
        ks = jax.random.split(key, 9)
        C = EMBED_DIM
        s = 1.0 / np.sqrt(C)
        x = jax.random.normal(ks[0], (B, C, H, W), dtype=jnp.float32)
        wq = jax.random.normal(ks[1], (C, C), dtype=jnp.float32) * s
        bq = jax.random.normal(ks[2], (C,), dtype=jnp.float32) * 0.01
        wk = jax.random.normal(ks[3], (C, C), dtype=jnp.float32) * s
        bk = jax.random.normal(ks[4], (C,), dtype=jnp.float32) * 0.01
        wv = jax.random.normal(ks[5], (C, C), dtype=jnp.float32) * s
        bv = jax.random.normal(ks[6], (C,), dtype=jnp.float32) * 0.01
        wo = jax.random.normal(ks[7], (C, C), dtype=jnp.float32) * s
        bo = jax.random.normal(ks[8], (C,), dtype=jnp.float32) * 0.01
        return {'x': x, 'wq': wq, 'bq': bq, 'wk': wk, 'bk': bk, 'wv': wv, 'bv': bv, 'wo': wo, 'bo': bo}
    _L1_conv_all = _L1_conv_setup()
    _L1_conv_in = {k: v for k, v in _L1_conv_all.items() if k in ('wq', 'bq', 'wk', 'bk', 'wv', 'bv', 'wo', 'bo')}
    del _L1_conv_all

    def _L1_ffn_setup():
        import jax, jax.numpy as jnp
        import numpy as np
        B, S, H, E, F, TOP_K = (4, 512, 128, 16, 256, 2)

        def _moe_forward(inputs, router_w, gate_w, up_w, down_w):
            b, s, h = inputs.shape
            x = inputs.reshape(-1, h)
            T = x.shape[0]
            router_logits = x @ router_w.T
            top_vals, top_idx = jax.lax.top_k(router_logits, TOP_K)
            weights = jax.nn.softmax(top_vals.astype(jnp.float32), axis=-1)
            combine = jnp.zeros((T, router_w.shape[0]), jnp.float32)
            combine = combine.at[jnp.arange(T)[:, None], top_idx].set(weights)

            def step(acc, ew):
                wg, wu, wd, ce = ew
                hid = jax.nn.silu(x @ wg) * (x @ wu)
                y = hid @ wd
                return (acc + ce[:, None] * y, None)
            out0 = jnp.zeros_like(x)
            out, _ = jax.lax.scan(step, out0, (gate_w, up_w, down_w, combine.T))
            return (out.reshape(b, s, h), router_logits, top_idx)
        key = jax.random.key(seed)
        k0, k1, k2, k3, k4 = jax.random.split(key, 5)
        scale = 0.02
        return {'inputs': jax.random.normal(k0, (B, S, H), dtype=jnp.float32), 'router_w': jax.random.normal(k1, (E, H), dtype=jnp.float32) * scale, 'gate_w': jax.random.normal(k2, (E, H, F), dtype=jnp.float32) * scale, 'up_w': jax.random.normal(k3, (E, H, F), dtype=jnp.float32) * scale, 'down_w': jax.random.normal(k4, (E, F, H), dtype=jnp.float32) * scale}
    _L1_ffn_all = _L1_ffn_setup()
    _L1_ffn_in = {k: v for k, v in _L1_ffn_all.items() if k in ('router_w', 'gate_w', 'up_w', 'down_w')}
    del _L1_ffn_all
    return {'x': x, 'L0_conv_w_qkv': _L0_conv_in['w_qkv'], 'L0_conv_w_dw': _L0_conv_in['w_dw'], 'L0_conv_w_pw': _L0_conv_in['w_pw'], 'L0_conv_w_proj': _L0_conv_in['w_proj'], 'L0_conv_bn_gamma': _L0_conv_in['bn_gamma'], 'L0_conv_bn_beta': _L0_conv_in['bn_beta'], 'L0_conv_bn_mean': _L0_conv_in['bn_mean'], 'L0_conv_bn_var': _L0_conv_in['bn_var'], 'L0_ffn_gate_w': _L0_ffn_in['gate_w'], 'L0_ffn_w1': _L0_ffn_in['w1'], 'L0_ffn_b1': _L0_ffn_in['b1'], 'L0_ffn_w2': _L0_ffn_in['w2'], 'L0_ffn_b2': _L0_ffn_in['b2'], 'L1_conv_wq': _L1_conv_in['wq'], 'L1_conv_bq': _L1_conv_in['bq'], 'L1_conv_wk': _L1_conv_in['wk'], 'L1_conv_bk': _L1_conv_in['bk'], 'L1_conv_wv': _L1_conv_in['wv'], 'L1_conv_bv': _L1_conv_in['bv'], 'L1_conv_wo': _L1_conv_in['wo'], 'L1_conv_bo': _L1_conv_in['bo'], 'L1_ffn_router_w': _L1_ffn_in['router_w'], 'L1_ffn_gate_w': _L1_ffn_in['gate_w'], 'L1_ffn_up_w': _L1_ffn_in['up_w'], 'L1_ffn_down_w': _L1_ffn_in['down_w']}

def reference(x, L0_conv_w_qkv, L0_conv_w_dw, L0_conv_w_pw, L0_conv_w_proj, L0_conv_bn_gamma, L0_conv_bn_beta, L0_conv_bn_mean, L0_conv_bn_var, L0_ffn_gate_w, L0_ffn_w1, L0_ffn_b1, L0_ffn_w2, L0_ffn_b2, L1_conv_wq, L1_conv_bq, L1_conv_wk, L1_conv_bk, L1_conv_wv, L1_conv_bv, L1_conv_wo, L1_conv_bo, L1_ffn_router_w, L1_ffn_gate_w, L1_ffn_up_w, L1_ffn_down_w):
    import jax
    import jax.numpy as jnp

    def _L0_conv_ref(x, w_qkv, w_dw, w_pw, w_proj, bn_gamma, bn_beta, bn_mean, bn_var):
        import jax, jax.numpy as jnp
        import numpy as np
        DIM = 16
        EPS = 1e-15
        BN_EPS = 1e-05

        def _conv(x, w, groups=1):
            return jax.lax.conv_general_dilated(x, w, window_strides=(1, 1), padding='SAME', feature_group_count=groups, dimension_numbers=('NCHW', 'OIHW', 'NCHW'))
        qkv = _conv(x, w_qkv)
        C3 = qkv.shape[1]
        agg = _conv(_conv(qkv, w_dw, groups=C3), w_pw, groups=3 * DIM)
        qkv = jnp.concatenate([qkv, agg], axis=1)
        B, _, H, W = qkv.shape
        S = H * W
        qkv = qkv.reshape(B, -1, 3 * DIM, S)
        q, k, v = jnp.split(qkv, 3, axis=2)
        q = jax.nn.relu(q)
        k = jax.nn.relu(k)
        v = jnp.concatenate([v, jnp.ones_like(v[:, :, :1])], axis=2)
        vk = jnp.einsum('bhds,bhes->bhde', v, k)
        out = jnp.einsum('bhde,bhes->bhds', vk, q)
        out = out[:, :, :-1] / (out[:, :, -1:] + EPS)
        out = out.reshape(B, -1, H, W)
        y = _conv(out, w_proj)
        inv = bn_gamma / jnp.sqrt(bn_var + BN_EPS)
        y = y * inv[:, None, None] + (bn_beta - bn_mean * inv)[:, None, None]
        return y

    def _L0_ffn_ref(hidden_states, gate_w, w1, b1, w2, b2):
        import jax, jax.numpy as jnp
        import numpy as np
        E = 8
        TOP_K = 2
        H = 128
        DFF = 512
        B, S = (4, 512)
        b, s, h = hidden_states.shape
        flat = hidden_states.reshape(-1, h)
        logits = flat @ gate_w.T
        top_vals, top_idx = jax.lax.top_k(logits, TOP_K)
        top_w = jax.nn.softmax(top_vals, axis=-1)
        combine = jnp.sum(jax.nn.one_hot(top_idx, E, dtype=flat.dtype) * top_w[..., None], axis=1)
        out = jnp.zeros_like(flat)
        for e in range(E):
            hdn = jax.nn.gelu(flat @ w1[e] + b1[e])
            out = out + combine[:, e:e + 1] * (hdn @ w2[e] + b2[e])
        return out.reshape(b, s, h)

    def _L1_conv_ref(x, wq, bq, wk, bk, wv, bv, wo, bo):
        import jax, jax.numpy as jnp
        import numpy as np
        EMBED_DIM = 128
        B, H, W = (2, 16, 16)

        def _conv1x1(x, w, b):
            return jnp.einsum('bchw,dc->bdhw', x, w) + b[None, :, None, None]
        b, c, h, w = x.shape
        n = h * w
        q = _conv1x1(x, wq, bq).reshape(b, c, n)
        k = _conv1x1(x, wk, bk).reshape(b, c, n)
        v = _conv1x1(x, wv, bv).reshape(b, c, n)
        scores = jnp.einsum('bcn,bcm->bnm', q, k) / jnp.sqrt(jnp.asarray(c, x.dtype))
        attn = jax.nn.softmax(scores, axis=-1)
        out = jnp.einsum('bcm,bnm->bcn', v, attn).reshape(b, c, h, w)
        return _conv1x1(out, wo, bo)

    def _L1_ffn_ref(inputs, router_w, gate_w, up_w, down_w):
        import jax, jax.numpy as jnp
        import numpy as np
        B, S, H, E, F, TOP_K = (4, 512, 128, 16, 256, 2)

        def _moe_forward(inputs, router_w, gate_w, up_w, down_w):
            b, s, h = inputs.shape
            x = inputs.reshape(-1, h)
            T = x.shape[0]
            router_logits = x @ router_w.T
            top_vals, top_idx = jax.lax.top_k(router_logits, TOP_K)
            weights = jax.nn.softmax(top_vals.astype(jnp.float32), axis=-1)
            combine = jnp.zeros((T, router_w.shape[0]), jnp.float32)
            combine = combine.at[jnp.arange(T)[:, None], top_idx].set(weights)

            def step(acc, ew):
                wg, wu, wd, ce = ew
                hid = jax.nn.silu(x @ wg) * (x @ wu)
                y = hid @ wd
                return (acc + ce[:, None] * y, None)
            out0 = jnp.zeros_like(x)
            out, _ = jax.lax.scan(step, out0, (gate_w, up_w, down_w, combine.T))
            return (out.reshape(b, s, h), router_logits, top_idx)
        out, router_logits, selected_experts = _moe_forward(inputs, router_w, gate_w, up_w, down_w)
        return out

    def _gn(v, G=32, eps=1e-05):
        B_, C_, H_, W_ = v.shape
        g = v.reshape(B_, G, C_ // G, H_, W_)
        m = jnp.mean(g, axis=(2, 3, 4), keepdims=True)
        s = jnp.var(g, axis=(2, 3, 4), keepdims=True)
        return ((g - m) / jnp.sqrt(s + eps)).reshape(v.shape)

    def _ln_c(v, eps=1e-06):
        m = jnp.mean(v, axis=1, keepdims=True)
        s = jnp.var(v, axis=1, keepdims=True)
        return (v - m) / jnp.sqrt(s + eps)

    def _ln_t(v, eps=1e-05):
        m = jnp.mean(v, axis=-1, keepdims=True)
        s = jnp.var(v, axis=-1, keepdims=True)
        return (v - m) / jnp.sqrt(s + eps)

    def _to_tokens(v):
        B_, C_, H_, W_ = v.shape
        return v.reshape(B_, C_, H_ * W_).transpose(0, 2, 1)

    def _from_tokens(t, like):
        B_, C_, H_, W_ = like.shape
        return t.transpose(0, 2, 1).reshape(B_, C_, H_, W_)
    x = x + _L0_conv_ref(_ln_c(x), L0_conv_w_qkv, L0_conv_w_dw, L0_conv_w_pw, L0_conv_w_proj, L0_conv_bn_gamma, L0_conv_bn_beta, L0_conv_bn_mean, L0_conv_bn_var)
    t = _to_tokens(x)
    t = t + _L0_ffn_ref(_ln_t(t), L0_ffn_gate_w, L0_ffn_w1, L0_ffn_b1, L0_ffn_w2, L0_ffn_b2)
    x = _from_tokens(t, x)
    x = x + _L1_conv_ref(_ln_c(x), L1_conv_wq, L1_conv_bq, L1_conv_wk, L1_conv_bk, L1_conv_wv, L1_conv_bv, L1_conv_wo, L1_conv_bo)
    t = _to_tokens(x)
    t = t + _L1_ffn_ref(_ln_t(t), L1_ffn_router_w, L1_ffn_gate_w, L1_ffn_up_w, L1_ffn_down_w)
    x = _from_tokens(t, x)
    return x

_drawn_inputs = setup_inputs


def setup_inputs(seed=0):
    import zlib

    import numpy as np

    out = dict(_drawn_inputs(seed))
    spreads = {'L0_conv_bn_gamma': (1.0, 0.2),
     'L0_conv_bn_beta': (0.0, 0.1),
     'L0_conv_bn_mean': (0.0, 0.1),
     'L0_conv_bn_var': (1.0, 0.2),
     'L0_ffn_b1': (0.0, 0.1),
     'L0_ffn_b2': (0.0, 0.1)}
    factors = {'L0_conv_w_dw': 8.0,
     'L0_conv_w_pw': 8.0,
     'L1_conv_bq': 8.0,
     'L1_conv_bk': 8.0,
     'L1_conv_bv': 5.885,
     'L1_conv_bo': 6.096,
     'L1_ffn_router_w': 8.0,
     'L1_ffn_gate_w': 8.0,
     'L1_ffn_up_w': 8.0,
     'L1_ffn_down_w': 8.0}
    for name, (base, spread) in spreads.items():
        noise = np.random.default_rng([zlib.crc32(name.encode()), seed]).standard_normal(out[name].shape)
        drawn = base * np.exp(spread * noise) if base else spread * noise
        out[name] = jnp.asarray(drawn.astype(out[name].dtype))
    for name, factor in factors.items():
        out[name] = (out[name] * factor).astype(out[name].dtype)
    return out
```

```python
from contextlib import ExitStack

import concourse.bass as bass
from concourse import mybir

F32 = mybir.dt.float32
F32R = mybir.dt.float32r
ALU = mybir.AluOpType
ACT = mybir.ActivationFunctionType
AX = mybir.AxisListType

C = 128
B, HW = 8, 16
S = HW * HW
T = B * S
CH = 512
NCH = T // CH
TT = T // 128
HD = 16
KS, PADW = 5, HW + 4
TAPS = KS * KS
G8 = 8
E0, F0 = 8, 512
E1, F1 = 16, 256
M0 = F0 // 128
LN_C_EPS, LN_T_EPS, BN_EPS, DIV_EPS = 1e-6, 1e-5, 1e-5, 1e-15
ATT_SCALE = float(C) ** -0.5
MASKED = -1e30


def metaformer(nc, x, w_qkv, w_dw, w_pw, w_proj, bn_gamma, bn_beta, bn_mean, bn_var,
               gate_w, w1, b1, w2, b2, wq, bq, wk, bk, wv, bv, wo, bo,
               router_w, gate_ws, up_ws, down_ws, out):
    x_v = x.rearrange("b c h w -> c b (h w)")
    out_v = out.rearrange("b c h w -> c b (h w)")
    comb_dram = [nc.dram_tensor(f"comb{r}", (E, T), F32, kind="Internal").ap()
                 for r, E in enumerate((E0, E1))]

    ctx = ExitStack()
    with ctx:
        def sb(name, shape, dt=F32, own=ctx):
            return own.enter_context(nc.sbuf_tensor(name, shape, dt))

        def sem(name):
            return ctx.enter_context(nc.semaphore(name))

        bank = [ctx.enter_context(nc.psum_tensor(f"bank{i}", [128, CH], F32)) for i in range(8)]

        ident = sb("ident", [128, 128])
        mean_w = sb("mean_w", [128, 128])
        blk8 = sb("blk8", [128, 128])
        blk16 = sb("blk16", [128, 128])
        one = sb("one", [128, 1])
        rank = sb("rank", [128, E1])
        eps = sb("eps", [128, 3])
        NW = 11
        wraw = sb("wraw", [128, NW, 128])
        (W_Q, W_K, W_V, W_P0, W_P1, W_AQ, W_AK, W_AV, W_AO, W_SM, W_B1) = range(NW)
        NT = 14
        wT = sb("wT", [128, NT, 128])
        (PW0,) = (11,)
        pw_raw = sb("pw_raw", [128, 3, G8])
        pw_bd = sb("pw_bd", [128, 3, 128])
        dw = sb("dw", [128, 3, TAPS])
        SM = {n: i for i, n in enumerate(
            ["gamma", "beta", "mean", "var", "bq", "bk", "bv", "bo"])}
        ROUT0, ROUT1 = 8, 8 + E0
        SMROWS = ROUT1 + E1
        bn = sb("bn", [128, 4])
        b2_sb = sb("b2_sb", [E0, 128])
        b1_pair = sb("b1_pair", [128, 2 * M0])

        def vec(name):
            return wT[:, W_SM, SM[name]:SM[name] + 1]

        xs = sb("xs", [128, T])
        xc = sb("xc", [128, T])
        xn = sb("xn", [128, T])
        ln_sq = sb("ln_sq", [128, T])
        ln_std = ln_sq

        rt = [sb(f"rt{i}", [128, TT, E1]) for i in range(6)]
        rcomb = sb("rcomb", [128, E1, TT])
        rv = sb("rv", [128, 8, TT])
        combT = sb("combT", [128, 2, 128])

        conv_ctx = ExitStack()
        pad_hi = [sb(f"pad_hi{r}", [128, B, PADW, PADW], F32R, conv_ctx) for r in range(2)]
        pad_lo = [sb(f"pad_lo{r}", [128, B, PADW, PADW], F32R, conv_ctx) for r in range(2)]
        cw_full = sb("cw_full", [128, TAPS, 128], F32, conv_ctx)
        cw_hi = [sb(f"cw_hi{r}", [128, TAPS, 128], F32R, conv_ctx) for r in range(1)]
        cw_lo = [sb(f"cw_lo{r}", [128, TAPS, 128], F32R, conv_ctx) for r in range(1)]
        kvT = sb("kvT", [128, 2, 4, 132], F32, conv_ctx)
        kvm = sb("kvm", [128, 2, 2, 128], F32, conv_ctx)
        den = sb("den", [128, 2, 2, S], F32, conv_ctx)
        heads = [[sb(f"head{h}{t}", [128, T], F32, conv_ctx) for t in range(3)] for h in range(2)]
        att = heads
        conv_ctx.close()
        moe_ctx = ExitStack()
        WC = 2 * F0
        wr = [sb(f"wr{r}", [128, WC], F32, moe_ctx) for r in range(2)]
        wh = [sb(f"wh{r}", [128, WC], F32R, moe_ctx) for r in range(2)]
        wl = [sb(f"wl{r}", [128, WC], F32R, moe_ctx) for r in range(2)]
        ce = [sb(f"ce{r}", [128, T], F32, moe_ctx) for r in range(2)]
        comb_e = sb("comb_e", [E0, T], F32, moe_ctx)
        mid_ctx = ExitStack()
        sq_q = sb("sq_q", [128, T], F32, mid_ctx)
        sq_k = sb("sq_k", [128, T], F32, mid_ctx)
        sq_vT = sb("sq_vT", [128, TT, 128], F32, mid_ctx)
        sq_p = sb("sq_p", [128, 2, 2, S], F32, mid_ctx)
        sq_pn = sb("sq_pn", [128, 2, 2, S], F32, mid_ctx)
        sq_pT = sb("sq_pT", [128, 2, 2, S], F32, mid_ctx)
        sq_st = sb("sq_st", [128, 2, 4, 2], F32, mid_ctx)
        sq_o = sb("sq_o", [128, B, S], F32, mid_ctx)
        mid_ctx.close()
        h32 = sb("h32", [128, 4, CH], F32, moe_ctx)
        sg = sb("sg", [128, 2, CH], F32, moe_ctx)
        hh = sb("hh", [128, 4, CH], F32R, moe_ctx)
        hl = sb("hl", [128, 4, CH], F32R, moe_ctx)
        ytmp = sb("ytmp", [128, 4, CH], F32, moe_ctx)
        xh = sb("xh", [128, T], F32R, moe_ctx)
        xl = sb("xl", [128, T], F32R, moe_ctx)
        moe_ctx.close()

        x_in = [sem(f"x_in{c}") for c in range(NCH)]
        w_in = sem("w_in")
        consts = sem("consts")
        pw_built = sem("pw_built")
        w_turned = sem("w_turned")
        w_ready = sem("w_ready")
        bn_step = sem("bn_step")
        ln_mean, ln_cent, ln_sqd = sem("ln_mean"), sem("ln_cent"), sem("ln_sqd")
        ln_var, ln_root, ln_inv, ln_out = sem("ln_var"), sem("ln_root"), sem("ln_inv"), sem("ln_out")
        qkv_mm, head_a, padded_hi, padded_lo = sem("qkv_mm"), sem("head_a"), sem("padded_hi"), sem("padded_lo")
        pads_zero = sem("pads_zero")
        cw_step = sem("cw_step")
        conv_mm, head_b = sem("conv_mm"), sem("head_b")
        kv_turned, kv_copied, kv_mm, kv_masked = sem("kv_turned"), sem("kv_copied"), sem("kv_mm"), sem("kv_masked")
        nd_mm, den_step, att_out = sem("nd_mm"), sem("den_step"), sem("att_out")
        proj_mm, x1_ready = sem("proj_mm"), sem("x1_ready")
        rt_mm, rt_chain, rt_diff, rt_exp, rt_comb = (sem("rt_mm"), sem("rt_chain"), sem("rt_diff"), sem("rt_exp"),
                                                     sem("rt_comb"))
        rt_turned, rt_copied = sem("rt_turned"), sem("rt_copied")
        comb_out, comb_e_in = [sem("comb_out0"), sem("comb_out1")], sem("comb_e_in")
        xh_ready, xl_ready = sem("xh_ready"), sem("xl_ready")
        b1_here = sem("b1_here")
        b2_mm, b2_added = sem("b2_mm"), sem("b2_added")

        class Moe:
            def __init__(m, n):
                m.w_in = [sem(f"m{n}_w_in{r}") for r in range(2)]
                m.ce_in = [sem(f"m{n}_ce_in{r}") for r in range(2)]
                m.w_split = sem(f"m{n}_w_split")
                m.up = sem(f"m{n}_up")
                m.act = sem(f"m{n}_act")
                m.h = sem(f"m{n}_h")
                m.hi, m.lo = sem(f"m{n}_hi"), sem(f"m{n}_lo")
                m.down = sem(f"m{n}_down")
                m.scaled = sem(f"m{n}_scaled")
                m.added = sem(f"m{n}_added")
        moe = [Moe(0), Moe(1)]
        sq_qk_mm, sq_qk_out, sq_v_mm, sq_v_out = sem("sq_qk_mm"), sem("sq_qk_out"), sem("sq_v_mm"), sem("sq_v_out")
        sq_s, sq_max, sq_nmax, sq_exp, sq_inv, sq_norm = (sem("sq_s"), sem("sq_max"), sem("sq_nmax"),
                                                          sem("sq_exp"), sem("sq_inv"), sem("sq_norm"))
        sq_turned, sq_copied, sq_mm, sq_out = sem("sq_turned"), sem("sq_copied"), sem("sq_mm"), sem("sq_out")
        wo_mm, x3_ready = sem("wo_mm"), sem("x3_ready")
        stored = sem("stored")

        block = ctx.enter_context(nc.Block())

        def chunk(t, c, n=CH):
            return t[:, c * n:(c + 1) * n]

        def f(ap):
            return ap.bitcast(F32)

        STEPS0 = 2 * M0
        STEPS1 = 2 * NCH
        PAIR = 2

        @block.sync
        def _(sp):
            for c in range(NCH):
                sp.dma_start(xs[:, c * CH:(c + 1) * CH].rearrange("p (b s) -> p b s", b=2),
                             x_v[:, 2 * c:2 * c + 2, :]).then_inc(x_in[c], 16)

            def comb_store(r, E):
                g = E * TT // 128
                sp.wait_ge(rt_copied, r + 1)
                sp.dma_start(comb_dram[r].rearrange("e (t q) -> (e t) q", q=128)
                             .rearrange("(g p) q -> p g q", p=128),
                             combT[:, 0:g, :]).then_inc(comb_out[r], 16)
                sp.wait_ge(comb_out[r], 16)

            def ce_load(m, r, e, slot):
                sp.dma_start(ce[slot][:, :], comb_dram[r][bass.ds(e, 1), :].broadcast_to([128, T]))\
                    .then_inc(m.ce_in[slot], 16)

            def moe_loads(r, E, units):
                m = moe[r]

                def weights(e, slot):
                    if r == 0:
                        sp.dma_start(wr[slot][:, 0:F0], w1[bass.ds(e, 1), :, :].rearrange("e c f -> (e c) f"))\
                          .then_inc(m.w_in[slot], 16)
                        sp.dma_start(wr[slot][:, F0:2 * F0].rearrange("p (k h) -> p k h", k=M0),
                                     w2[bass.ds(e, 1), :, :].rearrange("e (k p) h -> p (e k) h", p=128))\
                          .then_inc(m.w_in[slot], 16)
                    else:
                        sp.dma_start(wr[slot][:, 0:F1], gate_ws[bass.ds(e, 1), :, :].rearrange("e c f -> (e c) f"))\
                          .then_inc(m.w_in[slot], 16)
                        sp.dma_start(wr[slot][:, F1:2 * F1], up_ws[bass.ds(e, 1), :, :].rearrange("e c f -> (e c) f"))\
                          .then_inc(m.w_in[slot], 16)
                        sp.dma_start(wr[slot][:, 2 * F1:3 * F1].rearrange("p (k h) -> p k h", k=2),
                                     down_ws[bass.ds(e, 1), :, :].rearrange("e (k p) h -> p (e k) h", p=128))\
                          .then_inc(m.w_in[slot], 16)

                if r == 0:
                    sp.wait_ge(conv_mm, 3 * NCH)
                    sp.wait_ge(cw_step, 9)
                else:
                    sp.wait_ge(moe[0].w_split, 2 * E0)
                for e in range(PAIR):
                    weights(e, e)
                comb_store(r, E)
                if r == 0:
                    sp.dma_start(comb_e[:, :], comb_dram[0]).then_inc(comb_e_in, 16)
                for e in range(PAIR):
                    ce_load(m, r, e, e)
                with sp.Fori(1, E // PAIR) as it:
                    for k in range(PAIR):
                        sp.wait_ge(m.w_split, (it - 1) * (2 * PAIR) + 2 * (k + 1))
                        weights(it * PAIR + k, k)
                        sp.wait_ge(m.scaled, (it - 1) * (PAIR * units) + units * (k + 1))
                        ce_load(m, r, it * PAIR + k, k)

            moe_loads(0, E0, 2)
            moe_loads(1, E1, NCH)
            for c in range(NCH):
                sp.wait_ge(moe[1].added, (E1 - 1) * NCH + c + 1)
                sp.dma_start(out_v[:, 2 * c:2 * c + 2, :],
                             xs[:, c * CH:(c + 1) * CH].rearrange("p (b s) -> p b s", b=2)).then_inc(stored, 16)
            sp.wait_ge(stored, 16 * NCH)

        NLOADS = 3 + 6 + 1 + 8 + 2 + 4 + 1 + 1

        @block.gpsimd
        def _(pool):
            pool.memset(ident[:, :], 0.0).then_inc(consts, 1)
            pool.memset(blk8[:, :], 1.0).then_inc(consts, 1)
            pool.memset(blk16[:, :], 1.0).then_inc(consts, 1)
            pool.memset(mean_w[:, :], 1.0 / C).then_inc(consts, 1)
            for i, v in enumerate((LN_C_EPS, LN_T_EPS, BN_EPS)):
                pool.memset(eps[:, i:i + 1], v).then_inc(consts, 1)
            pool.wait_ge(consts, 7)
            pool.affine_select(out=ident[:, :], in_=ident[:, :], compare_op=ALU.not_equal, fill=1.0,
                               base=0, pattern=[[-1, 128]], channel_multiplier=1).then_inc(consts, 1)
            for blk, n in ((blk8, G8), (blk16, HD)):
                v = blk[:, :].rearrange("p (g i) -> p g i", i=n)
                pool.affine_select(out=v, in_=v, compare_op=ALU.is_ge, fill=0.0, base=0,
                                   pattern=[[-n, 128 // n], [0, n]], channel_multiplier=1).then_inc(consts, 1)
            pool.wait_ge(consts, 10)
            for blk, n in ((blk8, G8), (blk16, HD)):
                v = blk[:, :].rearrange("p (g i) -> p g i", i=n)
                pool.affine_select(out=v, in_=v, compare_op=ALU.is_ge, fill=0.0, base=n - 1,
                                   pattern=[[n, 128 // n], [0, n]], channel_multiplier=-1).then_inc(consts, 1)
            pool.wait_ge(consts, 12)
            pool.wait_ge(w_in, 16 * NLOADS)
            for t in range(3):
                pool.tensor_tensor(pw_bd[:, t, :].rearrange("p (g i) -> p g i", i=G8),
                                   pw_raw[:, t, :].unsqueeze(1).broadcast_to([128, 128 // G8, G8]),
                                   blk8[:, :].rearrange("p (g i) -> p g i", i=G8), ALU.mult)\
                    .then_inc(pw_built, 1)
            pool.memset(one[:, :], 1.0).then_inc(consts, 1)
            for e in range(E1):
                pool.memset(rank[:, e:e + 1], float(E1 - e)).then_inc(consts, 1)
            pool.memset(kvT[:, :, :, 128:129], 1.0).then_inc(pads_zero, 1)
            for t in (pad_hi[0], pad_lo[0], pad_hi[1], pad_lo[1]):
                pool.memset(f(t[:, :, :, :]), 0.0).then_inc(pads_zero, 1)

            def conv_weights(t):
                if t >= 1:
                    pool.wait_ge(conv_mm, NCH * t)
                pool.tensor_tensor(cw_full[:, :, :],
                                   wT[:, PW0 + t, :].unsqueeze(1).broadcast_to([128, TAPS, 128]),
                                   dw[:, t, :].unsqueeze(2).broadcast_to([128, TAPS, 128]),
                                   ALU.mult).then_inc(cw_step, 1)
                pool.wait_ge(cw_step, 3 * t + 1)
                pool.tensor_copy(cw_hi[0][:, :, :], cw_full[:, :, :]).then_inc(cw_step, 1)
                pool.wait_ge(cw_step, 3 * t + 2)
                pool.tensor_tensor(cw_lo[0][:, :, :], cw_full[:, :, :], f(cw_hi[0][:, :, :]),
                                   ALU.subtract).then_inc(cw_step, 1)

            pool.wait_ge(w_ready, 6)
            for t in range(3):
                conv_weights(t)

            def moe_pool(r, E, units, cols):
                m = moe[r]

                def split(e_done, slot, first):
                    nld = 2 if r == 0 else 3
                    pool.wait_ge(m.w_in[slot], (e_done + 1) * (16 * nld))
                    if not first:
                        pool.wait_ge(m.down, (e_done - 1) * (PAIR * steps) + steps * (slot + 1))
                    pool.tensor_tensor(wh[slot][:, 0:cols], wr[slot][:, 0:cols],
                                       one[:, :].broadcast_to([128, cols]), ALU.mult).then_inc(m.w_split, 1)
                    pool.wait_ge(m.w_split, e_done * (2 * PAIR) + 2 * slot + 1)
                    pool.tensor_tensor(wl[slot][:, 0:cols], wr[slot][:, 0:cols], f(wh[slot][:, 0:cols]),
                                       ALU.subtract).then_inc(m.w_split, 1)

                def add(it, k, u):
                    n = T // units
                    pool.wait_ge(m.scaled, it * (PAIR * units) + k * units + u + 1)
                    w = n // CH
                    pool.tensor_tensor(chunk(xs, u, n), chunk(xs, u, n),
                                       ytmp[:, u * w:(u + 1) * w, :].rearrange("p a b -> p (a b)"),
                                       ALU.add).then_inc(m.added, 1)

                steps = STEPS0 if r == 0 else STEPS1
                if r == 1:
                    pool.wait_ge(xl_ready, 2 * NCH)
                for k in range(PAIR):
                    split(0, k, True)

                def pair_body(it, last):
                    for k in range(PAIR):
                        for u in range(units):
                            add(it, k, u)
                        if not last:
                            split(it + 1, k, False)
                with pool.Fori(0, E // PAIR - 1) as it:
                    pair_body(it, False)
                pair_body(E // PAIR - 1, True)

            moe_pool(0, E0, 2, 2 * F0)
            moe_pool(1, E1, NCH, 3 * F1)

        @block.scalar
        def _(act):
            def load(dst, src):
                act.dma_start(dst, src).then_inc(w_in, 16)

            def tile_rows(w):
                return w.rearrange("(h t d) k -> t h d k", t=3, d=HD)

            qkv_rows = tile_rows(w_qkv.rearrange("o i h w -> o (i h w)"))
            pw_rows = tile_rows(w_pw.rearrange("o i h w -> o (i h w)"))
            dw_rows = tile_rows(w_dw.rearrange("o i h w -> o (i h w)"))
            load(wraw[:, W_Q, :], qkv_rows[0])
            load(wraw[:, W_K, :], qkv_rows[1])
            load(wraw[:, W_V, :], qkv_rows[2])
            for t in range(3):
                load(pw_raw[:, t, :], pw_rows[t])
                load(dw[:, t, :], dw_rows[t])
            load(wraw[:, W_P0:W_P1 + 1, :], w_proj.rearrange("o (a i) h w -> o a (i h w)", a=2))
            for i, v in enumerate((bn_gamma, bn_beta, bn_mean, bn_var, bq, bk, bv, bo)):
                load(wraw[i:i + 1, W_SM, :], v.rearrange("(a n) -> a n", a=1))
            load(wraw[ROUT0:ROUT0 + E0, W_SM, :], gate_w)
            load(wraw[ROUT1:ROUT1 + E1, W_SM, :], router_w)
            for i, v in ((W_AQ, wq), (W_AK, wk), (W_AV, wv), (W_AO, wo)):
                load(wraw[:, i, :], v)
            load(wraw[0:E0 * M0, W_B1, :], b1.rearrange("e (k p) -> (e k) p", p=128))
            load(b2_sb[:, :], b2)

            def ln_roots(n, e):
                for c in range(NCH):
                    act.wait_ge(ln_cent, NCH * n + c + 1)
                    act.activation(chunk(ln_sq, c), chunk(xc, c), ACT.Square).then_inc(ln_sqd, 1)
                for c in range(NCH):
                    act.wait_ge(ln_var, NCH * n + c + 1)
                    act.activation(chunk(ln_std, c), bank[4 + c][:, :], ACT.Sqrt,
                                   bias=eps[:, e:e + 1]).then_inc(ln_root, 1)

            def inner(t, c):
                return t[:, 2 * c:2 * c + 2, 2:2 + HW, 2:2 + HW]

            def image(t):
                return t.rearrange("p (b h w) -> p b h w", b=2, h=HW)

            act.wait_ge(consts, 12)
            act.wait_ge(w_ready, 6)
            act.activation(bn[:, 0:1], vec("var"), ACT.Sqrt, bias=eps[:, 2:3]).then_inc(bn_step, 1)
            ln_roots(0, 0)

            def qkv_out(t):
                for c in range(NCH):
                    act.wait_ge(qkv_mm, NCH * t + c + 1)
                    act.activation(chunk(heads[0][t], c), bank[4 + c][:, :],
                                   ACT.Relu if t < 2 else ACT.Copy).then_inc(head_a, 1)
                    if t == 0 and c == 0:
                        act.wait_ge(pads_zero, 5)
                    if t == 2:
                        act.wait_ge(conv_mm, NCH)
                    act.activation(inner(pad_hi[t % 2], c), image(bank[4 + c][:, :]),
                                   ACT.Copy).then_inc(padded_hi, 1)

            def conv_out(t):
                for c in range(NCH):
                    act.wait_ge(conv_mm, NCH * t + c + 1)
                    act.activation(chunk(heads[1][t], c), bank[c][:, :],
                                   ACT.Relu if t < 2 else ACT.Copy).then_inc(head_b, 1)

            qkv_out(0)
            qkv_out(1)
            conv_out(0)
            qkv_out(2)
            conv_out(1)
            conv_out(2)

            for i in range(2 * B):
                act.wait_ge(kv_turned, i + 1)
                if i >= 2:
                    act.wait_ge(kv_mm, i - 1)
                act.activation(kvT[:, i % 2, :, 0:128],
                               bank[i % 2][:, :].rearrange("p (j q) -> p j q", j=4),
                               ACT.Copy).then_inc(kv_copied, 1)

            def router_exp(r):
                act.wait_ge(rt_diff, r + 1)
                act.activation(rv[:, 3, :], rv[:, 2, :], ACT.Exp).then_inc(rt_exp, 1)
                act.wait_ge(rt_turned, r + 1)
                g = (E0, E1)[r] * TT // 128
                act.activation(combT[:, 0:g, :], bank[1][:, 0:g * 128].rearrange("p (g q) -> p g q", g=g),
                               ACT.Copy).then_inc(rt_copied, 1)

            def split_x(r):
                for c in range(NCH):
                    act.wait_ge(ln_out, NCH * (2 * r + 1) + c + 1)
                    if r == 0 and c == 0:
                        act.wait_ge(cw_step, 9)
                    act.activation(chunk(xh, c), chunk(xn, c), ACT.Copy).then_inc(xh_ready, 1)

            ln_roots(1, 1)
            split_x(0)
            router_exp(0)

            m = moe[0]
            n = 2

            def ring0(t, s):
                return t[:, 2 * (s % n):2 * (s % n) + 2, :]

            def gelu_body(it, first):
                src = wT[:, W_B1, 0:PAIR * M0] if first else wT[:, W_B1, bass.ds(it * (PAIR * M0), PAIR * M0)]
                act.activation(b1_pair[:, :], src, ACT.Copy).then_inc(b1_here, 1)
                act.wait_ge(b1_here, it + 1)
                for s in range(PAIR * STEPS0):
                    g = it * (PAIR * STEPS0) + s
                    act.wait_ge(m.up, g + 1)
                    if not (first and s < 2):
                        act.wait_ge(m.lo, g - 1)
                    col = (s // STEPS0) * M0 + s % M0
                    for j in range(2):
                        a = act.activation(h32[:, 2 * (s % 2) + j, :], bank[2 * (s % 2) + j][:, :],
                                           ACT.Gelu_apprx_tanh, bias=b1_pair[:, col:col + 1])
                        if j == 1:
                            a.then_inc(m.act, 1)
                    act.wait_ge(m.act, g + 1)
                    if not (first and s < 2):
                        act.wait_ge(m.down, g - 1)
                    act.activation(ring0(hh, s), ring0(h32, s), ACT.Copy).then_inc(m.hi, 1)

            gelu_body(0, True)
            with act.Fori(1, E0 // PAIR) as it:
                gelu_body(it, False)

            ln_roots(2, 0)
            for c in range(NCH):
                for j, (dst, b) in enumerate(((sq_q, "bq"), (sq_k, "bk"))):
                    act.wait_ge(sq_qk_mm, 2 * c + j + 1)
                    act.activation(chunk(dst, c), bank[2 * j + c % 2][:, :], ACT.Identity,
                                   bias=vec(b)).then_inc(sq_qk_out, 1)
            for i in range(B + 1):
                if i < B:
                    act.wait_ge(sq_max, i + 1)
                    act.activation(sq_st[:, i % 2, 1, :], sq_st[:, i % 2, 0, :], ACT.Copy,
                                   scale=-ATT_SCALE).then_inc(sq_nmax, 1)
                    act.wait_ge(sq_nmax, i + 1)
                    if i >= 2:
                        act.wait_ge(sq_norm, 2 * (i - 1))
                    for j in range(2):
                        act.activation(sq_p[:, i % 2, j, :], bank[i % 2][:, j * S:(j + 1) * S], ACT.Exp,
                                       bias=sq_st[:, i % 2, 1, j:j + 1], scale=ATT_SCALE,
                                       accum_out=sq_st[:, i % 2, 2, j:j + 1]).then_inc(sq_exp, 1)
                if i >= 1:
                    k = i - 1
                    act.wait_ge(sq_turned, k + 1)
                    if k >= 2:
                        act.wait_ge(sq_mm, k - 1)
                    act.activation(sq_pT[:, k % 2, :, :],
                                   bank[2 + k % 2][:, :].rearrange("p (m n) -> p m n", m=2),
                                   ACT.Copy).then_inc(sq_copied, 1)

            ln_roots(3, 1)
            split_x(1)
            router_exp(1)

            m1 = moe[1]

            def silu(g, s, first):
                act.wait_ge(m1.up, g + 1)
                if not (first and s < 2):
                    act.wait_ge(m1.h, g - 1)
                act.activation(sg[:, s % 2, :], bank[s % 2][:, :], ACT.Silu).then_inc(m1.act, 1)

            def high(g, s, first):
                act.wait_ge(m1.h, g + 1)
                if not (first and s < 4):
                    act.wait_ge(m1.down, g - 3)
                act.activation(hh[:, s % 4, :], h32[:, s % 4, :], ACT.Copy).then_inc(m1.hi, 1)

            def silu_body(it, first):
                base = it * (PAIR * STEPS1)
                for s in range(PAIR * STEPS1):
                    silu(base + s, s, first)
                    if not (first and s < 1):
                        high(base + (s - 1), s - 1, first)

            silu_body(0, True)
            with act.Fori(1, E1 // PAIR) as it:
                silu_body(it, False)
            high(E1 * STEPS1 - 1, -1, False)

        @block.vector
        def _(dve):
            dve.wait_ge(w_turned, 1)
            for g in range(2):
                dve.tensor_copy(wT[:, 4 * g:4 * g + 4, :],
                                bank[g][:, :].rearrange("p (j q) -> p j q", q=128)).then_inc(w_ready, 1)
            dve.tensor_copy(wT[:, W_AO, :], bank[2][:, 0:128]).then_inc(w_ready, 1)
            dve.tensor_copy(wT[:, W_SM, 0:SMROWS], bank[2][:, 128:128 + SMROWS]).then_inc(w_ready, 1)
            dve.tensor_copy(wT[:, W_B1, 0:E0 * M0], bank[2][:, 256:256 + E0 * M0]).then_inc(w_ready, 1)
            dve.tensor_copy(wT[:, PW0:PW0 + 3, :], bank[3][:, 0:384].rearrange("p (j q) -> p j q", q=128))\
                .then_inc(w_ready, 1)

            def ln_center(n, src_ready):
                for c in range(NCH):
                    dve.wait_ge(ln_mean, NCH * n + c + 1)
                    dve.tensor_tensor(chunk(xc, c), chunk(xs, c), bank[c][:, :], ALU.subtract)\
                        .then_inc(ln_cent, 1)

            def ln_scale(n):
                for c in range(NCH):
                    dve.wait_ge(ln_root, NCH * n + c + 1)
                    dve.reciprocal(chunk(ln_std, c), chunk(ln_std, c)).then_inc(ln_inv, 1)
                    dve.wait_ge(ln_inv, NCH * n + c + 1)
                    dve.tensor_tensor(chunk(xn, c), chunk(xc, c), chunk(ln_std, c), ALU.mult)\
                        .then_inc(ln_out, 1)

            ln_center(0, None)
            ln_scale(0)

            dve.wait_ge(bn_step, 1)
            dve.reciprocal(bn[:, 1:2], bn[:, 0:1]).then_inc(bn_step, 1)
            dve.wait_ge(bn_step, 2)
            dve.tensor_tensor(bn[:, 2:3], vec("gamma"), bn[:, 1:2], ALU.mult).then_inc(bn_step, 1)
            dve.wait_ge(bn_step, 3)
            dve.tensor_tensor(bn[:, 3:4], vec("mean"), bn[:, 2:3], ALU.mult).then_inc(bn_step, 1)
            dve.wait_ge(bn_step, 4)
            dve.tensor_tensor(bn[:, 3:4], vec("beta"), bn[:, 3:4], ALU.subtract).then_inc(bn_step, 1)
            dve.wait_ge(bn_step, 5)
            dve.tensor_scalar(xs[:, :], xs[:, :], bn[:, 3:4], None, ALU.add).then_inc(bn_step, 1)

            for t in range(3):
                for c in range(NCH):
                    dve.wait_ge(padded_hi, NCH * t + c + 1)
                    dve.tensor_tensor(pad_lo[t % 2][:, 2 * c:2 * c + 2, 2:2 + HW, 2:2 + HW],
                                      bank[4 + c][:, :].rearrange("p (b h w) -> p b h w", b=2, h=HW),
                                      f(pad_hi[t % 2][:, 2 * c:2 * c + 2, 2:2 + HW, 2:2 + HW]),
                                      ALU.subtract).then_inc(padded_lo, 1)

            for i in range(2 * B + 1):
                if i < 2 * B:
                    dve.wait_ge(kv_mm, i + 1)
                    if i >= 2:
                        dve.wait_ge(nd_mm, i - 1)
                    kv = bank[2 + i % 2]
                    dve.tensor_tensor(kvm[:, i % 2, 0, :], kv[:, 0:128], blk16[:, :], ALU.mult)
                    dve.tensor_scalar(kvm[:, i % 2, 1, :], blk16[:, :], kv[:, 128:129], None, ALU.mult)\
                        .then_inc(kv_masked, 1)
                if i >= 1:
                    k = i - 1
                    h, b = k // B, k % B
                    nd = bank[4 + k % 2]
                    d0, d1 = den[:, k % 2, 0, :], den[:, k % 2, 1, :]
                    dve.wait_ge(nd_mm, k + 1)
                    dve.tensor_scalar(d0, nd[:, S:2 * S], DIV_EPS, None, ALU.add).then_inc(den_step, 1)
                    dve.wait_ge(den_step, 2 * k + 1)
                    dve.reciprocal(d1, d0).then_inc(den_step, 1)
                    dve.wait_ge(den_step, 2 * k + 2)
                    dve.tensor_tensor(att[h][0][:, b * S:(b + 1) * S], nd[:, 0:S], d1, ALU.mult)\
                        .then_inc(att_out, 1)
            for c in range(NCH):
                dve.wait_ge(proj_mm, c + 1)
                if c == 0:
                    dve.wait_ge(bn_step, 6)
                dve.scalar_tensor_tensor(out=chunk(xs, c), in0=bank[6 + c % 2][:, :], scalar=bn[:, 2:3],
                                         in1=chunk(xs, c), op0=ALU.mult, op1=ALU.add).then_inc(x1_ready, 1)

            def low_x(r):
                for c in range(NCH):
                    dve.wait_ge(xh_ready, NCH * r + c + 1)
                    dve.tensor_tensor(chunk(xl, c), chunk(xn, c), f(chunk(xh, c)), ALU.subtract)\
                        .then_inc(xl_ready, 1)

            CHAIN = 17

            def router(r, E):
                lg, eq, oh1, l2, oh2, sc = (t[:, :, 0:E] for t in rt)
                m1, m2, d, ex = (rv[:, i, :] for i in range(4))
                mx, sm, w1_, w2_ = (rv[:, i, :] for i in range(4, 8))
                base = CHAIN * r
                n = [0]

                def step(ins):
                    n[0] += 1
                    ins.then_inc(rt_chain, 1)
                    dve.wait_ge(rt_chain, base + n[0])

                def per_e(v):
                    return v.unsqueeze(2).broadcast_to([128, TT, E])

                rk = rank[:, 0:E].unsqueeze(1).broadcast_to([128, TT, E])
                dve.wait_ge(rt_mm, r + 1)
                step(dve.tensor_copy(lg, bank[0][:, 0:TT * E].rearrange("p (t e) -> p t e", e=E)))
                for src, top, oh in ((lg, m1, oh1), (l2, m2, oh2)):
                    step(dve.tensor_reduce(top, src, AX.X, ALU.max))
                    step(dve.tensor_tensor(eq, src, per_e(top), ALU.is_equal))
                    step(dve.tensor_tensor(sc, eq, rk, ALU.mult))
                    step(dve.tensor_reduce(mx, sc, AX.X, ALU.max))
                    step(dve.tensor_tensor(oh, sc, per_e(mx), ALU.is_equal))
                    if src is lg:
                        step(dve.scalar_tensor_tensor(out=l2, in0=oh1, scalar=MASKED, in1=lg,
                                                      op0=ALU.mult, op1=ALU.add))
                dve.tensor_tensor(d, m2, m1, ALU.subtract).then_inc(rt_diff, 1)
                dve.wait_ge(rt_exp, r + 1)
                step(dve.tensor_scalar(sm, ex, 1.0, None, ALU.add))
                step(dve.reciprocal(w1_, sm))
                step(dve.tensor_tensor(w2_, ex, w1_, ALU.mult))
                step(dve.tensor_tensor(oh1, oh1, per_e(w1_), ALU.mult))
                dve.tensor_tensor(oh2, oh2, per_e(w2_), ALU.mult).then_inc(rt_chain, 1)
                dve.wait_ge(rt_chain, base + n[0] + 1)
                dve.tensor_tensor(rcomb[:, 0:E, :].rearrange("p e t -> p t e"), oh1, oh2, ALU.add)\
                    .then_inc(rt_comb, 1)
                assert n[0] + 1 == CHAIN

            ln_center(1, x1_ready)
            ln_scale(1)
            router(0, E0)
            low_x(0)

            for c in range(NCH):
                dve.wait_ge(b2_mm, c + 1)
                dve.tensor_tensor(chunk(xs, c), chunk(xs, c), bank[4 + c][:, :], ALU.add).then_inc(b2_added, 1)

            def low(m, g, slot):
                dve.wait_ge(m.hi, g + 1)
                dve.tensor_tensor(hl[:, slot, :], h32[:, slot, :], f(hh[:, slot, :]), ALU.subtract)\
                    .then_inc(m.lo, 1)

            m0 = moe[0]

            def scale0(it, k, u, first):
                g = it * (PAIR * 2) + k * 2 + u
                dve.wait_ge(m0.down, (g + 1) * M0)
                dve.wait_ge(m0.ce_in[k], it * 16 + 16)
                if not (first and k == 0):
                    dve.wait_ge(m0.added, g - 1)
                for j in range(2):
                    y = dve.tensor_tensor(ytmp[:, 2 * u + j, :], bank[4 + 2 * u + j][:, :],
                                          ce[k][:, (2 * u + j) * CH:(2 * u + j + 1) * CH], ALU.mult)
                y.then_inc(m0.scaled, 1)

            def low_body0(it, first):
                for s in range(PAIR * STEPS0):
                    g = it * (PAIR * STEPS0) + s
                    low(m0, g, slice(2 * (s % 2), 2 * (s % 2) + 2))
                    if s % M0 == 1 and not (first and s < M0):
                        p = (s // M0 - 1) % (2 * PAIR)
                        scale0(it if s >= M0 else it - 1, p // 2, p % 2, first and s >= M0)

            low_body0(0, True)
            with dve.Fori(1, E0 // PAIR) as it:
                low_body0(it, False)
            scale0(E0 // PAIR - 1, 1, 1, False)

            ln_center(2, None)
            ln_scale(2)
            for g in range(4):
                dve.wait_ge(sq_v_mm, g + 1)
                dve.tensor_copy(sq_vT[:, 4 * g:4 * g + 4, :],
                                bank[4 + g][:, :].rearrange("p (j q) -> p j q", j=4)).then_inc(sq_v_out, 1)
            for i in range(B + 2):
                if i < B:
                    dve.wait_ge(sq_s, i + 1)
                    dve.tensor_reduce(sq_st[:, i % 2, 0, :], bank[i % 2][:, :].rearrange("p (j m) -> p j m", j=2),
                                      AX.X, ALU.max).then_inc(sq_max, 1)
                if 1 <= i <= B:
                    k = i - 1
                    dve.wait_ge(sq_exp, 2 * k + 2)
                    dve.reciprocal(sq_st[:, k % 2, 3, :], sq_st[:, k % 2, 2, :]).then_inc(sq_inv, 1)
                    dve.wait_ge(sq_inv, k + 1)
                    if k >= 2:
                        dve.wait_ge(sq_turned, k - 1)
                    for j in range(2):
                        dve.tensor_scalar(sq_pn[:, k % 2, j, :], sq_p[:, k % 2, j, :],
                                          sq_st[:, k % 2, 3, j:j + 1], None, ALU.mult).then_inc(sq_norm, 1)
                if i >= 2:
                    k = i - 2
                    dve.wait_ge(sq_mm, k + 1)
                    dve.tensor_scalar(sq_o[:, k, :], bank[4 + k % 2][:, 0:S], vec("bv"), None, ALU.add)\
                        .then_inc(sq_out, 1)
            for c in range(NCH):
                dve.wait_ge(wo_mm, c + 1)
                dve.scalar_tensor_tensor(out=chunk(xs, c), in0=bank[6 + c % 2][:, :], scalar=vec("bo"),
                                         in1=chunk(xs, c), op0=ALU.add, op1=ALU.add).then_inc(x3_ready, 1)

            ln_center(3, x3_ready)
            ln_scale(3)
            router(1, E1)
            low_x(1)

            m1 = moe[1]

            def gated(g, s, first):
                dve.wait_ge(m1.act, g + 1)
                if not (first and s < 4):
                    dve.wait_ge(m1.hi, g - 3)
                dve.tensor_tensor(h32[:, s % 4, :], sg[:, s % 2, :], bank[2 + s % 2][:, :], ALU.mult)\
                    .then_inc(m1.h, 1)

            def scale1(it, k, u, first):
                g = it * (PAIR * NCH) + k * NCH + u
                dve.wait_ge(m1.down, (g + 1) * 2)
                dve.wait_ge(m1.ce_in[k], it * 16 + 16)
                if not (first and k == 0):
                    dve.wait_ge(m1.added, g - 3)
                dve.tensor_tensor(ytmp[:, u, :], bank[4 + u][:, :], chunk(ce[k], u), ALU.mult)\
                    .then_inc(m1.scaled, 1)

            LAG1 = 4

            def gated_body(it, first):
                base = it * (PAIR * STEPS1)
                for s in range(PAIR * STEPS1):
                    gated(base + s, s, first)
                    if not (first and s < 1):
                        low(m1, base + (s - 1), (s - 1) % 4)
                    if s % 2 == 0 and not (first and s < LAG1):
                        p = ((s - LAG1) // 2) % (PAIR * NCH)
                        scale1(it if s >= LAG1 else it - 1, p // NCH, p % NCH, first and s >= LAG1)

            gated_body(0, True)
            with dve.Fori(1, E1 // PAIR) as it:
                gated_body(it, False)
            low(m1, E1 * STEPS1 - 1, 3)
            for p in range(PAIR * NCH - LAG1 // 2, PAIR * NCH):
                scale1(E1 // PAIR - 1, p // NCH, p % NCH, False)

        @block.tensor
        def _(pe):
            pe.wait_ge(consts, 12)
            pe.wait_ge(w_in, 16 * NLOADS)
            for i in range(9):
                pe.transpose(bank[i // 4][:, (i % 4) * 128:(i % 4 + 1) * 128], wraw[:, i, :], ident[:, :])
            pe.transpose(bank[2][:, 128:128 + SMROWS], wraw[0:SMROWS, W_SM, :], ident[0:SMROWS, 0:SMROWS])
            pe.transpose(bank[2][:, 256:256 + E0 * M0], wraw[0:E0 * M0, W_B1, :],
                         ident[0:E0 * M0, 0:E0 * M0])
            pe.wait_ge(pw_built, 3)
            for t in range(3):
                mm = pe.transpose(bank[3][:, t * 128:(t + 1) * 128], pw_bd[:, t, :], ident[:, :])
            mm.then_inc(w_turned, 1)

            def layer_norm(n, ready):
                for c in range(NCH):
                    pe.wait_ge(*ready(c))
                    pe.matmul(bank[c][:, :], mean_w[:, :], chunk(xs, c), start=True, stop=True)\
                        .then_inc(ln_mean, 1)
                for c in range(NCH):
                    pe.wait_ge(ln_sqd, NCH * n + c + 1)
                    pe.matmul(bank[4 + c][:, :], mean_w[:, :], chunk(ln_sq, c), start=True, stop=True)\
                        .then_inc(ln_var, 1)

            pe.wait_ge(w_ready, 6)
            layer_norm(0, lambda c: (x_in[c], 16))

            def qkv(t):
                for c in range(NCH):
                    pe.wait_ge(ln_out, c + 1)
                    if t >= 1:
                        pe.wait_ge(padded_lo, NCH * (t - 1) + c + 1)
                    pe.matmul(bank[4 + c][:, :], wT[:, W_Q + t, :], chunk(xn, c), start=True, stop=True)\
                        .then_inc(qkv_mm, 1)

            def conv(t):
                pe.wait_ge(cw_step, 3 * (t + 1))
                for c in range(NCH):
                    pe.wait_ge(padded_lo, NCH * t + c + 1)
                    if t >= 1:
                        pe.wait_ge(head_b, NCH * (t - 1) + c + 1)
                    for tap in range(TAPS):
                        dy, dx = tap // KS, tap % KS

                        def win(p):
                            return p[t % 2][:, 2 * c:2 * c + 2, dy:dy + HW, dx:dx + HW]
                        for n, (w, p) in enumerate(((cw_hi, pad_hi), (cw_hi, pad_lo), (cw_lo, pad_hi))):
                            mm = pe.matmul(bank[c][:, :].rearrange("p (b h w) -> p b h w", b=2, h=HW),
                                           w[0][:, tap, :], win(p),
                                           start=(tap == 0 and n == 0), stop=(tap == TAPS - 1 and n == 2))
                    mm.then_inc(conv_mm, 1)

            qkv(0)
            qkv(1)
            conv(0)
            qkv(2)
            conv(1)
            conv(2)

            def turn_kv(i):
                h, b = i // B, i % B
                pe.wait_ge(head_b, 3 * NCH)
                if i >= 2:
                    pe.wait_ge(kv_copied, i - 1)
                for j in range(4):
                    src = heads[h][1 + j // 2][:, b * S + (j % 2) * 128:b * S + (j % 2 + 1) * 128]
                    mm = pe.transpose(bank[i % 2][:, j * 128:(j + 1) * 128], src, ident[:, :])
                mm.then_inc(kv_turned, 1)

            def kv_product(i):
                pe.wait_ge(kv_copied, i + 1)
                if i >= 2:
                    pe.wait_ge(kv_masked, i - 1)
                for j in range(2):
                    mm = pe.matmul(bank[2 + i % 2][:, 0:129], kvT[:, i % 2, j, 0:128],
                                   kvT[:, i % 2, 2 + j, 0:129], start=(j == 0), stop=(j == 1))
                mm.then_inc(kv_mm, 1)

            def num_den(i):
                h, b = i // B, i % B
                pe.wait_ge(kv_masked, i + 1)
                if i >= 2:
                    pe.wait_ge(att_out, i - 1)
                for j in range(2):
                    mm = pe.matmul(bank[4 + i % 2][:, j * S:(j + 1) * S], kvm[:, i % 2, j, :],
                                   heads[h][0][:, b * S:(b + 1) * S], start=True, stop=True)
                mm.then_inc(nd_mm, 1)

            for i in range(2 * B + 2):
                if i < 2 * B:
                    turn_kv(i)
                if 1 <= i <= 2 * B:
                    kv_product(i - 1)
                if i >= 2:
                    num_den(i - 2)
            for c in range(NCH):
                pe.wait_ge(att_out, B + 2 * c + 2)
                if c >= 2:
                    pe.wait_ge(x1_ready, c - 1)
                for h in range(2):
                    mm = pe.matmul(bank[6 + c % 2][:, :], wT[:, W_P0 + h, :], chunk(att[h][0], c),
                                   start=(h == 0), stop=(h == 1))
                mm.then_inc(proj_mm, 1)
            layer_norm(1, lambda c: (x1_ready, c + 1))

            def router(r, E, row):
                pe.wait_ge(ln_out, NCH * (2 * r + 2))
                for i in range(TT):
                    mm = pe.matmul(bank[0][:, i * E:(i + 1) * E], xn[:, i * 128:(i + 1) * 128],
                                   wT[:, W_SM, row:row + E], start=True, stop=True)
                mm.then_inc(rt_mm, 1)

            def turn_comb(r, E):
                pe.wait_ge(rt_comb, r + 1)
                g = E * TT // 128
                for j in range(g):
                    mm = pe.transpose(bank[1][:, j * 128:(j + 1) * 128],
                                      rcomb[:, j * 8:(j + 1) * 8, :].rearrange("p e t -> p (e t)"), ident[:, :])
                mm.then_inc(rt_turned, 1)

            PASSES = ((wh, xh), (wh, xl), (wl, xh))

            router(0, E0, ROUT0)
            turn_comb(0, E0)

            m0 = moe[0]

            def up0(it, s, first):
                g = it * (PAIR * STEPS0) + s
                k, half, m = s // STEPS0, (s // M0) % 2, s % M0
                if s % STEPS0 == 0:
                    pe.wait_ge(m0.w_split, it * (2 * PAIR) + 2 * (k + 1))
                if not (first and s < 2):
                    pe.wait_ge(m0.act, g - 1)
                for j in range(2):
                    c = 2 * half + j
                    for n, (w, v) in enumerate(PASSES):
                        mm = pe.matmul(bank[2 * (s % 2) + j][:, :], w[k][:, m * 128:(m + 1) * 128],
                                       chunk(v, c), start=(n == 0), stop=(n == 2))
                mm.then_inc(m0.up, 1)

            def down0(it, s, first):
                g = it * (PAIR * STEPS0) + s
                k, half, m = s // STEPS0, (s // M0) % 2, s % M0
                pe.wait_ge(m0.lo, g + 1)
                if m == 0 and not (first and s < 2 * M0):
                    pe.wait_ge(m0.scaled, it * (PAIR * 2) + (s // M0 - 1))
                for j in range(2):
                    for n, (w, v) in enumerate(((wh, hh), (wh, hl), (wl, hh))):
                        mm = pe.matmul(bank[4 + 2 * half + j][:, :],
                                       w[k][:, F0 + m * 128:F0 + (m + 1) * 128],
                                       v[:, 2 * (s % 2) + j, :], start=(m == 0 and n == 0),
                                       stop=(m == M0 - 1 and n == 2))
                mm.then_inc(m0.down, 1)

            def body0(it, first):
                for s in range(PAIR * STEPS0):
                    up0(it, s, first)
                    if first and s == 1:
                        add_b2()
                    if s >= 2:
                        down0(it, s - 2, first)
                    elif not first:
                        down0(it - 1, s - 2 + PAIR * STEPS0, False)

            def add_b2():
                pe.wait_ge(comb_e_in, 16)
                for c in range(NCH):
                    pe.matmul(bank[4 + c][:, :], b2_sb[:, :], chunk(comb_e, c), start=True, stop=True)\
                        .then_inc(b2_mm, 1)
                pe.wait_ge(b2_added, NCH)

            pe.wait_ge(xl_ready, NCH)
            pe.wait_ge(rt_copied, 1)
            body0(0, True)
            with pe.Fori(1, E0 // PAIR) as it:
                body0(it, False)
            for s in (PAIR * STEPS0 - 2, PAIR * STEPS0 - 1):
                down0(E0 // PAIR - 1, s, False)

            layer_norm(2, lambda c: (m0.added, 2 * E0 - 1 + c // 2))
            for c in range(NCH):
                pe.wait_ge(ln_out, 2 * NCH + c + 1)
                for j in range(2):
                    if c >= 2:
                        pe.wait_ge(sq_qk_out, 2 * (c - 2) + j + 1)
                    pe.matmul(bank[2 * j + c % 2][:, :], wT[:, W_AQ + j, :], chunk(xn, c),
                              start=True, stop=True).then_inc(sq_qk_mm, 1)
            for g in range(4):
                for j in range(4):
                    i = 4 * g + j
                    mm = pe.matmul(bank[4 + g][:, j * 128:(j + 1) * 128], xn[:, i * 128:(i + 1) * 128],
                                   wT[:, W_AV, :], start=True, stop=True)
                mm.then_inc(sq_v_mm, 1)

            def scores(b):
                if b == 0:
                    pe.wait_ge(sq_qk_out, 2 * NCH)
                if b >= 2:
                    pe.wait_ge(sq_exp, 2 * (b - 1))
                for j in range(2):
                    mm = pe.matmul(bank[b % 2][:, j * S:(j + 1) * S],
                                   sq_q[:, b * S + j * 128:b * S + (j + 1) * 128],
                                   sq_k[:, b * S:(b + 1) * S], start=True, stop=True)
                mm.then_inc(sq_s, 1)

            def turn_p(b):
                pe.wait_ge(sq_norm, 2 * (b + 1))
                if b >= 2:
                    pe.wait_ge(sq_copied, b - 1)
                for j in range(2):
                    for m in range(2):
                        mm = pe.transpose(bank[2 + b % 2][:, m * S + j * 128:m * S + (j + 1) * 128],
                                          sq_pn[:, b % 2, j, m * 128:(m + 1) * 128], ident[:, :])
                mm.then_inc(sq_turned, 1)

            def weigh_v(b):
                pe.wait_ge(sq_copied, b + 1)
                if b == 0:
                    pe.wait_ge(sq_v_out, 4)
                if b >= 2:
                    pe.wait_ge(sq_out, b - 1)
                for m in range(2):
                    mm = pe.matmul(bank[4 + b % 2][:, 0:S], sq_vT[:, 2 * b + m, :], sq_pT[:, b % 2, m, :],
                                   start=(m == 0), stop=(m == 1))
                mm.then_inc(sq_mm, 1)

            for i in range(B + 2):
                if i < B:
                    scores(i)
                if 1 <= i <= B:
                    turn_p(i - 1)
                if i >= 2:
                    weigh_v(i - 2)
            for c in range(NCH):
                pe.wait_ge(sq_out, 2 * c + 2)
                if c >= 2:
                    pe.wait_ge(x3_ready, c - 1)
                pe.matmul(bank[6 + c % 2][:, :], wT[:, W_AO, :],
                          sq_o[:, 2 * c:2 * c + 2, :].rearrange("p b s -> p (b s)"), start=True, stop=True)\
                    .then_inc(wo_mm, 1)
            layer_norm(3, lambda c: (x3_ready, c + 1))
            router(1, E1, ROUT1)
            turn_comb(1, E1)

            m1 = moe[1]
            LAG = 3

            def up1(it, s, first):
                g = it * (PAIR * STEPS1) + s
                k, c, m = s // STEPS1, (s // 2) % NCH, s % 2
                if s % STEPS1 == 0:
                    pe.wait_ge(m1.w_split, it * (2 * PAIR) + 2 * (k + 1))
                if not (first and s < 2):
                    pe.wait_ge(m1.h, g - 1)
                for j in range(2):
                    for n, (w, v) in enumerate(PASSES):
                        mm = pe.matmul(bank[2 * j + s % 2][:, :],
                                       w[k][:, j * F1 + m * 128:j * F1 + (m + 1) * 128],
                                       chunk(v, c), start=(n == 0), stop=(n == 2))
                mm.then_inc(m1.up, 1)

            def down1(it, s, first):
                g = it * (PAIR * STEPS1) + s
                k, c, m = s // STEPS1, (s // 2) % NCH, s % 2
                pe.wait_ge(m1.lo, g + 1)
                if m == 0 and not (first and s < STEPS1):
                    pe.wait_ge(m1.scaled, it * (PAIR * NCH) + (s // 2 - NCH + 1))
                for n, (w, v) in enumerate(((wh, hh), (wh, hl), (wl, hh))):
                    mm = pe.matmul(bank[4 + c][:, :], w[k][:, 2 * F1 + m * 128:2 * F1 + (m + 1) * 128],
                                   v[:, s % 4, :], start=(m == 0 and n == 0), stop=(m == 1 and n == 2))
                mm.then_inc(m1.down, 1)

            def body1(it, first):
                for s in range(PAIR * STEPS1):
                    up1(it, s, first)
                    if s >= LAG:
                        down1(it, s - LAG, first)
                    elif not first:
                        down1(it - 1, s - LAG + PAIR * STEPS1, False)

            pe.wait_ge(xl_ready, 2 * NCH)
            pe.wait_ge(rt_copied, 2)
            body1(0, True)
            with pe.Fori(1, E1 // PAIR) as it:
                body1(it, False)
            for s in range(PAIR * STEPS1 - LAG, PAIR * STEPS1):
                down1(E1 // PAIR - 1, s, False)


_INS = ['x', 'L0_conv_w_qkv', 'L0_conv_w_dw', 'L0_conv_w_pw', 'L0_conv_w_proj', 'L0_conv_bn_gamma',
        'L0_conv_bn_beta', 'L0_conv_bn_mean', 'L0_conv_bn_var', 'L0_ffn_gate_w', 'L0_ffn_w1', 'L0_ffn_b1',
        'L0_ffn_w2', 'L0_ffn_b2', 'L1_conv_wq', 'L1_conv_bq', 'L1_conv_wk', 'L1_conv_bk', 'L1_conv_wv',
        'L1_conv_bv', 'L1_conv_wo', 'L1_conv_bo', 'L1_ffn_router_w', 'L1_ffn_gate_w', 'L1_ffn_up_w',
        'L1_ffn_down_w']


def kernel(**inputs):
    import numpy as _np
    import concourse.bacc as _bacc
    from concourse import mybir as _mybir
    from concourse.bass_utils import run_bass_kernel_spmd as _run

    nc = _bacc.Bacc("TRN2", target_bir_lowering=False, num_devices=1)
    arrays, args = {}, []
    for name in _INS:
        a = _np.ascontiguousarray(inputs[name])
        arrays[f"in_{name}_dram"] = a
        args.append(nc.dram_tensor(f"in_{name}_dram", a.shape, _mybir.dt.from_np(a.dtype), kind="ExternalInput").ap())
    args.append(nc.dram_tensor("out_dram", (B, C, HW, HW), F32, kind="ExternalOutput").ap())
    metaformer(nc, *args)
    r = _run(nc, [arrays], core_ids=[0])
    return r.results[0]["out_dram"]
```

```python
from contextlib import ExitStack

import concourse.bass as bass
from concourse import mybir

F32 = mybir.dt.float32
I32 = mybir.dt.int32
ALU = mybir.AluOpType
ACT = mybir.ActivationFunctionType
AX = mybir.AxisListType

C = 128
B, HW = 8, 16
S = HW * HW
T = B * S
CH = 512
NCH = T // CH
TT = T // 128
HD = 16
KS = 5
PADH = HW + KS - 1
G8 = 8
NG = 3 * C // G8
GT = C // G8
NH = C // HD
GU = 4
UPT = GT // GU
ORDER = (1, 2, 0)
UNITS = [(t, v) for t in ORDER for v in range(UPT)]
CWR = 3
E0, F0 = 8, 512
E1, F1 = 16, 256
M0 = F0 // 128
LN_C_EPS, LN_T_EPS, BN_EPS, DIV_EPS = 1e-6, 1e-5, 1e-5, 1e-15
UNR = 4


def block_count(experts):
    most = (2 * T - experts) // 128 + experts
    return -(-most // UNR) * UNR


NB0, NB1 = block_count(E0), block_count(E1)
ATT_SCALE = float(C) ** -0.5
V_BANKS = (6, 7, 2, 3)
MASKED = -1e30


def metaformer(nc, x, w_qkv, w_dw, w_pw, w_proj, bn_gamma, bn_beta, bn_mean, bn_var,
               gate_w, w1, b1, w2, b2, wq, bq, wk, bk, wv, bv, wo, bo,
               router_w, gate_ws, up_ws, down_ws, out):
    x_v = x.rearrange("b c h w -> c b (h w)")
    out_v = out.rearrange("b c h w -> c b (h w)")
    tok_dram = [nc.dram_tensor(f"tok{r}", (T, C), F32, kind="Internal").ap() for r in range(2)]
    y_dram = [nc.dram_tensor(f"y{r}", (2 * T + NB * 128, C), F32, kind="Internal").ap()
              for r, NB in enumerate((NB0, NB1))]

    ctx = ExitStack()
    with ctx:
        def sb(name, shape, dt=F32, own=ctx):
            return own.enter_context(nc.sbuf_tensor(name, shape, dt))

        def sem(name):
            return ctx.enter_context(nc.semaphore(name))

        bank = [ctx.enter_context(nc.psum_tensor(f"bank{i}", [128, CH], F32)) for i in range(8)]

        ident = sb("ident", [128, 128])
        mean_w = sb("mean_w", [128, 128])
        ones = sb("ones", [128, 128])
        before = sb("before", [128, 128])
        iota = sb("iota", [128, 128])
        pair_id = sb("pair_id", [128, 2, TT])
        spare = sb("spare", [128, 2, NB1])
        blk16 = sb("blk16", [128, 128])
        rank = sb("rank", [128, E1])
        eps = sb("eps", [128, 3])
        (W_Q, W_K, W_V, W_P0, W_P1, W_AQ, W_AK, W_AV, W_AO, W_SM) = range(10)
        wT = sb("wT", [128, 10, 128])
        SM = {n: i for i, n in enumerate(
            ["gamma", "beta", "mean", "var", "bq", "bk", "bv", "bo"])}
        ROUT0, ROUT1 = 8, 8 + E0
        SMROWS = ROUT1 + E1
        bn = sb("bn", [128, 4])

        def vec(name):
            return wT[:, W_SM, SM[name]:SM[name] + 1]

        xs = sb("xs", [128, T])
        xc = sb("xc", [128, T])
        xn = sb("xn", [128, T])
        ln_sq = sb("ln_sq", [128, T])
        ln_r = sb("ln_r", [128, 2, TT])
        ln_diag = sb("ln_diag", [128, 2, 4, 128])
        att = [xc, ln_sq]

        rt = [sb(f"rt{i}", [128, TT, E1]) for i in range(5)]
        rv = sb("rv", [128, 8, TT])
        SCAN = 8
        tsum = [sb(f"tsum{i}", [128, SCAN + TT, E1]) for i in range(2)]
        bsum = [sb(f"bsum{i}", [128, SCAN + E1]) for i in range(2)]
        rcnt = sb("rcnt", [128, 2, E1], I32)
        slot_f = sb("slot_f", [128, 2, TT])
        slot_i = sb("slot_i", [128, 3, 2, TT], I32)
        place = sb("place", [128, 2, 2, TT])
        pair_w = sb("pair_w", [128, 2, TT])
        dest = [sb(f"dest{r}", [128, NB], I32) for r, NB in enumerate((NB0, NB1))]
        token = [sb(f"token{r}", [128, NB], I32) for r, NB in enumerate((NB0, NB1))]
        slot_w = [sb(f"slot_w{r}", [128, NB]) for r, NB in enumerate((NB0, NB1))]
        expert = [sb(f"expert{r}", [128, NB], I32) for r, NB in enumerate((NB0, NB1))]
        ended = sb("ended", [128, NB1])
        taken = sb("taken", [128, NB1])

        conv_ctx = ExitStack()
        cmap = sb("cmap", [128, 3, GT, PADH * B], F32, conv_ctx)
        cw = sb("cw", [128, CWR, GU, KS, 128], F32, conv_ctx)
        conv_out = sb("conv_out", [128, 2, GU, HW * B], F32, conv_ctx)
        dw_band = sb("dw_band", [128, KS, NG, HW], F32, conv_ctx)
        pw_in = sb("pw_in", [128, G8, NG], F32, conv_ctx)
        heads_raw = [sb(f"heads{t}", [128, HW, HW, B], F32, conv_ctx) for t in range(3)]
        q_relu = sb("q_relu", [128, HW, HW, B], F32, conv_ctx)
        kvT = sb("kvT", [128, 2, 4, 132], F32, conv_ctx)
        kvm = sb("kvm", [128, 2, 128 + NH], F32, conv_ctx)
        den = sb("den", [128, 2, 2, 2, NH], F32, conv_ctx)
        att_rows = sb("att_rows", [128, 2, 2, 128], F32, conv_ctx)
        wraw = sb("wraw", [128, 10, 128], F32, conv_ctx)
        dw_raw = sb("dw_raw", [NG, G8, KS, KS], F32, conv_ctx)
        pw_raw = sb("pw_raw", [NG, G8, G8], F32, conv_ctx)
        dw_t = sb("dw_t", [G8 * KS, KS, NG], F32, conv_ctx)
        pw_t = sb("pw_t", [G8, G8, NG], F32, conv_ctx)
        band = sb("band", [G8 * KS, HW, G8, HW], F32, conv_ctx)
        dw_row = sb("dw_row", [NG, KS, G8, KS], F32, conv_ctx)
        spread = sb("spread", [G8, G8, HW], F32, conv_ctx)
        conv_ctx.close()

        moe_ctx = ExitStack()
        mid_ctx = ExitStack()
        sq_q = sb("sq_q", [128, T], F32, mid_ctx)
        sq_k = sb("sq_k", [128, T], F32, mid_ctx)
        sq_vT = sb("sq_vT", [128, TT, 128], F32, mid_ctx)
        sq_p = sb("sq_p", [128, 2, 2, S], F32, mid_ctx)
        sq_pn = sb("sq_pn", [128, 2, 2, S], F32, mid_ctx)
        sq_pT = sb("sq_pT", [128, 2, 2, S], F32, mid_ctx)
        sq_st = sb("sq_st", [128, 2, 4, 2], F32, mid_ctx)
        sq_o = sb("sq_o", [128, B, S], F32, mid_ctx)
        mid_ctx.close()
        w_up0 = sb("w_up0", [128, E0 * F0], F32, moe_ctx)
        w_down0 = sb("w_down0", [128, E0 * M0 * C], F32, moe_ctx)
        b1_all = sb("b1_all", [128, E0 * F0], F32, moe_ctx)
        b2_all = sb("b2_all", [128, E0 * C], F32, moe_ctx)
        place_hot = sb("place_hot", [128, 2 * TT, 128], F32, moe_ctx)
        block_hot = sb("block_hot", [128, 2 * TT, NB1], F32, moe_ctx)
        block_val = sb("block_val", [128, 2 * TT, 2 * NB1], F32, moe_ctx)
        x_rows = sb("x_rows", [128, UNR, C], F32, moe_ctx)
        x_cols = sb("x_cols", [128, 2, 128], F32, moe_ctx)
        h_in = sb("h_in", [128, 2, F0], F32, moe_ctx)
        h_rows = sb("h_rows", [128, 2, F0], F32, moe_ctx)
        h_cols = sb("h_cols", [128, 2, F0], F32, moe_ctx)
        y_rows = sb("y_rows", [128, UNR, C], F32, moe_ctx)
        w_up1 = sb("w_up1", [128, E1 * 2 * F1], F32, moe_ctx)
        w_down1 = sb("w_down1", [128, E1 * 2 * C], F32, moe_ctx)
        moe_ctx.close()

        x_in = [sem(f"x_in{c}") for c in range(NCH)]
        w_in = sem("w_in")
        consts = sem("consts")
        w_turned = sem("w_turned")
        w_ready = sem("w_ready")
        bn_step = sem("bn_step")
        ln_mean, ln_cent, ln_sqd = sem("ln_mean"), sem("ln_cent"), sem("ln_sqd")
        ln_spread = sem("ln_spread")
        ln_var, ln_root, ln_inv, ln_out = sem("ln_var"), sem("ln_root"), sem("ln_inv"), sem("ln_out")
        tables = sem("tables")
        qkv_mm, head_a, q_relued = sem("qkv_mm"), sem("head_a"), sem("q_relued")
        edges_zero = sem("edges_zero")
        dw_rows_in = sem("dw_rows_in")
        map_in = [sem(f"map_in{t}") for t in range(3)]
        band_mm, band_out = sem("band_mm"), sem("band_out")
        cw_built, conv_mm, conv_copied = sem("cw_built"), sem("conv_mm"), sem("conv_copied")
        conv_sent = [sem(f"conv_sent{i}") for i in range(2)]
        kv_turned, kv_copied, kv_mm, kv_masked = sem("kv_turned"), sem("kv_copied"), sem("kv_mm"), sem("kv_masked")
        nd_mm, den_step, att_div = sem("nd_mm"), sem("den_step"), sem("att_div")
        att_turned, att_out = sem("att_turned"), sem("att_out")
        proj_mm, x1_ready = sem("proj_mm"), sem("x1_ready")
        rt_mm, rt_chain, rt_diff, rt_exp = sem("rt_mm"), sem("rt_chain"), sem("rt_diff"), sem("rt_exp")
        rt_mask, rt_prefix, rt_place, rt_value = sem("rt_mask"), sem("rt_prefix"), sem("rt_place"), sem("rt_value")
        rt_inverse, rt_table = sem("rt_inverse"), sem("rt_table")
        rows_mm, rows_copied = sem("rows_mm"), sem("rows_copied")
        rows_out = [sem("rows_out0"), sem("rows_out1")]
        moe_w = [sem("moe_w0"), sem("moe_w1")]
        y_in = [sem(f"y_in{c}") for c in range(NCH)]
        y_added, y_turned, x_moe = sem("y_added"), sem("y_turned"), sem("x_moe")

        class Moe:
            def __init__(m, n):
                m.gathered = [sem(f"m{n}_gathered{i}") for i in range(UNR)]
                m.scattered = [sem(f"m{n}_scattered{i}") for i in range(UNR)]
                m.turned = sem(f"m{n}_turned")
                m.x_copied = sem(f"m{n}_x_copied")
                m.up = sem(f"m{n}_up")
                m.h_in = sem(f"m{n}_h_in")
                m.act = sem(f"m{n}_act")
                m.h_turned = sem(f"m{n}_h_turned")
                m.h_copied = sem(f"m{n}_h_copied")
                m.down = sem(f"m{n}_down")
                m.y_sum = sem(f"m{n}_y_sum")
                m.y = sem(f"m{n}_y")
        moe = [Moe(0), Moe(1)]
        sq_qk_mm, sq_qk_out, sq_v_mm, sq_v_out = sem("sq_qk_mm"), sem("sq_qk_out"), sem("sq_v_mm"), sem("sq_v_out")
        sq_s, sq_max, sq_nmax, sq_exp, sq_inv, sq_norm = (sem("sq_s"), sem("sq_max"), sem("sq_nmax"),
                                                          sem("sq_exp"), sem("sq_inv"), sem("sq_norm"))
        sq_turned, sq_copied, sq_mm, sq_out = sem("sq_turned"), sem("sq_copied"), sem("sq_mm"), sem("sq_out")
        wo_mm, x3_ready = sem("wo_mm"), sem("x3_ready")
        stored = sem("stored")

        block = ctx.enter_context(nc.Block())

        def chunk(t, c, n=CH):
            return t[:, c * n:(c + 1) * n]

        def in_loop(q, first):
            return not first or q >= 0

        def at(it, q):
            return (it, q) if q >= 0 else (it - 1, q + UNR)

        @block.sync
        def _(sp):
            for c in range(NCH):
                sp.dma_start(xs[:, c * CH:(c + 1) * CH].rearrange("p (b s) -> p b s", b=2),
                             x_v[:, 2 * c:2 * c + 2, :]).then_inc(x_in[c], 16)

            def rows_store(r):
                for c in range(NCH):
                    sp.wait_ge(rows_copied, NCH * r + c + 1)
                    sp.dma_start(tok_dram[r][c * CH:(c + 1) * CH, :].rearrange("(t p) c -> p t c", p=128),
                                 chunk(ln_sq, c).rearrange("p (t c) -> p t c", c=C)).then_inc(rows_out[r], 16)

            def y_load(r, NB):
                for i in range(UNR):
                    sp.wait_ge(moe[r].scattered[i], 16 * NB // UNR)
                for c in range(NCH):
                    for k, dst in enumerate((xc, ln_sq)):
                        sp.dma_start(chunk(dst, c).rearrange("p (t c) -> p t c", c=C),
                                     y_dram[r][k * T + c * CH:k * T + (c + 1) * CH, :]
                                     .rearrange("(t p) c -> p t c", p=128)).then_inc(y_in[c], 16)

            for i, v in enumerate((bn_gamma, bn_beta, bn_mean, bn_var, bq, bk, bv, bo)):
                sp.dma_start(wraw[i:i + 1, W_SM, :], v.rearrange("(a n) -> a n", a=1)).then_inc(w_in, 16)
            sp.dma_start(wraw[ROUT0:ROUT0 + E0, W_SM, :], gate_w).then_inc(w_in, 16)
            sp.dma_start(wraw[ROUT1:ROUT1 + E1, W_SM, :], router_w).then_inc(w_in, 16)
            for n, t in enumerate(ORDER):
                sp.wait_ge(head_a, NCH * (n + 1))
                sp.wait_ge(edges_zero, 6)
                for g in range(GT):
                    sp.dma_start(cmap[:, t, g, 2 * B:(2 + HW) * B],
                                 heads_raw[t][G8 * g:G8 * (g + 1), :, :, :].rearrange("p x y b -> p x (y b)"))\
                        .then_inc(map_in[t], 16)
            for u, (t, v) in enumerate(UNITS):
                sp.wait_ge(conv_copied, u + 1)
                for i in range(GU):
                    g = v * GU + i
                    sp.dma_start(heads_raw[t][G8 * g:G8 * (g + 1), :, :, :].rearrange("p x y b -> p x (y b)"),
                                 conv_out[:, u % 2, i, :]).then_inc(conv_sent[u % 2], 16)
            sp.wait_ge(conv_mm, len(UNITS))
            sp.dma_start(w_up0[:, :].rearrange("p (e f) -> p e f", e=E0), w1.rearrange("e c f -> c e f"))\
                .then_inc(moe_w[0], 16)
            sp.dma_start(w_down0[:, :].rearrange("p (e h) -> p e h", h=C), w2.rearrange("e (k p) h -> p (e k) h", p=128))\
                .then_inc(moe_w[0], 16)
            sp.wait_ge(x1_ready, NCH)
            sp.dma_start(b1_all[:, :], b1.rearrange("(a e) f -> a (e f)", a=1).broadcast_to([128, E0 * F0]))\
                .then_inc(moe_w[0], 16)
            sp.dma_start(b2_all[:, :], b2.rearrange("(a e) f -> a (e f)", a=1).broadcast_to([128, E0 * C]))\
                .then_inc(moe_w[0], 16)
            rows_store(0)
            sp.wait_ge(rows_out[0], 16 * NCH)
            w_up1_v = w_up1[:, :].rearrange("p (e g f) -> p e g f", e=E1, g=2)
            sp.dma_start(w_up1_v[:, :, 0, :], gate_ws.rearrange("e c f -> c e f")).then_inc(moe_w[1], 16)
            sp.dma_start(w_up1_v[:, :, 1, :], up_ws.rearrange("e c f -> c e f")).then_inc(moe_w[1], 16)
            sp.dma_start(w_down1[:, :].rearrange("p (e h) -> p e h", h=C), down_ws.rearrange("e (k p) h -> p (e k) h", p=128))\
                .then_inc(moe_w[1], 16)
            y_load(0, NB0)
            rows_store(1)
            y_load(1, NB1)
            for c in range(NCH):
                sp.wait_ge(x_moe, NCH + c + 1)
                sp.dma_start(out_v[:, 2 * c:2 * c + 2, :],
                             xs[:, c * CH:(c + 1) * CH].rearrange("p (b s) -> p b s", b=2)).then_inc(stored, 16)
            sp.wait_ge(stored, 16 * NCH)

        NLOADS = 3 + 2 + 1 + 8 + 2 + 4

        @block.gpsimd
        def _(pool):
            pool.memset(ident[:, :], 0.0).then_inc(consts, 1)
            pool.memset(band[:, :, :, :], 0.0).then_inc(consts, 1)
            pool.memset(spread[:, :, :], 0.0).then_inc(consts, 1)
            pool.memset(blk16[:, :], 1.0).then_inc(consts, 1)
            pool.memset(mean_w[:, :], 1.0 / C).then_inc(consts, 1)
            for i, v in enumerate((LN_C_EPS, LN_T_EPS, BN_EPS)):
                pool.memset(eps[:, i:i + 1], v).then_inc(consts, 1)
            pool.memset(ones[:, :], 1.0).then_inc(consts, 1)
            pool.memset(before[:, :], 1.0).then_inc(consts, 1)
            pool.wait_ge(consts, 10)
            pool.affine_select(out=ident[:, :], in_=ident[:, :], compare_op=ALU.not_equal, fill=1.0,
                               base=0, pattern=[[-1, 128]], channel_multiplier=1).then_inc(consts, 1)
            pool.affine_select(out=spread[:, :, :], in_=spread[:, :, :], compare_op=ALU.not_equal, fill=1.0,
                               base=0, pattern=[[-1, G8], [0, HW]], channel_multiplier=1).then_inc(consts, 1)
            edge = KS // 2
            pool.affine_select(out=band[:, :, :, :], in_=band[:, :, :, :], compare_op=ALU.not_equal, fill=1.0,
                               base=-edge, pattern=[[1, HW], [-KS, G8], [-1, HW]], channel_multiplier=1)\
                .then_inc(consts, 1)
            v = blk16[:, :].rearrange("p (g i) -> p g i", i=HD)
            pool.affine_select(out=v, in_=v, compare_op=ALU.is_ge, fill=0.0, base=0,
                               pattern=[[-HD, 128 // HD], [0, HD]], channel_multiplier=1).then_inc(consts, 1)
            pool.wait_ge(consts, 14)
            pool.affine_select(out=band[:, :, :, :], in_=band[:, :, :, :], compare_op=ALU.is_ge, fill=0.0,
                               base=edge, pattern=[[-1, HW], [0, G8], [1, HW]], channel_multiplier=0)\
                .then_inc(consts, 1)
            pool.affine_select(out=v, in_=v, compare_op=ALU.is_ge, fill=0.0, base=HD - 1,
                               pattern=[[HD, 128 // HD], [0, HD]], channel_multiplier=-1).then_inc(consts, 1)
            pool.wait_ge(consts, 16)
            pool.affine_select(out=band[:, :, :, :], in_=band[:, :, :, :], compare_op=ALU.is_ge, fill=0.0,
                               base=KS - 1 - edge, pattern=[[1, HW], [0, G8], [-1, HW]], channel_multiplier=0)\
                .then_inc(consts, 1)
            for t in range(3):
                for rows in (slice(0, 2 * B), slice((2 + HW) * B, PADH * B)):
                    pool.memset(cmap[:, t, :, rows], 0.0).then_inc(edges_zero, 1)
            pool.memset(kvT[:, :, :, 128:129], 1.0).then_inc(edges_zero, 1)
            for e in range(E1):
                pool.memset(rank[:, e:e + 1], float(E1 - e)).then_inc(consts, 1)
            pool.affine_select(out=before[:, :], in_=before[:, :], compare_op=ALU.is_gt, fill=0.0, base=0,
                               pattern=[[1, 128]], channel_multiplier=-1).then_inc(tables, 1)

            def table(out, pattern, base, step):
                pool.iota(out, pattern, base=base, channel_multiplier=step,
                          allow_small_or_imprecise_dtypes=True).then_inc(tables, 1)
            table(iota[:, :], [[1, 128]], 0, 0)
            table(pair_id[:, :, :], [[T, 2], [128, TT]], 1, 1)
            table(spare[:, 0, :], [[128, NB1]], 2 * T, 1)
            table(spare[:, 1, :], [[-128, NB1]], -(2 * T + 1), -1)
            for i in range(2):
                pool.memset(tsum[i][:, 0:SCAN, :], 0.0).then_inc(tables, 1)
                pool.memset(bsum[i][:, 0:SCAN], 0.0).then_inc(tables, 1)

            pool.wait_ge(band_out, 9)
            for u, (t, v) in enumerate(UNITS):
                if u >= CWR:
                    pool.wait_ge(conv_mm, u - CWR + 1)
                for i in range(GU):
                    gt = v * GU + i
                    g = (gt // 2) * 6 + 2 * t + gt % 2
                    pool.tensor_tensor(
                        cw[:, u % CWR, i, :, :].rearrange("p k (o x) -> p k o x", x=HW),
                        pw_in[:, :, g].unsqueeze(1).unsqueeze(3).broadcast_to([128, KS, G8, HW]),
                        dw_band[:, :, g, :].unsqueeze(2).broadcast_to([128, KS, G8, HW]),
                        ALU.mult).then_inc(cw_built, 1)

            def moe_pool(r, NB):
                m = moe[r]
                AHEAD = 3
                pool.wait_ge(rows_out[r], 16 * NCH)
                pool.wait_ge(rt_table, 4 * (r + 1))
                for j in range(-AHEAD, NB + AHEAD):
                    g, s = j + AHEAD, j - AHEAD
                    if g < NB:
                        if g >= UNR:
                            pool.wait_ge(m.turned, g - UNR + 1)
                        pool.indirect_dma_start(
                            out=x_rows[:, g % UNR, :], out_offset=None, in_=tok_dram[r],
                            in_offset=bass.IndirectOffsetOnAxis(ap=token[r][:, g:g + 1], axis=0))\
                            .then_inc(m.gathered[g % UNR], 16)
                    if s >= 0:
                        pool.wait_ge(m.y, s + 1)
                        pool.indirect_dma_start(
                            out=y_dram[r], in_=y_rows[:, s % UNR, :], in_offset=None,
                            out_offset=bass.IndirectOffsetOnAxis(ap=dest[r][:, s:s + 1], axis=0))\
                            .then_inc(m.scattered[s % UNR], 16)

            moe_pool(0, NB0)
            moe_pool(1, NB1)

        @block.scalar
        def _(act):
            def load(dst, src):
                act.dma_start(dst, src).then_inc(w_in, 16)

            def tile_rows(w):
                return w.rearrange("(h t d) k -> t h d k", t=3, d=HD)

            qkv_rows = tile_rows(w_qkv.rearrange("o i h w -> o (i h w)"))
            load(wraw[:, W_Q, :], qkv_rows[0])
            load(wraw[:, W_K, :], qkv_rows[1])
            load(wraw[:, W_V, :], qkv_rows[2])
            load(dw_raw[:, :, :, :], w_dw.rearrange("(g i) a h w -> g (i a) h w", i=G8))
            load(pw_raw[:, :, :], w_pw.rearrange("(g o) i h w -> g o (i h w)", o=G8))
            load(wraw[:, W_P0:W_P1 + 1, :], w_proj.rearrange("o (a i) h w -> o a (i h w)", a=2))
            for i, v in ((W_AQ, wq), (W_AK, wk), (W_AV, wv), (W_AO, wo)):
                load(wraw[:, i, :], v)

            def ln_roots(n, e):
                for c in range(NCH):
                    act.wait_ge(ln_cent, NCH * n + c + 1)
                    act.activation(chunk(ln_sq, c), chunk(xc, c), ACT.Square).then_inc(ln_sqd, 1)
                for c in range(NCH):
                    act.wait_ge(ln_var, NCH * n + c + 1)
                    act.activation(ln_r[:, 0, 4 * c:4 * c + 4], bank[4 + c][:, 0:4], ACT.Sqrt,
                                   bias=eps[:, e:e + 1]).then_inc(ln_root, 1)

            act.wait_ge(consts, 17)
            act.wait_ge(w_in, 16 * NLOADS)
            act.activation(dw_row[:, :, :, :].rearrange("g k i c -> g i k c"), dw_raw[:, :, :, :], ACT.Copy)\
                .then_inc(dw_rows_in, 1)
            ln_roots(0, 0)
            act.wait_ge(w_ready, 6)
            act.activation(bn[:, 0:1], vec("var"), ACT.Sqrt, bias=eps[:, 2:3]).then_inc(bn_step, 1)

            for n, t in enumerate(ORDER):
                for c in range(NCH):
                    act.wait_ge(qkv_mm, NCH * n + c + 1)
                    src = bank[c][:, :].rearrange("p (b y x) -> p b y x", b=2, y=HW)

                    def to(m):
                        return m[:, :, :, 2 * c:2 * c + 2].rearrange("p x y b -> p b y x")
                    if t == 0:
                        act.activation(to(q_relu), src, ACT.Relu).then_inc(q_relued, 1)
                    act.activation(to(heads_raw[t]), src, ACT.Copy).then_inc(head_a, 1)

            for k in range(9):
                act.wait_ge(band_mm, k + 1)
                if k < 8:
                    act.activation(dw_band[:, :, :, 2 * k:2 * k + 2].rearrange("p k g x -> p x (k g)"),
                                   bank[4 + k % 4][:, 0:2 * KS * NG].rearrange("p (x n) -> p x n", x=2),
                                   ACT.Copy).then_inc(band_out, 1)
                else:
                    act.activation(pw_in[:, :, :].rearrange("p o g -> p (o g)"), bank[4][:, 0:G8 * NG],
                                   ACT.Copy).then_inc(band_out, 1)

            def linear_attention(h):
                for n in range(B + 3):
                    if n < B:
                        i = h * B + n
                        act.wait_ge(kv_turned, i + 1)
                        if i >= 2:
                            act.wait_ge(kv_mm, i - 1)
                        if i == 0:
                            act.wait_ge(edges_zero, 7)
                        src = bank[2 + i % 2][:, :].rearrange("p (j q) -> p j q", j=4)
                        act.activation(kvT[:, i % 2, 0:2, 0:128], src[:, 0:2, :], ACT.Relu)
                        act.activation(kvT[:, i % 2, 2:4, 0:128], src[:, 2:4, :], ACT.Copy).then_inc(kv_copied, 1)
                    if n >= 3:
                        i = h * B + n - 3
                        b = n - 3
                        act.wait_ge(att_turned, i + 1)
                        act.activation(att[h][:, b * S:(b + 1) * S].rearrange("p (y x) -> p x y", x=HW),
                                       bank[i % 2][:, 0:S].rearrange("p (x y) -> p x y", x=HW),
                                       ACT.Copy).then_inc(att_out, 1)

            linear_attention(0)
            for u, (t, v) in enumerate(UNITS):
                act.wait_ge(conv_mm, u + 1)
                if u >= 2:
                    act.wait_ge(conv_sent[u % 2], 16 * GU * (u // 2))
                act.activation(conv_out[:, u % 2, :, :], bank[u % 2][:, :].rearrange("p (g n) -> p g n", g=GU),
                               ACT.Relu if t == 0 else ACT.Copy).then_inc(conv_copied, 1)
            linear_attention(1)

            def router_exp(r):
                act.wait_ge(rt_diff, r + 1)
                act.activation(rv[:, 3, :], rv[:, 2, :], ACT.Exp).then_inc(rt_exp, 1)

            def token_rows(r):
                for c in range(NCH):
                    act.wait_ge(rows_mm, NCH * r + c + 1)
                    act.activation(chunk(ln_sq, c), bank[4 + c][:, :], ACT.Copy).then_inc(rows_copied, 1)

            def moe_act(r, NB):
                m = moe[r]

                def x_copy(it, q, first):
                    j = it * UNR + q
                    act.wait_ge(m.turned, j + 1)
                    if not (first and q < 2):
                        act.wait_ge(m.up, j - 1)
                    act.activation(x_cols[:, q % 2, :], bank[q % 2][:, 0:128], ACT.Copy).then_inc(m.x_copied, 1)

                def hidden(it, q, first):
                    j = it * UNR + q
                    if r == 0:
                        act.wait_ge(m.h_in, j + 1)
                        if not (first and q < 2):
                            act.wait_ge(m.h_turned, j - 1)
                        act.activation(h_rows[:, q % 2, :], h_in[:, q % 2, :], ACT.Gelu_apprx_tanh)\
                            .then_inc(m.act, 1)
                    else:
                        act.wait_ge(m.up, j + 1)
                        if not (first and q < 2):
                            act.wait_ge(m.h_in, j - 1)
                        act.activation(h_in[:, q % 2, 0:F1], bank[2 + q % 2][:, 0:F1], ACT.Silu)\
                            .then_inc(m.act, 1)

                def body(it, first):
                    for q in range(UNR):
                        x_copy(it, q, first)
                        if in_loop(q - 1, first):
                            hidden(*at(it, q - 1), first)

                body(0, True)
                with act.Fori(1, NB // UNR) as it:
                    body(it, False)
                hidden(NB // UNR - 1, UNR - 1, False)

            ln_roots(1, 1)
            token_rows(0)
            router_exp(0)
            moe_act(0, NB0)

            ln_roots(2, 0)
            for c in range(NCH):
                for j, (dst, b) in enumerate(((sq_q, "bq"), (sq_k, "bk"))):
                    act.wait_ge(sq_qk_mm, 2 * c + j + 1)
                    act.activation(chunk(dst, c), bank[4 * j + c % 2][:, :], ACT.Identity,
                                   bias=vec(b)).then_inc(sq_qk_out, 1)
            for i in range(B + 1):
                if i < B:
                    act.wait_ge(sq_max, i + 1)
                    act.activation(sq_st[:, i % 2, 1, :], sq_st[:, i % 2, 0, :], ACT.Copy,
                                   scale=-ATT_SCALE).then_inc(sq_nmax, 1)
                    act.wait_ge(sq_nmax, i + 1)
                    if i >= 2:
                        act.wait_ge(sq_norm, 2 * (i - 1))
                    for j in range(2):
                        act.activation(sq_p[:, i % 2, j, :], bank[i % 2][:, j * S:(j + 1) * S], ACT.Exp,
                                       bias=sq_st[:, i % 2, 1, j:j + 1], scale=ATT_SCALE,
                                       accum_out=sq_st[:, i % 2, 2, j:j + 1]).then_inc(sq_exp, 1)
                if i >= 1:
                    k = i - 1
                    act.wait_ge(sq_turned, k + 1)
                    if k >= 2:
                        act.wait_ge(sq_mm, k - 1)
                    act.activation(sq_pT[:, k % 2, :, :],
                                   bank[2 + k % 2][:, :].rearrange("p (m n) -> p m n", m=2),
                                   ACT.Copy).then_inc(sq_copied, 1)

            ln_roots(3, 1)
            token_rows(1)
            router_exp(1)
            moe_act(1, NB1)

        @block.vector
        def _(dve):
            def ln_center(n):
                for c in range(NCH):
                    dve.wait_ge(ln_mean, NCH * n + c + 1)
                    dve.tensor_tensor(chunk(xc, c), chunk(xs, c), bank[c][:, :], ALU.subtract)\
                        .then_inc(ln_cent, 1)

            def ln_scale(n):
                for c in range(NCH + 1):
                    if c < NCH:
                        g = NCH * n + c
                        std, inv = (ln_r[:, i, 4 * c:4 * c + 4] for i in range(2))
                        dve.wait_ge(ln_root, g + 1)
                        dve.reciprocal(inv, std).then_inc(ln_inv, 1)
                        dve.wait_ge(ln_inv, 2 * g + 1)
                        if c >= 2:
                            dve.wait_ge(ln_spread, g - 1)
                        dve.tensor_tensor(ln_diag[:, c % 2, :, :],
                                          ident[:, :].unsqueeze(1).broadcast_to([128, 4, 128]),
                                          inv.unsqueeze(2).broadcast_to([128, 4, 128]), ALU.mult)\
                            .then_inc(ln_inv, 1)
                    if c >= 1:
                        g = NCH * n + c - 1
                        dve.wait_ge(ln_spread, g + 1)
                        dve.tensor_tensor(chunk(xn, c - 1), chunk(xc, c - 1), bank[c - 1][:, :], ALU.mult)\
                            .then_inc(ln_out, 1)

            dve.wait_ge(consts, 17)
            ln_center(0)
            ln_scale(0)
            dve.wait_ge(w_turned, 1)
            for g in range(2):
                dve.tensor_copy(wT[:, 4 * g:4 * g + 4, :],
                                bank[4 + g][:, :].rearrange("p (j q) -> p j q", q=128)).then_inc(w_ready, 1)
            dve.tensor_copy(wT[:, W_AO, :], bank[6][:, 0:128]).then_inc(w_ready, 1)
            dve.tensor_copy(wT[:, W_SM, 0:SMROWS], bank[6][:, 128:128 + SMROWS]).then_inc(w_ready, 1)
            dve.tensor_copy(dw_t[:, :, :].rearrange("p k g -> p (k g)"), bank[6][0:G8 * KS, 256:256 + KS * NG])\
                .then_inc(w_ready, 1)
            dve.tensor_copy(pw_t[:, :, :].rearrange("p o g -> p (o g)"), bank[7][0:G8, 0:G8 * NG])\
                .then_inc(w_ready, 1)

            dve.wait_ge(bn_step, 1)
            dve.reciprocal(bn[:, 1:2], bn[:, 0:1]).then_inc(bn_step, 1)
            dve.wait_ge(bn_step, 2)
            dve.tensor_tensor(bn[:, 2:3], vec("gamma"), bn[:, 1:2], ALU.mult).then_inc(bn_step, 1)
            dve.wait_ge(bn_step, 3)
            dve.tensor_tensor(bn[:, 3:4], vec("mean"), bn[:, 2:3], ALU.mult).then_inc(bn_step, 1)
            dve.wait_ge(bn_step, 4)
            dve.tensor_tensor(bn[:, 3:4], vec("beta"), bn[:, 3:4], ALU.subtract).then_inc(bn_step, 1)
            dve.wait_ge(bn_step, 5)
            dve.tensor_scalar(xs[:, :], xs[:, :], bn[:, 3:4], None, ALU.add).then_inc(bn_step, 1)

            def linear_attention(h):
                for n in range(B + 2):
                    if n < B:
                        i = h * B + n
                        dve.wait_ge(kv_mm, i + 1)
                        if i >= 2:
                            dve.wait_ge(nd_mm, i - 1)
                        kv = bank[4 + i % 2]
                        dve.tensor_tensor(kvm[:, i % 2, 0:128], kv[:, 0:128], blk16[:, :], ALU.mult)
                        dve.tensor_scalar(kvm[:, i % 2, 128:128 + NH], blk16[:, 0:128:HD], kv[:, 128:129], None,
                                          ALU.mult).then_inc(kv_masked, 1)
                    if n >= 2:
                        i = h * B + n - 2
                        nd = bank[6 + i % 2][:, 0:2 * (128 + NH)].rearrange("p (j n) -> p j n", j=2)
                        d0, d1 = den[:, i % 2, 0, :, :], den[:, i % 2, 1, :, :]
                        dve.wait_ge(nd_mm, i + 1)
                        dve.tensor_scalar(d0, nd[:, :, 128:128 + NH], DIV_EPS, None, ALU.add).then_inc(den_step, 1)
                        dve.wait_ge(den_step, 2 * i + 1)
                        dve.reciprocal(d1, d0).then_inc(den_step, 1)
                        dve.wait_ge(den_step, 2 * i + 2)
                        if i >= 2:
                            dve.wait_ge(att_turned, i - 1)
                        dve.tensor_tensor(att_rows[:, i % 2, :, :].rearrange("p j (h d) -> p j h d", d=HD),
                                          nd[:, :, 0:128].rearrange("p j (h d) -> p j h d", d=HD),
                                          d1.unsqueeze(3).broadcast_to([128, 2, NH, HD]), ALU.mult)\
                            .then_inc(att_div, 1)

            linear_attention(0)
            linear_attention(1)
            for c in range(NCH):
                dve.wait_ge(proj_mm, c + 1)
                if c == 0:
                    dve.wait_ge(bn_step, 6)
                dve.scalar_tensor_tensor(out=chunk(xs, c), in0=bank[6 + c % 2][:, :], scalar=bn[:, 2:3],
                                         in1=chunk(xs, c), op0=ALU.mult, op1=ALU.add).then_inc(x1_ready, 1)

            n_rt = [0]

            def step(ins):
                n_rt[0] += 1
                ins.then_inc(rt_chain, 1)
                dve.wait_ge(rt_chain, n_rt[0])

            def router(r, E, NB):
                lg, eq, oh1, oh2, sc = (t[:, :, 0:E] for t in rt)
                l2 = lg
                m1, m2, d, ex = (rv[:, i, :] for i in range(4))
                mx, sm = rv[:, 4, :], rv[:, 5, :]

                def per_e(v):
                    return v.unsqueeze(2).broadcast_to([128, TT, E])

                rk = rank[:, 0:E].unsqueeze(1).broadcast_to([128, TT, E])
                dve.wait_ge(rt_mm, r + 1)
                step(dve.tensor_copy(lg, bank[0][:, 0:TT * E].rearrange("p (t e) -> p t e", e=E)))
                for src, top, oh in ((lg, m1, oh1), (l2, m2, oh2)):
                    step(dve.tensor_reduce(top, src, AX.X, ALU.max))
                    step(dve.tensor_tensor(eq, src, per_e(top), ALU.is_equal))
                    step(dve.tensor_tensor(sc, eq, rk, ALU.mult))
                    step(dve.tensor_reduce(mx, sc, AX.X, ALU.max))
                    step(dve.tensor_tensor(oh, sc, per_e(mx), ALU.is_equal))
                    if oh is oh1:
                        step(dve.scalar_tensor_tensor(out=l2, in0=oh1, scalar=MASKED, in1=lg,
                                                      op0=ALU.mult, op1=ALU.add))
                dve.tensor_tensor(sc, oh1, oh2, ALU.add).then_inc(rt_mask, 1)
                dve.tensor_tensor(d, m2, m1, ALU.subtract).then_inc(rt_diff, 1)
                dve.wait_ge(rt_exp, r + 1)
                step(dve.tensor_scalar(sm, ex, 1.0, None, ALU.add))
                step(dve.reciprocal(pair_w[:, 0, :], sm))
                dve.tensor_tensor(pair_w[:, 1, :], ex, pair_w[:, 0, :], ALU.mult).then_inc(rt_chain, 1)
                n_rt[0] += 1

                dve.wait_ge(rt_prefix, r + 1)
                prefix = bank[1][:, 0:TT * E].rearrange("p (t e) -> p t e", e=E)
                total = bank[1][:, TT * E:2 * TT * E].rearrange("p (t e) -> p t e", e=E)
                a, b = (t[:, :, 0:E] for t in tsum)
                if r == 0:
                    dve.wait_ge(tables, 9)
                step(dve.tensor_copy(a[:, SCAN:, :], total))
                for k in (1, 2, 4, 8):
                    step(dve.tensor_tensor(b[:, SCAN:, :], a[:, SCAN:, :], a[:, SCAN - k:SCAN + TT - k, :], ALU.add))
                    a, b = b, a
                step(dve.tensor_scalar(rcnt[:, 0, 0:E], a[:, SCAN + TT - 1, :], 127.0, None, ALU.add))
                step(dve.tensor_scalar(rcnt[:, 1, 0:E], rcnt[:, 0, 0:E], 7, None, ALU.arith_shift_right))
                u, v = bsum
                step(dve.tensor_copy(u[:, SCAN:SCAN + E], rcnt[:, 1, 0:E]))
                k = 1
                while k < E:
                    step(dve.tensor_tensor(v[:, SCAN:SCAN + E], u[:, SCAN:SCAN + E], u[:, SCAN - k:SCAN + E - k],
                                           ALU.add))
                    u, v, k = v, u, 2 * k
                block_end = u[:, SCAN:SCAN + E]
                step(dve.tensor_tensor(l2, prefix, a[:, SCAN - 1:SCAN + TT - 1, :], ALU.add))
                step(dve.scalar_tensor_tensor(
                    out=l2, in0=u[:, SCAN - 1:SCAN + E - 1].unsqueeze(1).broadcast_to([128, TT, E]),
                    scalar=128.0, in1=l2, op0=ALU.mult, op1=ALU.add))
                step(dve.tensor_tensor(oh1, oh1, l2, ALU.mult))
                step(dve.tensor_reduce(slot_f[:, 0, :], oh1, AX.X, ALU.add))
                step(dve.tensor_tensor(oh2, oh2, l2, ALU.mult))
                step(dve.tensor_reduce(slot_f[:, 1, :], oh2, AX.X, ALU.add))
                step(dve.tensor_copy(slot_i[:, 0, :, :], slot_f[:, :, :]))
                step(dve.tensor_scalar(slot_i[:, 1, :, :], slot_i[:, 0, :, :], 127, None, ALU.bitwise_and))
                step(dve.tensor_scalar(slot_i[:, 2, :, :], slot_i[:, 0, :, :], 7, None, ALU.arith_shift_right))
                step(dve.tensor_copy(place[:, :, :, :], slot_i[:, 1:3, :, :]))

                def pairs(t, n):
                    return t.rearrange("p k t -> p (k t)").unsqueeze(2).broadcast_to([128, 2 * TT, n])

                def along(n):
                    return iota[:, 0:n].unsqueeze(1).broadcast_to([128, 2 * TT, n])

                step(dve.tensor_tensor(block_hot[:, :, 0:NB], along(NB), pairs(place[:, 1, :, :], NB), ALU.is_equal))
                dve.tensor_tensor(block_val[:, :, 0:NB], block_hot[:, :, 0:NB], pairs(pair_id[:, :, :], NB),
                                  ALU.mult).then_inc(rt_value, 1)
                dve.tensor_tensor(block_val[:, :, NB:2 * NB], block_hot[:, :, 0:NB], pairs(pair_w[:, :, :], NB),
                                  ALU.mult).then_inc(rt_value, 1)
                for k in range(2):
                    dve.tensor_tensor(place_hot[:, k * TT:(k + 1) * TT, :],
                                      iota[:, :].unsqueeze(1).broadcast_to([128, TT, 128]),
                                      place[:, 0, k, :].unsqueeze(2).broadcast_to([128, TT, 128]),
                                      ALU.is_equal).then_inc(rt_place, 1)
                ends = block_hot[:, 0:E, 0:NB].rearrange("p e j -> p j e")
                dve.wait_ge(rt_value, 2 * (r + 1))
                step(dve.tensor_tensor(ends, iota[:, 0:NB].unsqueeze(2).broadcast_to([128, NB, E]),
                                       block_end.unsqueeze(1).broadcast_to([128, NB, E]), ALU.is_ge))
                step(dve.tensor_reduce(ended[:, 0:NB], ends, AX.X, ALU.add))
                dve.tensor_scalar(expert[r][:, :], ended[:, 0:NB], float(E - 1), None, ALU.min).then_inc(rt_table, 1)
                dve.wait_ge(rt_inverse, r + 1)
                v = bank[2][:, 0:NB]
                dve.tensor_copy(slot_w[r][:, :], bank[2][:, NB:2 * NB]).then_inc(rt_table, 1)
                step(dve.scalar_tensor_tensor(out=taken[:, 0:NB], in0=v, scalar=1.0, in1=spare[:, 1, 0:NB],
                                              op0=ALU.min, op1=ALU.mult))
                step(dve.tensor_tensor(taken[:, 0:NB], taken[:, 0:NB], v, ALU.add))
                dve.tensor_tensor(dest[r][:, :], taken[:, 0:NB], spare[:, 0, 0:NB], ALU.add).then_inc(rt_table, 1)
                dve.wait_ge(rt_table, 4 * r + 3)
                dve.tensor_scalar(token[r][:, :], dest[r][:, :], T - 1, None, ALU.bitwise_and)\
                    .then_inc(rt_table, 1)

            def moe_vector(r, E, NB):
                m = moe[r]
                K = (M0, 2)[r]

                def load_expert(it, q):
                    return dve.value_load(expert[r][0:1, bass.ds(it * UNR + q, 1)], min_val=0, max_val=E - 1)

                def hidden(it, q, first):
                    j = it * UNR + q
                    if r == 0:
                        e = load_expert(it, q)
                        dve.wait_ge(m.up, j + 1)
                        if not (first and q < 2):
                            dve.wait_ge(m.act, j - 1)
                        dve.tensor_tensor(h_in[:, q % 2, :], bank[2 + q % 2][:, :],
                                          b1_all[:, bass.ds(e * F0, F0)], ALU.add).then_inc(m.h_in, 1)
                    else:
                        dve.wait_ge(m.act, j + 1)
                        if not (first and q < 2):
                            dve.wait_ge(m.h_turned, j - 1)
                        dve.tensor_tensor(h_rows[:, q % 2, 0:F1], h_in[:, q % 2, 0:F1],
                                          bank[2 + q % 2][:, F1:2 * F1], ALU.mult).then_inc(m.h_in, 1)

                def h_copy(it, q, first):
                    j = it * UNR + q
                    dve.wait_ge(m.h_turned, j + 1)
                    if not (first and q < 2):
                        dve.wait_ge(m.down, j - 1)
                    dve.tensor_copy(h_cols[:, q % 2, 0:K * 128], bank[4 + q % 2][:, 0:K * 128])\
                        .then_inc(m.h_copied, 1)

                def weigh(it, q, first):
                    j = it * UNR + q
                    src = bank[6 + q % 2][:, 0:C]
                    if r == 0:
                        e = load_expert(it, q)
                    dve.wait_ge(m.down, j + 1)
                    if not isinstance(it, int) or it:
                        dve.wait_ge(m.scattered[q], it * 16)
                    if r == 0:
                        dve.tensor_tensor(y_rows[:, q, :], src, b2_all[:, bass.ds(e * C, C)], ALU.add)\
                            .then_inc(m.y_sum, 1)
                        dve.wait_ge(m.y_sum, j + 1)
                        src = y_rows[:, q, :]
                    dve.tensor_scalar(y_rows[:, q, :], src, slot_w[r][:, bass.ds(j, 1)], None, ALU.mult)\
                        .then_inc(m.y, 1)

                stages = ((1, hidden), (2, h_copy), (3, weigh))

                def body(it, first):
                    for q in range(UNR):
                        for lag, stage in stages:
                            if in_loop(q - lag, first):
                                stage(*at(it, q - lag), first)

                body(0, True)
                body(1, False)
                with dve.Fori(2, NB // UNR) as it:
                    body(it, False)
                for q in range(UNR, UNR + 3):
                    for lag, stage in stages[q - UNR:]:
                        stage(NB // UNR - 1, q - lag, False)

            def moe_sum(r):
                for c in range(NCH):
                    dve.wait_ge(y_in[c], 32 * (r + 1))
                    dve.tensor_tensor(chunk(xc, c), chunk(xc, c), chunk(ln_sq, c), ALU.add).then_inc(y_added, 1)
                for c in range(NCH):
                    dve.wait_ge(y_turned, NCH * r + c + 1)
                    dve.tensor_tensor(chunk(xs, c), chunk(xs, c), bank[c][:, :], ALU.add).then_inc(x_moe, 1)

            ln_center(1)
            ln_scale(1)
            router(0, E0, NB0)
            moe_vector(0, E0, NB0)
            moe_sum(0)

            ln_center(2)
            ln_scale(2)
            for g in range(4):
                dve.wait_ge(sq_v_mm, g + 1)
                dve.tensor_copy(sq_vT[:, 4 * g:4 * g + 4, :],
                                bank[V_BANKS[g]][:, :].rearrange("p (j q) -> p j q", j=4)).then_inc(sq_v_out, 1)
            for i in range(B + 2):
                if i < B:
                    dve.wait_ge(sq_s, i + 1)
                    dve.tensor_reduce(sq_st[:, i % 2, 0, :], bank[i % 2][:, :].rearrange("p (j m) -> p j m", j=2),
                                      AX.X, ALU.max).then_inc(sq_max, 1)
                if 1 <= i <= B:
                    k = i - 1
                    dve.wait_ge(sq_exp, 2 * k + 2)
                    dve.reciprocal(sq_st[:, k % 2, 3, :], sq_st[:, k % 2, 2, :]).then_inc(sq_inv, 1)
                    dve.wait_ge(sq_inv, k + 1)
                    if k >= 2:
                        dve.wait_ge(sq_turned, k - 1)
                    for j in range(2):
                        dve.tensor_scalar(sq_pn[:, k % 2, j, :], sq_p[:, k % 2, j, :],
                                          sq_st[:, k % 2, 3, j:j + 1], None, ALU.mult).then_inc(sq_norm, 1)
                if i >= 2:
                    k = i - 2
                    dve.wait_ge(sq_mm, k + 1)
                    dve.tensor_scalar(sq_o[:, k, :], bank[4 + k % 2][:, 0:S], vec("bv"), None, ALU.add)\
                        .then_inc(sq_out, 1)
            for c in range(NCH):
                dve.wait_ge(wo_mm, c + 1)
                dve.scalar_tensor_tensor(out=chunk(xs, c), in0=bank[6 + c % 2][:, :], scalar=vec("bo"),
                                         in1=chunk(xs, c), op0=ALU.add, op1=ALU.add).then_inc(x3_ready, 1)

            ln_center(3)
            ln_scale(3)
            router(1, E1, NB1)
            moe_vector(1, E1, NB1)
            moe_sum(1)

        @block.tensor
        def _(pe):
            pe.wait_ge(consts, 17)

            def layer_norm(n, ready):
                for c in range(NCH):
                    pe.wait_ge(*ready(c))
                    pe.matmul(bank[c][:, :], mean_w[:, :], chunk(xs, c), start=True, stop=True)\
                        .then_inc(ln_mean, 1)
                for c in range(NCH):
                    pe.wait_ge(ln_sqd, NCH * n + c + 1)
                    for i in range(4):
                        mm = pe.matmul(bank[4 + c][:, i:i + 1], ln_sq[:, (4 * c + i) * 128:(4 * c + i + 1) * 128],
                                       mean_w[:, 0:1], start=True, stop=True)
                    mm.then_inc(ln_var, 1)
                for c in range(NCH):
                    pe.wait_ge(ln_inv, 2 * (NCH * n + c) + 2)
                    pe.matmul(bank[c][:, :], ones[:, :], ln_diag[:, c % 2, :, :].rearrange("p j q -> p (j q)"),
                              start=True, stop=True).then_inc(ln_spread, 1)

            layer_norm(0, lambda c: (x_in[c], 16))

            pe.wait_ge(w_in, 16 * NLOADS)
            pe.wait_ge(ln_root, NCH)
            pe.wait_ge(dw_rows_in, 1)
            for i in range(9):
                pe.transpose(bank[4 + i // 4][:, (i % 4) * 128:(i % 4 + 1) * 128], wraw[:, i, :], ident[:, :])
            pe.transpose(bank[6][:, 128:128 + SMROWS], wraw[0:SMROWS, W_SM, :], ident[0:SMROWS, 0:SMROWS])
            for k in range(KS):
                pe.transpose(bank[6][0:G8 * KS, 256 + k * NG:256 + (k + 1) * NG], dw_row[:, k, :, :].rearrange("g i c -> g (i c)"),
                             ident[0:NG, 0:NG])
            for o in range(G8):
                mm = pe.transpose(bank[7][0:G8, o * NG:(o + 1) * NG], pw_raw[:, o, :], ident[0:NG, 0:NG])
            mm.then_inc(w_turned, 1)

            pe.wait_ge(w_ready, 6)
            for n, t in enumerate(ORDER):
                for c in range(NCH):
                    if n == 0:
                        pe.wait_ge(ln_out, c + 1)
                    else:
                        pe.wait_ge(head_a, NCH * (n - 1) + c + 1)
                    pe.matmul(bank[c][:, :], wT[:, W_Q + t, :], chunk(xn, c), start=True, stop=True)\
                        .then_inc(qkv_mm, 1)
            for k in range(8):
                if k >= 4:
                    pe.wait_ge(band_out, k - 3)
                for j in range(2):
                    x = 2 * k + j
                    mm = pe.matmul(bank[4 + k % 4][:, j * KS * NG:(j + 1) * KS * NG],
                                   band[:, x, :, :].rearrange("p i x -> p (i x)"),
                                   dw_t[:, :, :].rearrange("p k g -> p (k g)"), start=True, stop=True)
                mm.then_inc(band_mm, 1)
            pe.wait_ge(band_out, 5)
            pe.matmul(bank[4][:, 0:G8 * NG], spread[:, :, :].rearrange("p i x -> p (i x)"),
                      pw_t[:, :, :].rearrange("p o g -> p (o g)"), start=True, stop=True).then_inc(band_mm, 1)

            def linear_attention(h):
                def turn_kv(i, b):
                    if i >= 2:
                        pe.wait_ge(kv_copied, i - 1)
                    for j in range(4):
                        src = heads_raw[1 + j // 2][:, (j % 2) * 8:(j % 2) * 8 + 8, :, b]
                        mm = pe.transpose(bank[2 + i % 2][:, j * 128:(j + 1) * 128], src, ident[:, :])
                    mm.then_inc(kv_turned, 1)

                def kv_product(i, b):
                    pe.wait_ge(kv_copied, i + 1)
                    if i >= 2:
                        pe.wait_ge(kv_masked, i - 1)
                    for j in range(2):
                        mm = pe.matmul(bank[4 + i % 2][:, 0:129], kvT[:, i % 2, j, 0:128],
                                       kvT[:, i % 2, 2 + j, 0:129], start=(j == 0), stop=(j == 1))
                    mm.then_inc(kv_mm, 1)

                def num_den(i, b):
                    pe.wait_ge(kv_masked, i + 1)
                    if i >= 2:
                        pe.wait_ge(att_div, i - 1)
                    q = (q_relu, heads_raw[0])[h]
                    n = 128 + NH
                    for j in range(2):
                        mm = pe.matmul(bank[6 + i % 2][:, j * n:(j + 1) * n], q[:, 8 * j:8 * j + 8, :, b],
                                       kvm[:, i % 2, :], start=True, stop=True)
                    mm.then_inc(nd_mm, 1)

                def turn_rows(i, b):
                    pe.wait_ge(att_div, i + 1)
                    if i >= 2:
                        pe.wait_ge(att_out, i - 1)
                    for j in range(2):
                        mm = pe.transpose(bank[i % 2][:, j * 128:(j + 1) * 128], att_rows[:, i % 2, j, :],
                                          ident[:, :])
                    mm.then_inc(att_turned, 1)

                for n in range(B + 3):
                    for lag, stage in enumerate((turn_kv, kv_product, num_den, turn_rows)):
                        if 0 <= n - lag < B:
                            stage(h * B + n - lag, n - lag)

            pe.wait_ge(head_a, 3 * NCH)
            pe.wait_ge(q_relued, NCH)
            pe.wait_ge(band_out, 9)
            linear_attention(0)
            pe.wait_ge(att_out, B)
            for u, (t, v) in enumerate(UNITS):
                pe.wait_ge(map_in[t], 16 * GT)
                if u >= 2:
                    pe.wait_ge(conv_copied, u - 1)
                for i in range(GU):
                    pe.wait_ge(cw_built, GU * u + i + 1)
                    for k in range(KS):
                        mm = pe.matmul(bank[u % 2][:, i * 128:(i + 1) * 128], cw[:, u % CWR, i, k, :],
                                       cmap[:, t, v * GU + i, k * B:(k + HW) * B],
                                       start=(k == 0), stop=(k == KS - 1))
                mm.then_inc(conv_mm, 1)
            for i in range(2):
                pe.wait_ge(conv_sent[i], 16 * GU * len(UNITS) // 2)
            linear_attention(1)
            for c in range(NCH):
                pe.wait_ge(att_out, B + 2 * c + 2)
                if c >= 2:
                    pe.wait_ge(x1_ready, c - 1)
                for h in range(2):
                    mm = pe.matmul(bank[6 + c % 2][:, :], wT[:, W_P0 + h, :], chunk(att[h], c),
                                   start=(h == 0), stop=(h == 1))
                mm.then_inc(proj_mm, 1)
            layer_norm(1, lambda c: (x1_ready, c + 1))

            def router(r, E, row):
                pe.wait_ge(ln_out, NCH * (2 * r + 2))
                for i in range(TT):
                    mm = pe.matmul(bank[0][:, i * E:(i + 1) * E], xn[:, i * 128:(i + 1) * 128],
                                   wT[:, W_SM, row:row + E], start=True, stop=True)
                mm.then_inc(rt_mm, 1)

            def token_rows(r):
                for c in range(NCH):
                    for i in range(4):
                        mm = pe.transpose(bank[4 + c][:, i * 128:(i + 1) * 128],
                                          xn[:, (4 * c + i) * 128:(4 * c + i + 1) * 128], ident[:, :])
                    mm.then_inc(rows_mm, 1)

            def slots(r, E, NB):
                n = TT * E
                pe.wait_ge(rt_mask, r + 1)
                mask = rt[4][:, :, 0:E]
                pe.matmul(bank[1][:, 0:n].rearrange("p (t e) -> p t e", e=E), before[:, :], mask,
                          start=True, stop=True)
                pe.matmul(bank[1][:, n:2 * n].rearrange("p (t e) -> p t e", e=E), ones[:, :], mask,
                          start=True, stop=True).then_inc(rt_prefix, 1)
                pe.wait_ge(rt_value, 2 * (r + 1))
                for i in range(2 * TT):
                    if i % TT == 0:
                        pe.wait_ge(rt_place, 2 * r + i // TT + 1)
                    mm = pe.matmul(bank[2][:, 0:2 * NB], place_hot[:, i, :], block_val[:, i, 0:2 * NB],
                                   start=(i == 0), stop=(i == 2 * TT - 1))
                mm.then_inc(rt_inverse, 1)

            def moe_tensor(r, E, NB, w_up, w_down):
                m = moe[r]
                K = (M0, 2)[r]
                UP = (F0, 2 * F1)[r]
                pe.wait_ge(rt_table, 4 * (r + 1))
                pe.wait_ge(moe_w[r], 16 * (4, 3)[r])
                pe.wait_ge(rows_copied, NCH * (r + 1))

                def load_expert(it, q):
                    return pe.value_load(expert[r][0:1, bass.ds(it * UNR + q, 1)], min_val=0, max_val=E - 1)

                def turn_x(it, q, first):
                    j = it * UNR + q
                    pe.wait_ge(m.gathered[q], it * 16 + 16)
                    if not (first and q < 2):
                        pe.wait_ge(m.x_copied, j - 1)
                    pe.transpose(bank[q % 2][:, 0:128], x_rows[:, q, :], ident[:, :]).then_inc(m.turned, 1)

                def up(it, q, first):
                    j = it * UNR + q
                    e = load_expert(it, q)
                    pe.wait_ge(m.x_copied, j + 1)
                    if not (first and q < 2):
                        pe.wait_ge(m.h_in, j - 1)
                    pe.matmul(bank[2 + q % 2][:, 0:UP], x_cols[:, q % 2, :], w_up[:, bass.ds(e * UP, UP)],
                              start=True, stop=True).then_inc(m.up, 1)

                def turn_h(it, q, first):
                    j = it * UNR + q
                    pe.wait_ge((m.act, m.h_in)[r], j + 1)
                    if not (first and q < 2):
                        pe.wait_ge(m.h_copied, j - 1)
                    for i in range(K):
                        mm = pe.transpose(bank[4 + q % 2][:, i * 128:(i + 1) * 128],
                                          h_rows[:, q % 2, i * 128:(i + 1) * 128], ident[:, :])
                    mm.then_inc(m.h_turned, 1)

                def down(it, q, first):
                    j = it * UNR + q
                    e = load_expert(it, q)
                    pe.wait_ge(m.h_copied, j + 1)
                    if not (first and q < 2):
                        pe.wait_ge(m.y, j - 1)
                    for i in range(K):
                        mm = pe.matmul(bank[6 + q % 2][:, 0:C], h_cols[:, q % 2, i * 128:(i + 1) * 128],
                                       w_down[:, bass.ds(e * (K * C) + i * C, C)],
                                       start=(i == 0), stop=(i == K - 1))
                    mm.then_inc(m.down, 1)

                stages = ((0, turn_x), (1, up), (2, turn_h), (3, down))

                def body(it, first):
                    for q in range(UNR):
                        for lag, stage in stages:
                            if in_loop(q - lag, first):
                                stage(*at(it, q - lag), first)

                body(0, True)
                with pe.Fori(1, NB // UNR) as it:
                    body(it, False)
                for q in range(UNR, UNR + 3):
                    for lag, stage in stages[q - UNR + 1:]:
                        stage(NB // UNR - 1, q - lag, False)

            def y_columns(r):
                for c in range(NCH):
                    pe.wait_ge(y_added, NCH * r + c + 1)
                    for i in range(4):
                        mm = pe.transpose(bank[c][:, i * 128:(i + 1) * 128],
                                          xc[:, (4 * c + i) * 128:(4 * c + i + 1) * 128], ident[:, :])
                    mm.then_inc(y_turned, 1)

            router(0, E0, ROUT0)
            token_rows(0)
            slots(0, E0, NB0)
            moe_tensor(0, E0, NB0, w_up0, w_down0)
            y_columns(0)

            layer_norm(2, lambda c: (x_moe, c + 1))
            for c in range(NCH):
                pe.wait_ge(ln_out, 2 * NCH + c + 1)
                for j in range(2):
                    if c >= 2:
                        pe.wait_ge(sq_qk_out, 2 * (c - 2) + j + 1)
                    pe.matmul(bank[4 * j + c % 2][:, :], wT[:, W_AQ + j, :], chunk(xn, c),
                              start=True, stop=True).then_inc(sq_qk_mm, 1)
            for g in range(4):
                for j in range(4):
                    i = 4 * g + j
                    mm = pe.matmul(bank[V_BANKS[g]][:, j * 128:(j + 1) * 128], xn[:, i * 128:(i + 1) * 128],
                                   wT[:, W_AV, :], start=True, stop=True)
                mm.then_inc(sq_v_mm, 1)

            def scores(b):
                if b == 0:
                    pe.wait_ge(sq_qk_out, 2 * NCH)
                if b >= 2:
                    pe.wait_ge(sq_exp, 2 * (b - 1))
                for j in range(2):
                    mm = pe.matmul(bank[b % 2][:, j * S:(j + 1) * S],
                                   sq_q[:, b * S + j * 128:b * S + (j + 1) * 128],
                                   sq_k[:, b * S:(b + 1) * S], start=True, stop=True)
                mm.then_inc(sq_s, 1)

            def turn_p(b):
                pe.wait_ge(sq_norm, 2 * (b + 1))
                if b >= 2:
                    pe.wait_ge(sq_copied, b - 1)
                for j in range(2):
                    for m in range(2):
                        mm = pe.transpose(bank[2 + b % 2][:, m * S + j * 128:m * S + (j + 1) * 128],
                                          sq_pn[:, b % 2, j, m * 128:(m + 1) * 128], ident[:, :])
                mm.then_inc(sq_turned, 1)

            def weigh_v(b):
                pe.wait_ge(sq_copied, b + 1)
                if b == 0:
                    pe.wait_ge(sq_v_out, 4)
                if b >= 2:
                    pe.wait_ge(sq_out, b - 1)
                for m in range(2):
                    mm = pe.matmul(bank[4 + b % 2][:, 0:S], sq_vT[:, 2 * b + m, :], sq_pT[:, b % 2, m, :],
                                   start=(m == 0), stop=(m == 1))
                mm.then_inc(sq_mm, 1)

            for i in range(B + 2):
                if i < B:
                    scores(i)
                if 1 <= i <= B:
                    turn_p(i - 1)
                if i >= 2:
                    weigh_v(i - 2)
            for c in range(NCH):
                pe.wait_ge(sq_out, 2 * c + 2)
                if c >= 2:
                    pe.wait_ge(x3_ready, c - 1)
                pe.matmul(bank[6 + c % 2][:, :], wT[:, W_AO, :],
                          sq_o[:, 2 * c:2 * c + 2, :].rearrange("p b s -> p (b s)"), start=True, stop=True)\
                    .then_inc(wo_mm, 1)
            layer_norm(3, lambda c: (x3_ready, c + 1))
            router(1, E1, ROUT1)
            token_rows(1)
            slots(1, E1, NB1)
            moe_tensor(1, E1, NB1, w_up1, w_down1)
            y_columns(1)


_INS = ['x', 'L0_conv_w_qkv', 'L0_conv_w_dw', 'L0_conv_w_pw', 'L0_conv_w_proj', 'L0_conv_bn_gamma',
        'L0_conv_bn_beta', 'L0_conv_bn_mean', 'L0_conv_bn_var', 'L0_ffn_gate_w', 'L0_ffn_w1', 'L0_ffn_b1',
        'L0_ffn_w2', 'L0_ffn_b2', 'L1_conv_wq', 'L1_conv_bq', 'L1_conv_wk', 'L1_conv_bk', 'L1_conv_wv',
        'L1_conv_bv', 'L1_conv_wo', 'L1_conv_bo', 'L1_ffn_router_w', 'L1_ffn_gate_w', 'L1_ffn_up_w',
        'L1_ffn_down_w']


def kernel(**inputs):
    import numpy as _np
    import concourse.bacc as _bacc
    from concourse import mybir as _mybir
    from concourse.bass_utils import run_bass_kernel_spmd as _run

    nc = _bacc.Bacc("TRN2", target_bir_lowering=False, num_devices=1)
    arrays, args = {}, []
    for name in _INS:
        a = _np.ascontiguousarray(inputs[name])
        arrays[f"in_{name}_dram"] = a
        args.append(nc.dram_tensor(f"in_{name}_dram", a.shape, _mybir.dt.from_np(a.dtype), kind="ExternalInput").ap())
    args.append(nc.dram_tensor("out_dram", (B, C, HW, HW), F32, kind="ExternalOutput").ap())
    metaformer(nc, *args)
    r = _run(nc, [arrays], core_ids=[0])
    return r.results[0]["out_dram"]
```

```python
from contextlib import ExitStack

import concourse.bass as bass
from concourse import mybir

F32 = mybir.dt.float32
F16 = mybir.dt.float16
I32 = mybir.dt.int32
ALU = mybir.AluOpType
ACT = mybir.ActivationFunctionType
AX = mybir.AxisListType

C = 128
B, HW = 8, 16
S = HW * HW
T = B * S
CH = 512
NCH = T // CH
TT = T // 128
HD = 16
KS = 5
EDGE = KS // 2
G8 = 8
NG = 3 * C // G8
GT = C // G8
NH = C // HD
GU = 4
UPT = GT // GU
ORDER = (1, 2, 0)
UNITS = [(t, v) for t in ORDER for v in range(UPT)]
CWR = 3
STEPS = {3 * n + 1: (0, n) for n in range(B + 3)} | {4 * 2 * UPT + 6 + n: (1, n) for n in range(B + 1)}
MAPS_AHEAD = 4
E0, F0 = 8, 512
E1, F1 = 16, 256
M0 = F0 // 128
LN_C_EPS, LN_T_EPS, BN_EPS, DIV_EPS = 1e-6, 1e-5, 1e-5, 1e-15
W1_LOADS = 4
RING = 8


def block_count(experts):
    return (2 * T - experts) // 128 + experts


NB0, NB1 = block_count(E0), block_count(E1)
ATT_SCALE = float(C) ** -0.5
V_BANKS = (6, 7, 2, 3)
P_BANKS = (3, 6)
MASKED = -1e30


def metaformer(nc, x, w_qkv, w_dw, w_pw, w_proj, bn_gamma, bn_beta, bn_mean, bn_var,
               gate_w, w1, b1, w2, b2, wq, bq, wk, bk, wv, bv, wo, bo,
               router_w, gate_ws, up_ws, down_ws, out):
    x_v = x.rearrange("b c h w -> c b (h w)")
    out_v = out.rearrange("b c h w -> c b (h w)")
    tok_dram = [nc.dram_tensor(f"tok{r}", (T, C), F32, kind="Internal").ap() for r in range(2)]
    y_dram = [nc.dram_tensor(f"y{r}", (2 * T + NB * 128, C), F32, kind="Internal").ap()
              for r, NB in enumerate((NB0, NB1))]

    ctx = ExitStack()
    with ctx:
        def sb(name, shape, dt=F32, own=ctx):
            return own.enter_context(nc.sbuf_tensor(name, shape, dt))

        def sem(name):
            return ctx.enter_context(nc.semaphore(name))

        bank = [ctx.enter_context(nc.psum_tensor(f"bank{i}", [128, CH], F32)) for i in range(8)]

        ident = sb("ident", [128, 128])
        center = sb("center", [128, 128])
        mean_w = sb("mean_w", [128, 1])
        ones = sb("ones", [128, 128])
        before = sb("before", [128, 128], F16)
        ones16 = sb("ones16", [128, 128], F16)
        iota = sb("iota", [128, 128])
        pair_id = sb("pair_id", [128, 2, TT])
        spare = sb("spare", [128, NB1])
        blk16 = sb("blk16", [128, 128])
        rank = sb("rank", [128, E1])
        eps = sb("eps", [128, 3])
        act_scratch = sb("act_scratch", [128, 1])
        (W_Q, W_K, W_V, W_P0, W_P1, W_AQ, W_AK, W_AV, W_AO, W_SM) = range(10)
        wT = sb("wT", [128, 10, 128])
        SM = {n: i for i, n in enumerate(
            ["gamma", "beta", "mean", "var", "bq", "bk", "bv", "bo"])}
        ROUT0, ROUT1 = 8, 8 + E0
        B1ROW = ROUT1 + E1
        SMROWS = B1ROW + E0 * M0
        bn = sb("bn", [128, 4])

        def vec(name):
            return wT[:, W_SM, SM[name]:SM[name] + 1]

        xs = sb("xs", [128, T])
        xc = sb("xc", [128, T])
        xn = sb("xn", [128, T])
        ln_sq = sb("ln_sq", [128, T])
        ln_r = sb("ln_r", [128, 2, TT])
        ln_diag = sb("ln_diag", [128, 2, 4, 128])
        att = [xc, ln_sq]

        rt = [sb(f"rt{i}", [128, TT, E1]) for i in range(5)]
        chosen = sb("chosen", [128, TT, E1], F16)
        ended = sb("ended", [128, 1 + E1])
        col_id = sb("col_id", [128, 1])
        rv = sb("rv", [128, 8, TT])
        SCAN = 8
        tsum = [sb(f"tsum{i}", [128, SCAN + TT, E1]) for i in range(2)]
        bsum = [sb(f"bsum{i}", [128, SCAN + E1]) for i in range(2)]
        rcnt = sb("rcnt", [128, 2, E1], I32)
        slot_f = sb("slot_f", [128, 2, TT])
        slot_i = sb("slot_i", [128, 3, 2, TT], I32)
        place = sb("place", [128, 2, 2, TT])
        pair_w = sb("pair_w", [128, 2, TT])
        dest = [sb(f"dest{r}", [128, NB], I32) for r, NB in enumerate((NB0, NB1))]
        token = [sb(f"token{r}", [128, NB], I32) for r, NB in enumerate((NB0, NB1))]
        expert = [sb(f"expert{r}", [1, NB], I32) for r, NB in enumerate((NB0, NB1))]
        taken = sb("taken", [128, 3, NB1])

        conv_ctx = ExitStack()
        cmap = sb("cmap", [128, 3, GT, HW * B], F32, conv_ctx)
        cw = sb("cw", [128, CWR, GU, KS, 128], F32, conv_ctx)
        conv_out = sb("conv_out", [128, 2, GU, HW * B], F32, conv_ctx)
        dw_band = sb("dw_band", [128, KS, NG, HW], F32, conv_ctx)
        pw_in = sb("pw_in", [128, G8, NG], F32, conv_ctx)
        heads_raw = [sb(f"heads{t}", [128, HW, HW, B], F32, conv_ctx) for t in range(3)]
        q_relu = sb("q_relu", [128, HW, HW, B], F32, conv_ctx)
        heads_agg = [heads_raw[0]] + [t[:, :].rearrange("p (x y b) -> p x y b", x=HW, y=HW) for t in (xn, ln_sq)]
        kvT = sb("kvT", [128, 2, 4, 132], F32, conv_ctx)
        kvm = sb("kvm", [128, B, 128 + NH], F32, conv_ctx)
        den = sb("den", [128, 2, 2, 2, NH], F32, conv_ctx)
        att_rows = sb("att_rows", [128, 2, 2, 128], F32, conv_ctx)
        wraw = sb("wraw", [128, 10, 128], F32, conv_ctx)
        dw_raw = sb("dw_raw", [NG, G8, KS, KS], F32, conv_ctx)
        pw_raw = sb("pw_raw", [NG, G8, G8], F32, conv_ctx)
        dw_t = sb("dw_t", [128, KS, NG], F32, conv_ctx)
        pw_t = sb("pw_t", [G8, G8, NG], F32, conv_ctx)
        band = sb("band", [128, HW, G8, HW], F32, conv_ctx)
        dw_row = sb("dw_row", [NG, KS, G8, KS], F32, conv_ctx)
        spread = sb("spread", [G8, G8, HW], F32, conv_ctx)
        conv_ctx.close()

        moe_ctx = ExitStack()
        mid_ctx = ExitStack()
        sq_q = sb("sq_q", [128, T], F32, mid_ctx)
        sq_k = sb("sq_k", [128, T], F32, mid_ctx)
        sq_vT = sb("sq_vT", [128, TT, 128], F32, mid_ctx)
        sq_p = sb("sq_p", [128, 3, 2, S], F32, mid_ctx)
        sq_pn = sb("sq_pn", [128, 2, 2, S], F32, mid_ctx)
        sq_pT = sb("sq_pT", [128, 2, 2, S], F32, mid_ctx)
        sq_st = sb("sq_st", [128, 3, 4, 2], F32, mid_ctx)
        sq_o = sb("sq_o", [128, B, S], F32, mid_ctx)
        mid_ctx.close()
        w_up0 = sb("w_up0", [128, E0 * F0], F32, moe_ctx)
        w_down0 = sb("w_down0", [128, E0 * M0 * C], F32, moe_ctx)
        b2_all = sb("b2_all", [128, E0 * C], F32, moe_ctx)
        place_hot = sb("place_hot", [128, 2 * TT, 128], F16, moe_ctx)
        block_val = sb("block_val", [128, 2 * TT, NB1], F16, moe_ctx)
        block_hot = sb("block_hot", [128, 2 * TT, NB1], F32, moe_ctx)
        x_rows = sb("x_rows", [128, RING, C], F32, moe_ctx)
        x_cols = sb("x_cols", [128, 2, 128], F32, moe_ctx)
        w_block = sb("w_block", [128, 3, F0], F32, moe_ctx)
        h_in = sb("h_in", [128, 2, F0], F32, moe_ctx)
        h_cols = sb("h_cols", [128, 2, F0], F32, moe_ctx)
        y_rows = sb("y_rows", [128, RING, C], F32, moe_ctx)
        w_up1 = sb("w_up1", [128, E1 * 2 * F1], F32, moe_ctx)
        w_down1 = sb("w_down1", [128, E1 * 2 * C], F32, moe_ctx)
        moe_ctx.close()

        x_in = [sem(f"x_in{c}") for c in range(NCH)]
        qkv_in, w_in = sem("qkv_in"), sem("w_in")
        norm_consts = sem("norm_consts")
        consts = sem("consts")
        dw_zero = sem("dw_zero")
        att_consts = sem("att_consts")
        w_turned = sem("w_turned")
        w_ready = sem("w_ready")
        bn_step = sem("bn_step")
        ln_cent, ln_sqd = sem("ln_cent"), sem("ln_sqd")
        ln_spread, ln_kept = sem("ln_spread"), sem("ln_kept")
        ln_var, ln_root, ln_inv, ln_out = sem("ln_var"), sem("ln_root"), sem("ln_inv"), sem("ln_out")
        tables = sem("tables")
        qkv_mm, head_a, q_relued = sem("qkv_mm"), sem("head_a"), sem("q_relued")
        kv_ones = sem("kv_ones")
        dw_rows_in = sem("dw_rows_in")
        map_in = [sem(f"map_in{u}") for u in range(len(UNITS))]
        band_mm, band_out = sem("band_mm"), sem("band_out")
        cw_built = [sem("cw_built_pool"), sem("cw_built_dve")]
        conv_mm, conv_copied = sem("conv_mm"), sem("conv_copied")
        conv_sent = [sem(f"conv_sent{i}") for i in range(2)]
        kv_turned, kv_copied, kv_mm, kv_masked = sem("kv_turned"), sem("kv_copied"), sem("kv_mm"), sem("kv_masked")
        nd_mm, den_step, att_div = sem("nd_mm"), sem("den_step"), sem("att_div")
        att_turned, att_out = sem("att_turned"), sem("att_out")
        proj_mm, x1_ready = sem("proj_mm"), sem("x1_ready")
        rt_mm, rt_chain, rt_diff, rt_exp = sem("rt_mm"), sem("rt_chain"), sem("rt_diff"), sem("rt_exp")
        rt_mask, rt_prefix, rt_place, rt_value = sem("rt_mask"), sem("rt_prefix"), sem("rt_place"), sem("rt_value")
        rt_blocks, rt_weights, rt_ended, rt_expert = (sem("rt_blocks"), sem("rt_weights"), sem("rt_ended"),
                                                      sem("rt_expert"))
        rt_inverse, rt_table = sem("rt_inverse"), sem("rt_table")
        rows_mm, rows_copied = sem("rows_mm"), sem("rows_copied")
        rows_out = [sem("rows_out0"), sem("rows_out1")]
        moe_w = [sem("moe_w0"), sem("moe_w1")]
        y_in = [sem(f"y_in{c}") for c in range(NCH)]
        y_weighed, y_added, y_turned, x_moe = sem("y_weighed"), sem("y_added"), sem("y_turned"), sem("x_moe")

        class Moe:
            def __init__(m, n):
                m.gathered = [sem(f"m{n}_gathered{i}") for i in range(RING)]
                m.scattered = [sem(f"m{n}_scattered{i}") for i in range(RING)]
                m.turned = sem(f"m{n}_turned")
                m.x_copied = sem(f"m{n}_x_copied")
                m.w = sem(f"m{n}_w")
                m.up = sem(f"m{n}_up")
                m.h_in = sem(f"m{n}_h_in")
                m.act = sem(f"m{n}_act")
                m.down = sem(f"m{n}_down")
                m.y = sem(f"m{n}_y")
        moe = [Moe(0), Moe(1)]
        sq_qk_mm, sq_qk_out, sq_v_mm, sq_v_out = sem("sq_qk_mm"), sem("sq_qk_out"), sem("sq_v_mm"), sem("sq_v_out")
        sq_s, sq_max, sq_nmax, sq_exp, sq_inv, sq_norm = (sem("sq_s"), sem("sq_max"), sem("sq_nmax"),
                                                          sem("sq_exp"), sem("sq_inv"), sem("sq_norm"))
        sq_turned, sq_copied, sq_mm, sq_out = sem("sq_turned"), sem("sq_copied"), sem("sq_mm"), sem("sq_out")
        wo_mm, x3_ready = sem("wo_mm"), sem("x3_ready")
        stored = sem("stored")

        block = ctx.enter_context(nc.Block())

        def nd_bank(i):
            return 6 + i % 2 if i < B else (6, 7, 0, 1)[(i - B) % 4]

        def conv_send(queue, u, i):
            t, v = UNITS[u]
            g = v * GU + i
            queue.dma_start(heads_agg[t][G8 * g:G8 * (g + 1), :, :, :].rearrange("p x y b -> p x (y b)"),
                            conv_out[:, u % 2, i, :]).then_inc(conv_sent[u % 2], 16)

        def build_weights(engine, u, i):
            t, v = UNITS[u]
            gt = v * GU + i
            g = (gt // 2) * 6 + 2 * t + gt % 2
            if u >= CWR:
                engine.wait_ge(conv_mm, u - CWR + 1)
            engine.tensor_tensor(
                cw[:, u % CWR, i, :, :].rearrange("p k (o x) -> p k o x", x=HW),
                pw_in[:, :, g].unsqueeze(1).unsqueeze(3).broadcast_to([128, KS, G8, HW]),
                dw_band[:, :, g, :].unsqueeze(2).broadcast_to([128, KS, G8, HW]),
                ALU.mult).then_inc(cw_built[i % 2], 1)

        def chunk(t, c, n=CH):
            return t[:, c * n:(c + 1) * n]

        @block.sync
        def _(sp):
            for c in range(NCH):
                sp.dma_start(xs[:, c * CH:(c + 1) * CH].rearrange("p (b s) -> p b s", b=2),
                             x_v[:, 2 * c:2 * c + 2, :]).then_inc(x_in[c], 16)

            def rows_store(r):
                for c in range(NCH):
                    sp.wait_ge(rows_copied, NCH * r + c + 1)
                    sp.dma_start(tok_dram[r][c * CH:(c + 1) * CH, :].rearrange("(t p) c -> p t c", p=128),
                                 chunk(ln_sq, c).rearrange("p (t c) -> p t c", c=C)).then_inc(rows_out[r], 16)

            def y_load(r, NB):
                for i in range(RING):
                    sp.wait_ge(moe[r].scattered[i], 16 * ((NB - i + RING - 1) // RING))
                for c in range(NCH):
                    for k, dst in enumerate((xc, ln_sq)):
                        sp.dma_start(chunk(dst, c).rearrange("p (t c) -> p t c", c=C),
                                     y_dram[r][k * T + c * CH:k * T + (c + 1) * CH, :]
                                     .rearrange("(t p) c -> p t c", p=128)).then_inc(y_in[c], 16)

            sp.dma_start(dw_raw[:, :, :, :], w_dw.rearrange("(g i) a h w -> g (i a) h w", i=G8)).then_inc(qkv_in, 16)
            sp.dma_start(pw_raw[:, :, :], w_pw.rearrange("(g o) i h w -> g o (i h w)", o=G8)).then_inc(qkv_in, 16)
            sp.dma_start(wraw[:, W_P0:W_P1 + 1, :], w_proj.rearrange("o (a i) h w -> o a (i h w)", a=2))\
                .then_inc(w_in, 16)
            for i, v in enumerate((bn_gamma, bn_beta, bn_mean, bn_var, bq, bk, bv, bo)):
                sp.dma_start(wraw[i:i + 1, W_SM, :], v.rearrange("(a n) -> a n", a=1)).then_inc(w_in, 16)
            sp.dma_start(wraw[ROUT0:ROUT0 + E0, W_SM, :], gate_w).then_inc(w_in, 16)
            sp.dma_start(wraw[ROUT1:ROUT1 + E1, W_SM, :], router_w).then_inc(w_in, 16)
            sp.dma_start(wraw[B1ROW:SMROWS, W_SM, :], b1.rearrange("e (k p) -> (e k) p", p=128)).then_inc(w_in, 16)
            for i, w in ((W_AQ, wq), (W_AK, wk), (W_AV, wv), (W_AO, wo)):
                sp.dma_start(wraw[:, i, :], w).then_inc(w_in, 16)
            for n in range(len(UNITS) + MAPS_AHEAD):
                if n < len(UNITS):
                    t, v = UNITS[n]
                    sp.wait_ge(head_a, NCH * (n // UPT + 1))
                    for g in range(v * GU, (v + 1) * GU):
                        sp.dma_start(cmap[:, t, g, :],
                                     heads_raw[t][G8 * g:G8 * (g + 1), :, :, :].rearrange("p x y b -> p x (y b)"))\
                            .then_inc(map_in[n], 16)
                if n >= MAPS_AHEAD:
                    sp.wait_ge(conv_copied, n - MAPS_AHEAD + 1)
                    for i in (1, 3):
                        conv_send(sp, n - MAPS_AHEAD, i)
            sp.wait_ge(conv_mm, len(UNITS))
            sp.dma_start(w_up0[:, :].rearrange("p (e f) -> p e f", e=E0), w1.rearrange("e c f -> c e f"))\
                .then_inc(moe_w[0], 16)
            sp.dma_start(w_down0[:, :].rearrange("p (e h) -> p e h", h=C), w2.rearrange("e (k p) h -> p (e k) h", p=128))\
                .then_inc(moe_w[0], 16)
            sp.wait_ge(x1_ready, NCH)
            sp.dma_start(b2_all[:, :], b2.rearrange("(a e) f -> a (e f)", a=1).broadcast_to([128, E0 * C]))\
                .then_inc(moe_w[0], 16)
            rows_store(0)
            w_up1_v = w_up1[:, :].rearrange("p (e g f) -> p e g f", e=E1, g=2)
            w_down1_v = w_down1[:, :].rearrange("p (e k h) -> p e k h", e=E1, k=2)
            for i in range(W1_LOADS):
                es = slice(i * E1 // W1_LOADS, (i + 1) * E1 // W1_LOADS)
                sp.wait_ge(moe[0].turned, 4 * i + 4)
                sp.dma_start(w_up1_v[:, es, 0, :], gate_ws[es].rearrange("e c f -> c e f")).then_inc(moe_w[1], 16)
                sp.dma_start(w_up1_v[:, es, 1, :], up_ws[es].rearrange("e c f -> c e f")).then_inc(moe_w[1], 16)
                sp.dma_start(w_down1_v[:, es, :, :], down_ws[es].rearrange("e (k p) h -> p e k h", p=128))\
                    .then_inc(moe_w[1], 16)
            y_load(0, NB0)
            rows_store(1)
            y_load(1, NB1)
            for c in range(NCH):
                sp.wait_ge(x_moe, NCH + c + 1)
                sp.dma_start(out_v[:, 2 * c:2 * c + 2, :],
                             xs[:, c * CH:(c + 1) * CH].rearrange("p (b s) -> p b s", b=2)).then_inc(stored, 16)
            sp.wait_ge(stored, 16 * NCH)

        NLOADS = 1 + 8 + 3 + 4

        @block.gpsimd
        def _(pool):
            pool.memset(ident[:, :], 0.0).then_inc(norm_consts, 1)
            pool.memset(center[:, :], -1.0 / C).then_inc(norm_consts, 1)
            pool.memset(mean_w[:, :], 1.0 / C).then_inc(norm_consts, 1)
            pool.memset(ones[:, :], 1.0).then_inc(norm_consts, 1)
            for i, v in enumerate((LN_C_EPS, LN_T_EPS, BN_EPS)):
                pool.memset(eps[:, i:i + 1], v).then_inc(norm_consts, 1)
            pool.wait_ge(norm_consts, 7)
            pool.affine_select(out=ident[:, :], in_=ident[:, :], compare_op=ALU.not_equal, fill=1.0,
                               base=0, pattern=[[-1, 128]], channel_multiplier=1).then_inc(norm_consts, 1)
            pool.affine_select(out=center[:, :], in_=center[:, :], compare_op=ALU.not_equal, fill=1.0 - 1.0 / C,
                               base=0, pattern=[[-1, 128]], channel_multiplier=1).then_inc(norm_consts, 1)
            pool.memset(band[:, :, :, :], 0.0).then_inc(consts, 1)
            pool.memset(spread[:, :, :], 0.0).then_inc(consts, 1)
            pool.memset(dw_t[:, :, :], 0.0).then_inc(dw_zero, 1)
            pool.wait_ge(consts, 2)
            pool.affine_select(out=band[0:G8 * KS, :, :, :], in_=band[0:G8 * KS, :, :, :], compare_op=ALU.not_equal, fill=1.0,
                               base=-EDGE, pattern=[[1, HW], [-KS, G8], [-1, HW]], channel_multiplier=1)\
                .then_inc(consts, 1)
            pool.affine_select(out=spread[:, :, :], in_=spread[:, :, :], compare_op=ALU.not_equal, fill=1.0,
                               base=0, pattern=[[-1, G8], [0, HW]], channel_multiplier=1).then_inc(consts, 1)
            pool.wait_ge(consts, 4)
            pool.affine_select(out=band[0:G8 * KS, :, :, :], in_=band[0:G8 * KS, :, :, :], compare_op=ALU.is_ge, fill=0.0,
                               base=EDGE, pattern=[[-1, HW], [0, G8], [1, HW]], channel_multiplier=0)\
                .then_inc(consts, 1)
            pool.wait_ge(consts, 5)
            pool.affine_select(out=band[0:G8 * KS, :, :, :], in_=band[0:G8 * KS, :, :, :], compare_op=ALU.is_ge, fill=0.0,
                               base=KS - 1 - EDGE, pattern=[[1, HW], [0, G8], [-1, HW]], channel_multiplier=0)\
                .then_inc(consts, 1)
            pool.memset(blk16[:, :], 1.0).then_inc(att_consts, 1)
            pool.wait_ge(att_consts, 1)
            v = blk16[:, :].rearrange("p (g i) -> p g i", i=HD)
            pool.affine_select(out=v, in_=v, compare_op=ALU.is_ge, fill=0.0, base=0,
                               pattern=[[-HD, 128 // HD], [0, HD]], channel_multiplier=1).then_inc(att_consts, 1)
            pool.wait_ge(att_consts, 2)
            pool.affine_select(out=v, in_=v, compare_op=ALU.is_ge, fill=0.0, base=HD - 1,
                               pattern=[[HD, 128 // HD], [0, HD]], channel_multiplier=-1).then_inc(att_consts, 1)
            pool.memset(kvT[:, :, :, 128:129], 1.0).then_inc(kv_ones, 1)
            for e in range(E1):
                pool.memset(rank[:, e:e + 1], float(E1 - e)).then_inc(tables, 1)
            pool.memset(before[:, :], 1.0).then_inc(tables, 1)
            pool.wait_ge(tables, E1 + 1)
            pool.affine_select(out=before[:, :], in_=before[:, :], compare_op=ALU.is_gt, fill=0.0, base=0,
                               pattern=[[1, 128]], channel_multiplier=-1).then_inc(tables, 1)

            def table(out, pattern, base, step):
                pool.iota(out, pattern, base=base, channel_multiplier=step,
                          allow_small_or_imprecise_dtypes=True).then_inc(tables, 1)
            table(iota[:, :], [[1, 128]], 0, 0)
            table(pair_id[:, 0, :], [[128, TT]], 1, 1)
            table(pair_id[:, 1, :], [[-128, TT]], -1, -1)
            table(spare[:, :], [[128, NB1]], 2 * T, 1)
            table(col_id[:, :], [[0, 1]], 0, 1)
            pool.memset(ones16[:, :], 1.0).then_inc(tables, 1)
            for i in range(2):
                pool.memset(tsum[i][:, 0:SCAN, :], 0.0).then_inc(tables, 1)
                pool.memset(bsum[i][:, 0:SCAN], 0.0).then_inc(tables, 1)

            pool.wait_ge(band_out, 9)
            for u in range(len(UNITS)):
                for i in (0, 2):
                    build_weights(pool, u, i)

            def pair_values(r, NB):
                pool.wait_ge(rt_blocks, r + 1)
                pool.tensor_tensor(block_val[:, :, 0:NB], block_hot[:, :, 0:NB],
                                   pair_id[:, :, :].rearrange("p k t -> p (k t)").unsqueeze(2)
                                   .broadcast_to([128, 2 * TT, NB]), ALU.mult).then_inc(rt_value, 1)

            def moe_pool(r, NB):
                m = moe[r]
                LAG = RING - 1
                pool.wait_ge(rows_out[r], 16 * NCH)
                pool.wait_ge(rt_table, 3 * (r + 1))
                for j in range(NB + LAG):
                    if j < NB:
                        if j >= RING:
                            pool.wait_ge(m.turned, j - RING + 1)
                        pool.indirect_dma_start(
                            out=x_rows[:, j % RING, :], out_offset=None, in_=tok_dram[r],
                            in_offset=bass.IndirectOffsetOnAxis(ap=token[r][:, j:j + 1], axis=0))\
                            .then_inc(m.gathered[j % RING], 16)
                    if j >= LAG:
                        s = j - LAG
                        pool.wait_ge(m.y, s + 1)
                        pool.indirect_dma_start(
                            out=y_dram[r], in_=y_rows[:, s % RING, :], in_offset=None,
                            out_offset=bass.IndirectOffsetOnAxis(ap=dest[r][:, s:s + 1], axis=0))\
                            .then_inc(m.scattered[s % RING], 16)

            pair_values(0, NB0)
            moe_pool(0, NB0)
            pair_values(1, NB1)
            moe_pool(1, NB1)

        @block.scalar
        def _(act):
            def tile_rows(w):
                return w.rearrange("(h t d) k -> t h d k", t=3, d=HD)

            qkv_rows = tile_rows(w_qkv.rearrange("o i h w -> o (i h w)"))
            for t in ORDER:
                act.dma_start(wraw[:, W_Q + t, :], qkv_rows[t]).then_inc(qkv_in, 16)

            def load_table(func):
                act.activation(act_scratch[:, :], eps[:, 0:1], func)

            def ln_roots(n, e, between=None):
                load_table(ACT.Sqrt)
                for c in range(NCH):
                    act.wait_ge(ln_cent, NCH * n + c + 1)
                    act.activation(chunk(ln_sq, c), bank[c][:, :], ACT.Square).then_inc(ln_sqd, 1)
                if between:
                    between()
                for c in range(NCH):
                    act.wait_ge(ln_var, NCH * n + c + 1)
                    act.activation(ln_r[:, 0, 4 * c:4 * c + 4], bank[4 + c][:, 0:4], ACT.Sqrt,
                                   bias=eps[:, e:e + 1]).then_inc(ln_root, 1)

            act.wait_ge(norm_consts, 9)
            def turn_dw():
                act.wait_ge(qkv_in, 16 * 5)
                act.activation(dw_row[:, :, :, :].rearrange("g k i c -> g i k c"), dw_raw[:, :, :, :], ACT.Copy)\
                    .then_inc(dw_rows_in, 1)

            ln_roots(0, 0, turn_dw)

            def heads(n, t):
                for c in range(NCH):
                    act.wait_ge(qkv_mm, NCH * n + c + 1)
                    src = bank[c][:, :].rearrange("p (b y x) -> p b y x", b=2, y=HW)

                    def to(m):
                        return m[:, :, :, 2 * c:2 * c + 2].rearrange("p x y b -> p b y x")
                    if t == 0:
                        act.activation(to(q_relu), src, ACT.Relu).then_inc(q_relued, 1)
                    act.activation(to(heads_raw[t]), src, ACT.Copy).then_inc(head_a, 1)

            heads(0, ORDER[0])
            for k in range(9):
                act.wait_ge(band_mm, k + 1)
                if k < 8:
                    act.activation(dw_band[:, :, :, 2 * k:2 * k + 2].rearrange("p k g x -> p x (k g)"),
                                   bank[4 + k % 4][:, 0:2 * KS * NG].rearrange("p (x n) -> p x n", x=2),
                                   ACT.Copy).then_inc(band_out, 1)
                else:
                    act.activation(pw_in[:, :, :].rearrange("p o g -> p (o g)"), bank[4][:, 0:G8 * NG],
                                   ACT.Copy).then_inc(band_out, 1)
            for n in (1, 2):
                heads(n, ORDER[n])
            act.wait_ge(w_ready, 6)
            act.activation(bn[:, 0:1], vec("var"), ACT.Sqrt, bias=eps[:, 2:3]).then_inc(bn_step, 1)

            def kv_copy(h, b):
                i = h * B + b
                act.wait_ge(kv_turned, i + 1)
                if i >= 2:
                    act.wait_ge(kv_mm, i - 1)
                if i == 0:
                    act.wait_ge(kv_ones, 1)
                src = bank[2 + i % 2][:, :].rearrange("p (j q) -> p j q", j=4)
                act.activation(kvT[:, i % 2, 0:2, 0:128], src[:, 0:2, :], ACT.Relu)
                act.activation(kvT[:, i % 2, 2:4, 0:128], src[:, 2:4, :], ACT.Copy).then_inc(kv_copied, 1)

            def att_copy(h, b):
                i = h * B + b
                act.wait_ge(att_turned, i + 1)
                act.activation(att[h][:, b * S:(b + 1) * S].rearrange("p (y x) -> p x y", x=HW),
                               bank[4 + (i + 1) % 2][:, S:2 * S].rearrange("p (x y) -> p x y", x=HW),
                               ACT.Copy).then_inc(att_out, 1)

            for s in range(GU * len(UNITS)):
                if s in STEPS:
                    h, n = STEPS[s]
                    if n < B:
                        kv_copy(h, n)
                    if h == 0 and n >= 3:
                        att_copy(0, n - 3)
                if s % GU == GU - 1:
                    u = s // GU
                    act.wait_ge(conv_mm, u + 1)
                    if u >= 2:
                        act.wait_ge(conv_sent[u % 2], 16 * GU * (u // 2))
                    act.activation(conv_out[:, u % 2, :, :], bank[u % 2][:, :].rearrange("p (g n) -> p g n", g=GU),
                                   ACT.Relu if UNITS[u][0] == 0 else ACT.Copy).then_inc(conv_copied, 1)
                    act.wait_ge(conv_copied, u + 1)
                    for i in (0, 2):
                        conv_send(act, u, i)
            for b in range(B):
                att_copy(1, b)

            def router_exp(r):
                act.wait_ge(rt_diff, r + 1)
                act.activation(rv[:, 3, :], rv[:, 2, :], ACT.Exp).then_inc(rt_exp, 1)

            def token_rows(r):
                for c in range(NCH):
                    act.wait_ge(rows_mm, NCH * r + c + 1)
                    act.activation(chunk(ln_sq, c), bank[4 + c][:, :], ACT.Copy).then_inc(rows_copied, 1)

            def moe_act(r, NB):
                m = moe[r]
                load_table((ACT.Gelu_apprx_tanh, ACT.Silu)[r])
                for n in range(NB + 1):
                    if n < NB:
                        act.wait_ge(m.turned, n + 1)
                        if n >= 2:
                            act.wait_ge(m.up, n - 1)
                        act.activation(x_cols[:, n % 2, :], bank[n % 2][:, 0:128], ACT.Copy).then_inc(m.x_copied, 1)
                    if n >= 1:
                        j = n - 1
                        if r == 0:
                            act.wait_ge(m.h_in, j + 1)
                            if j >= 2:
                                act.wait_ge(m.down, j - 1)
                            act.activation(h_cols[:, j % 2, :], h_in[:, j % 2, :], ACT.Gelu_apprx_tanh)\
                                .then_inc(m.act, 1)
                        else:
                            act.wait_ge(m.up, j + 1)
                            if j >= 2:
                                act.wait_ge(m.h_in, j - 1)
                            act.activation(h_in[:, j % 2, 0:F1], bank[2 + j % 2][:, 0:F1], ACT.Silu)\
                                .then_inc(m.act, 1)

            def weigh_first(r):
                act.wait_ge(rt_weights, r + 1)
                for i in range(TT):
                    if i % 4 == 0:
                        act.wait_ge(y_in[i // 4], 32 * (r + 1))
                    act.activation(xc[:, i * 128:(i + 1) * 128], xc[:, i * 128:(i + 1) * 128], ACT.Copy,
                                   scale=pair_w[:, 0, i:i + 1]).then_inc(y_weighed, 1)

            ln_roots(1, 1)
            token_rows(0)
            router_exp(0)
            moe_act(0, NB0)
            weigh_first(0)

            ln_roots(2, 0)
            load_table(ACT.Exp)
            for c in range(NCH):
                for j, (dst, b) in enumerate(((sq_q, "bq"), (sq_k, "bk"))):
                    act.wait_ge(sq_qk_mm, 2 * c + j + 1)
                    act.activation(chunk(dst, c), bank[4 * j + c % 2][:, :], ACT.Identity,
                                   bias=vec(b)).then_inc(sq_qk_out, 1)
            for i in range(B + 2):
                if i < B:
                    st = sq_st[:, i % 3, :, :]
                    act.wait_ge(sq_max, i + 1)
                    act.activation(st[:, 1, :], st[:, 0, :], ACT.Copy, scale=-ATT_SCALE).then_inc(sq_nmax, 1)
                    act.wait_ge(sq_nmax, i + 1)
                    if i >= 3:
                        act.wait_ge(sq_norm, 2 * (i - 2))
                    for j in range(2):
                        act.activation(sq_p[:, i % 3, j, :], bank[i % 3][:, j * S:(j + 1) * S], ACT.Exp,
                                       bias=st[:, 1, j:j + 1], scale=ATT_SCALE,
                                       accum_out=st[:, 2, j:j + 1]).then_inc(sq_exp, 1)
                if i >= 2:
                    k = i - 2
                    act.wait_ge(sq_turned, k + 1)
                    if k >= 2:
                        act.wait_ge(sq_mm, k - 1)
                    act.activation(sq_pT[:, k % 2, :, :],
                                   bank[P_BANKS[k % 2]][:, :].rearrange("p (m n) -> p m n", m=2),
                                   ACT.Copy).then_inc(sq_copied, 1)

            ln_roots(3, 1)
            token_rows(1)
            router_exp(1)
            moe_act(1, NB1)
            weigh_first(1)

        @block.vector
        def _(dve):
            def ln_scale(n, between=None):
                for c in range(NCH):
                    dve.wait_ge(ln_sqd, NCH * n + c + 1)
                    dve.tensor_copy(chunk(xc, c), bank[c][:, :]).then_inc(ln_kept, 1)
                for c in range(NCH + 1):
                    if c == 2 and between:
                        between()
                    if c < NCH:
                        g = NCH * n + c
                        std, inv = (ln_r[:, i, 4 * c:4 * c + 4] for i in range(2))
                        dve.wait_ge(ln_root, g + 1)
                        dve.reciprocal(inv, std).then_inc(ln_inv, 1)
                        dve.wait_ge(ln_inv, 2 * g + 1)
                        if c >= 2:
                            dve.wait_ge(ln_spread, g - 1)
                        dve.tensor_tensor(ln_diag[:, c % 2, :, :],
                                          ident[:, :].unsqueeze(1).broadcast_to([128, 4, 128]),
                                          inv.unsqueeze(2).broadcast_to([128, 4, 128]), ALU.mult)\
                            .then_inc(ln_inv, 1)
                    if c >= 1:
                        g = NCH * n + c - 1
                        dve.wait_ge(ln_spread, g + 1)
                        dve.tensor_tensor(chunk(xn, c - 1), chunk(xc, c - 1), bank[3 + c][:, :], ALU.mult)\
                            .then_inc(ln_out, 1)

            dve.wait_ge(norm_consts, 9)
            def conv_weights():
                dve.wait_ge(w_turned, 1)
                dve.tensor_copy(wT[:, W_Q:W_V + 1, :], bank[0][:, 0:3 * 128].rearrange("p (j q) -> p j q", q=128))\
                    .then_inc(w_ready, 1)
                dve.wait_ge(dw_zero, 1)
                dve.tensor_copy(dw_t[0:G8 * KS, :, :].rearrange("p k g -> p (k g)"), bank[1][0:G8 * KS, 0:KS * NG])\
                    .then_inc(w_ready, 1)
                dve.tensor_copy(pw_t[:, :, :].rearrange("p o g -> p (o g)"), bank[2][0:G8, 0:G8 * NG])\
                    .then_inc(w_ready, 1)

            ln_scale(0, conv_weights)
            dve.wait_ge(w_turned, 2)
            dve.tensor_copy(wT[:, W_P0:W_P0 + 4, :], bank[6][:, :].rearrange("p (j q) -> p j q", q=128))\
                .then_inc(w_ready, 1)
            dve.tensor_copy(wT[:, W_AV:W_AO + 1, :], bank[7][:, 0:2 * 128].rearrange("p (j q) -> p j q", q=128))\
                .then_inc(w_ready, 1)
            dve.tensor_copy(wT[:, W_SM, 0:SMROWS], bank[7][:, 256:256 + SMROWS]).then_inc(w_ready, 1)

            def mask(h, b):
                i = h * B + b
                dve.wait_ge(kv_mm, i + 1)
                if h == 1:
                    dve.wait_ge(nd_mm, b + 1)
                kv = bank[4 + i % 2]
                dve.tensor_tensor(kvm[:, b, 0:128], kv[:, 0:128], blk16[:, :], ALU.mult)
                dve.tensor_scalar(kvm[:, b, 128:128 + NH], blk16[:, 0:128:HD], kv[:, 128:129], None,
                                  ALU.mult).then_inc(kv_masked, 1)

            def divide(h, b):
                i = h * B + b
                nd = bank[nd_bank(i)][:, 0:2 * (128 + NH)].rearrange("p (j n) -> p j n", j=2)
                d0, d1 = den[:, i % 2, 0, :, :], den[:, i % 2, 1, :, :]
                dve.wait_ge(nd_mm, i + 1)
                dve.tensor_scalar(d0, nd[:, :, 128:128 + NH], DIV_EPS, None, ALU.add).then_inc(den_step, 1)
                dve.wait_ge(den_step, 2 * i + 1)
                dve.reciprocal(d1, d0).then_inc(den_step, 1)
                dve.wait_ge(den_step, 2 * i + 2)
                if i >= 2:
                    dve.wait_ge(att_turned, i - 1)
                dve.tensor_tensor(att_rows[:, i % 2, :, :].rearrange("p j (h d) -> p j h d", d=HD),
                                  nd[:, :, 0:128].rearrange("p j (h d) -> p j h d", d=HD),
                                  d1.unsqueeze(3).broadcast_to([128, 2, NH, HD]), ALU.mult)\
                    .then_inc(att_div, 1)

            dve.wait_ge(band_out, 9)
            for u in range(CWR - 1):
                for i in (1, 3):
                    build_weights(dve, u, i)
            dve.wait_ge(att_consts, 3)
            for s in range(GU * len(UNITS)):
                if s % 2 == 1 and s // GU + CWR - 1 < len(UNITS):
                    build_weights(dve, s // GU + CWR - 1, s % GU)
                if s in STEPS:
                    h, n = STEPS[s]
                    if 0 <= n - 1 < B:
                        mask(h, n - 1)
                    if h == 0 and 0 <= n - 2 < B:
                        divide(0, n - 2)

            dve.wait_ge(bn_step, 1)
            dve.reciprocal(bn[:, 1:2], bn[:, 0:1]).then_inc(bn_step, 1)
            dve.wait_ge(bn_step, 2)
            dve.tensor_tensor(bn[:, 2:3], vec("gamma"), bn[:, 1:2], ALU.mult).then_inc(bn_step, 1)
            dve.wait_ge(bn_step, 3)
            dve.tensor_tensor(bn[:, 3:4], vec("mean"), bn[:, 2:3], ALU.mult).then_inc(bn_step, 1)
            dve.wait_ge(bn_step, 4)
            dve.tensor_tensor(bn[:, 3:4], vec("beta"), bn[:, 3:4], ALU.subtract).then_inc(bn_step, 1)
            dve.wait_ge(bn_step, 5)
            dve.tensor_scalar(xs[:, :], xs[:, :], bn[:, 3:4], None, ALU.add).then_inc(bn_step, 1)

            for n in range(B + 4):
                if n >= 5 and n % 2 == 1:
                    c = (n - 5) // 2
                    dve.wait_ge(proj_mm, c + 1)
                    if c == 0:
                        dve.wait_ge(bn_step, 6)
                    dve.scalar_tensor_tensor(out=chunk(xs, c), in0=bank[2 + c % 2][:, :], scalar=bn[:, 2:3],
                                             in1=chunk(xs, c), op0=ALU.mult, op1=ALU.add).then_inc(x1_ready, 1)
                if n < B:
                    divide(1, n)

            n_rt = [0]

            def step(ins):
                n_rt[0] += 1
                ins.then_inc(rt_chain, 1)
                dve.wait_ge(rt_chain, n_rt[0])

            def router(r, E, NB):
                l2, eq, oh1, oh2, sc = (t[:, :, 0:E] for t in rt)
                lg = bank[0][:, 0:TT * E].rearrange("p (t e) -> p t e", e=E)
                m1, m2, d, ex = (rv[:, i, :] for i in range(4))
                mx, sm = rv[:, 4, :], rv[:, 5, :]

                def per_e(v):
                    return v.unsqueeze(2).broadcast_to([128, TT, E])

                rk = rank[:, 0:E].unsqueeze(1).broadcast_to([128, TT, E])
                dve.wait_ge(rt_mm, NCH * (r + 1))
                if r == 0:
                    dve.wait_ge(tables, 12 + E1)
                for src, top, oh in ((lg, m1, oh1), (l2, m2, oh2)):
                    step(dve.tensor_reduce(top, src, AX.X, ALU.max))
                    step(dve.tensor_tensor(eq, src, per_e(top), ALU.is_equal))
                    step(dve.tensor_tensor(sc, eq, rk, ALU.mult))
                    step(dve.tensor_reduce(mx, sc, AX.X, ALU.max))
                    step(dve.tensor_tensor(oh, sc, per_e(mx), ALU.is_equal))
                    if oh is oh1:
                        step(dve.scalar_tensor_tensor(out=l2, in0=oh1, scalar=MASKED, in1=lg,
                                                      op0=ALU.mult, op1=ALU.add))
                dve.tensor_tensor(chosen[:, :, 0:E], oh1, oh2, ALU.add).then_inc(rt_mask, 1)
                dve.tensor_tensor(d, m2, m1, ALU.subtract).then_inc(rt_diff, 1)
                dve.wait_ge(rt_prefix, r + 1)
                prefix = bank[1][:, 0:TT * E].rearrange("p (t e) -> p t e", e=E)
                total = bank[1][:, TT * E:2 * TT * E].rearrange("p (t e) -> p t e", e=E)
                a, b = (t[:, :, 0:E] for t in tsum)
                step(dve.tensor_copy(a[:, SCAN:, :], total))
                for k in (1, 2, 4, 8):
                    step(dve.tensor_tensor(b[:, SCAN:, :], a[:, SCAN:, :], a[:, SCAN - k:SCAN + TT - k, :], ALU.add))
                    a, b = b, a
                step(dve.tensor_scalar(rcnt[:, 0, 0:E], a[:, SCAN + TT - 1, :], 127.0, None, ALU.add))
                step(dve.tensor_scalar(rcnt[:, 1, 0:E], rcnt[:, 0, 0:E], 7, None, ALU.arith_shift_right))
                u, v = bsum
                step(dve.tensor_copy(u[:, SCAN:SCAN + E], rcnt[:, 1, 0:E]))
                k = 1
                while k < E:
                    step(dve.tensor_tensor(v[:, SCAN:SCAN + E], u[:, SCAN:SCAN + E], u[:, SCAN - k:SCAN + E - k],
                                           ALU.add))
                    u, v, k = v, u, 2 * k
                step(dve.tensor_scalar(ended[:, 1:1 + E], u[:, SCAN:SCAN + E], col_id[:, :], None, ALU.is_le))
                dve.tensor_reduce(ended[:, 0:1], ended[:, 1:1 + E], AX.X, ALU.add).then_inc(rt_ended, 1)
                step(dve.tensor_tensor(l2, prefix, a[:, SCAN - 1:SCAN + TT - 1, :], ALU.add))
                step(dve.scalar_tensor_tensor(
                    out=l2, in0=u[:, SCAN - 1:SCAN + E - 1].unsqueeze(1).broadcast_to([128, TT, E]),
                    scalar=128.0, in1=l2, op0=ALU.mult, op1=ALU.add))
                dve.tensor_tensor(oh1, oh1, l2, ALU.mult).then_inc(rt_chain, 1)
                n_rt[0] += 1
                step(dve.tensor_tensor(oh2, oh2, l2, ALU.mult))
                dve.tensor_reduce(slot_f[:, 0, :], oh1, AX.X, ALU.add).then_inc(rt_chain, 1)
                n_rt[0] += 1
                step(dve.tensor_reduce(slot_f[:, 1, :], oh2, AX.X, ALU.add))
                step(dve.tensor_copy(slot_i[:, 0, :, :], slot_f[:, :, :]))
                step(dve.tensor_scalar(slot_i[:, 1, :, :], slot_i[:, 0, :, :], 127, None, ALU.bitwise_and))
                step(dve.tensor_scalar(slot_i[:, 2, :, :], slot_i[:, 0, :, :], 7, None, ALU.arith_shift_right))
                step(dve.tensor_copy(place[:, :, :, :], slot_i[:, 1:3, :, :]))

                def pairs(t, n):
                    return t.rearrange("p k t -> p (k t)").unsqueeze(2).broadcast_to([128, 2 * TT, n])

                def along(n):
                    return iota[:, 0:n].unsqueeze(1).broadcast_to([128, 2 * TT, n])

                dve.tensor_tensor(block_hot[:, :, 0:NB], along(NB), pairs(place[:, 1, :, :], NB), ALU.is_equal)\
                    .then_inc(rt_blocks, 1)
                for k in range(2):
                    dve.tensor_tensor(place_hot[:, k * TT:(k + 1) * TT, :],
                                      iota[:, :].unsqueeze(1).broadcast_to([128, TT, 128]),
                                      place[:, 0, k, :].unsqueeze(2).broadcast_to([128, TT, 128]),
                                      ALU.is_equal).then_inc(rt_place, 1)
                dve.wait_ge(rt_expert, r + 1)
                dve.tensor_scalar(expert[r][:, :], bank[0][0:1, 0:NB], float(E - 1), None, ALU.min)\
                    .then_inc(rt_table, 1)
                dve.wait_ge(rt_inverse, r + 1)
                s = bank[2][:, 0:NB]
                second, v, free = (taken[:, i, 0:NB] for i in range(3))
                step(dve.tensor_scalar(second, s, 0.0, float(T), ALU.is_lt, ALU.mult))
                step(dve.tensor_tensor(v, second, s, ALU.subtract))
                step(dve.tensor_tensor(v, v, s, ALU.max))
                step(dve.scalar_tensor_tensor(out=free, in0=v, scalar=0.0, in1=spare[:, 0:NB],
                                              op0=ALU.is_equal, op1=ALU.mult))
                dve.scalar_tensor_tensor(out=dest[r][:, :], in0=v, scalar=-1.0, in1=free,
                                         op0=ALU.add, op1=ALU.max).then_inc(rt_table, 1)
                dve.wait_ge(rt_table, 3 * r + 2)
                dve.tensor_scalar(token[r][:, :], dest[r][:, :], T - 1, None, ALU.bitwise_and)\
                    .then_inc(rt_table, 1)
                dve.wait_ge(rt_exp, r + 1)
                step(dve.tensor_scalar(sm, ex, 1.0, None, ALU.add))
                step(dve.reciprocal(pair_w[:, 0, :], sm))
                dve.tensor_tensor(pair_w[:, 1, :], ex, pair_w[:, 0, :], ALU.mult).then_inc(rt_weights, 1)

            def moe_vector(r, E, NB, w_up):
                m = moe[r]
                UP = (F0, 2 * F1)[r]
                dve.wait_ge(moe_w[r], 16 * (3, 3 * W1_LOADS)[r])
                e = {}
                for n in range(NB + 3):
                    if n < NB:
                        j = n
                        e[j] = dve.value_load(expert[r][0:1, j:j + 1], min_val=0, max_val=E - 1)
                        if j >= 3:
                            dve.wait_ge(m.up, j - 2)
                        dve.tensor_copy(w_block[:, j % 3, :], w_up[:, bass.ds(e[j] * UP, UP)]).then_inc(m.w, 1)
                    if 0 <= n - 1 < NB:
                        j = n - 1
                        if r == 0:
                            dve.wait_ge(m.up, j + 1)
                            if j >= 2:
                                dve.wait_ge(m.act, j - 1)
                            dve.tensor_tensor(h_in[:, j % 2, :].rearrange("p (k s) -> p k s", k=M0),
                                              bank[2 + j % 2][:, :].rearrange("p (k s) -> p k s", k=M0),
                                              wT[:, W_SM, bass.ds(e[j] * M0 + B1ROW, M0)].unsqueeze(2)
                                              .broadcast_to([128, M0, 128]), ALU.add).then_inc(m.h_in, 1)
                        else:
                            dve.wait_ge(m.act, j + 1)
                            if j >= 2:
                                dve.wait_ge(m.down, j - 1)
                            dve.tensor_tensor(h_cols[:, j % 2, 0:F1], h_in[:, j % 2, 0:F1],
                                              bank[2 + j % 2][:, F1:2 * F1], ALU.mult).then_inc(m.h_in, 1)
                    if n >= 3:
                        j = n - 3
                        ej = e.pop(j)
                        dve.wait_ge(m.down, j + 1)
                        if j >= RING:
                            dve.wait_ge(m.scattered[j % RING], 16 * (j // RING))
                        if r == 0:
                            ins = dve.tensor_tensor(y_rows[:, j % RING, :], bank[6 + j % 2][:, 0:C],
                                                    b2_all[:, bass.ds(ej * C, C)], ALU.add)
                        else:
                            ins = dve.tensor_copy(y_rows[:, j % RING, :], bank[6 + j % 2][:, 0:C])
                        ins.then_inc(m.y, 1)

            def moe_sum(r):
                dve.wait_ge(rt_weights, r + 1)
                for c in range(NCH + 1):
                    for i in range(4 * c, min(4 * c + 4, TT)):
                        rows = slice(i * 128, (i + 1) * 128)
                        dve.wait_ge(y_weighed, TT * r + i + 1)
                        dve.scalar_tensor_tensor(out=xc[:, rows], in0=ln_sq[:, rows], scalar=pair_w[:, 1, i:i + 1],
                                                 in1=xc[:, rows], op0=ALU.mult, op1=ALU.add).then_inc(y_added, 1)
                    if c >= 1:
                        dve.wait_ge(y_turned, NCH * r + c)
                        dve.tensor_tensor(chunk(xs, c - 1), chunk(xs, c - 1), bank[c - 1][:, :], ALU.add)\
                            .then_inc(x_moe, 1)

            ln_scale(1)
            router(0, E0, NB0)
            moe_vector(0, E0, NB0, w_up0)
            moe_sum(0)

            ln_scale(2)
            for g in range(4):
                dve.wait_ge(sq_v_mm, g + 1)
                dve.tensor_copy(sq_vT[:, 4 * g:4 * g + 4, :],
                                bank[V_BANKS[g]][:, :].rearrange("p (j q) -> p j q", j=4)).then_inc(sq_v_out, 1)
            for i in range(B + 6):
                if i < B:
                    dve.wait_ge(sq_s, i + 1)
                    dve.tensor_reduce(sq_st[:, i % 3, 0, :], bank[i % 3][:, :].rearrange("p (j m) -> p j m", j=2),
                                      AX.X, ALU.max).then_inc(sq_max, 1)
                if 1 <= i <= B:
                    k = i - 1
                    st = sq_st[:, k % 3, :, :]
                    dve.wait_ge(sq_exp, 2 * k + 2)
                    dve.reciprocal(st[:, 3, :], st[:, 2, :]).then_inc(sq_inv, 1)
                    dve.wait_ge(sq_inv, k + 1)
                    if k >= 2:
                        dve.wait_ge(sq_turned, k - 1)
                    for j in range(2):
                        dve.tensor_scalar(sq_pn[:, k % 2, j, :], sq_p[:, k % 3, j, :],
                                          st[:, 3, j:j + 1], None, ALU.mult).then_inc(sq_norm, 1)
                if 3 <= i < B + 3:
                    k = i - 3
                    dve.wait_ge(sq_mm, k + 1)
                    dve.tensor_scalar(sq_o[:, k, :], bank[4 + k % 2][:, 0:S], vec("bv"), None, ALU.add)\
                        .then_inc(sq_out, 1)
                if i >= 7 and i % 2 == 1:
                    c = (i - 7) // 2
                    dve.wait_ge(wo_mm, c + 1)
                    dve.scalar_tensor_tensor(out=chunk(xs, c), in0=bank[7][:, :], scalar=vec("bo"),
                                             in1=chunk(xs, c), op0=ALU.add, op1=ALU.add).then_inc(x3_ready, 1)

            ln_scale(3)
            router(1, E1, NB1)
            moe_vector(1, E1, NB1, w_up1)
            moe_sum(1)

        @block.tensor
        def _(pe):
            pe.wait_ge(norm_consts, 9)

            def keep_clock(b, n):
                for _ in range(n):
                    pe.matmul(bank[b][:, :], ident[:, :], ones[:, :].unsqueeze(1).broadcast_to([128, 4, 128]),
                              start=True, stop=True)

            def layer_norm(n, ready, before=None, between=None, after=None):
                for c in range(NCH + 1):
                    if before and c < NCH:
                        before(c)
                    if c >= 1:
                        pe.wait_ge(*ready(c - 1))
                        pe.matmul(bank[c - 1][:, :], center[:, :], chunk(xs, c - 1), start=True, stop=True)\
                            .then_inc(ln_cent, 1)
                LAG = 2
                for s in range(NCH + LAG + 1):
                    if s < NCH:
                        pe.wait_ge(ln_sqd, NCH * n + s + 1)
                        for i in range(4):
                            mm = pe.matmul(bank[4 + s][:, i:i + 1], ln_sq[:, (4 * s + i) * 128:(4 * s + i + 1) * 128],
                                           mean_w[:, :], start=True, stop=True)
                        mm.then_inc(ln_var, 1)
                    if s == 2 and between:
                        between()
                    c = s - LAG
                    if c == 0:
                        keep_clock(7, 1)
                    if 0 <= c < NCH:
                        pe.wait_ge(ln_inv, 2 * (NCH * n + c) + 2)
                        pe.matmul(bank[4 + c][:, :], ones[:, :],
                                  ln_diag[:, c % 2, :, :].rearrange("p j q -> p (j q)"),
                                  start=True, stop=True).then_inc(ln_spread, 1)
                    if after and 0 <= c - 1:
                        pe.wait_ge(ln_out, NCH * n + c)
                        after(c - 1)

            def turn_weights():
                pe.wait_ge(qkv_in, 16 * 5)
                pe.wait_ge(ln_kept, 3)
                pe.wait_ge(dw_rows_in, 1)
                for i in range(3):
                    pe.transpose(bank[0][:, i * 128:(i + 1) * 128], wraw[:, W_Q + i, :], ident[:, :])
                for k in range(KS):
                    pe.transpose(bank[1][0:G8 * KS, k * NG:(k + 1) * NG],
                                 dw_row[:, k, :, :].rearrange("g i c -> g (i c)"), ident[0:NG, 0:NG])
                for o in range(G8):
                    mm = pe.transpose(bank[2][0:G8, o * NG:(o + 1) * NG], pw_raw[:, o, :], ident[0:NG, 0:NG])
                mm.then_inc(w_turned, 1)

            def head(n, c):
                if n == 0:
                    pe.wait_ge(w_ready, 3)
                else:
                    pe.wait_ge(head_a, NCH * (n - 1) + c + 1)
                pe.matmul(bank[c][:, :], wT[:, W_Q + ORDER[n], :], chunk(xn, c), start=True, stop=True)\
                    .then_inc(qkv_mm, 1)

            layer_norm(0, lambda c: (x_in[c], 16), between=turn_weights, after=lambda c: head(0, c))

            pe.wait_ge(consts, 6)
            for k in range(8):
                if k >= 4:
                    pe.wait_ge(band_out, k - 3)
                for j in range(2):
                    x = 2 * k + j
                    mm = pe.matmul(bank[4 + k % 4][:, j * KS * NG:(j + 1) * KS * NG],
                                   band[:, x, :, :].rearrange("p i x -> p (i x)"),
                                   dw_t[:, :, :].rearrange("p k g -> p (k g)"), start=True, stop=True)
                mm.then_inc(band_mm, 1)
            pe.wait_ge(band_out, 5)
            pe.matmul(bank[4][:, 0:G8 * NG], spread[:, :, :].rearrange("p i x -> p (i x)"),
                      pw_t[:, :, :].rearrange("p o g -> p (o g)"), start=True, stop=True).then_inc(band_mm, 1)
            for n in (1, 2):
                for c in range(NCH):
                    head(n, c)
            pe.wait_ge(w_in, 16 * NLOADS)
            pe.wait_ge(band_out, 9)
            for i in range(6):
                pe.transpose(bank[6 + i // 4][:, (i % 4) * 128:(i % 4 + 1) * 128], wraw[:, W_P0 + i, :], ident[:, :])
            pe.transpose(bank[7][:, 256:256 + SMROWS], wraw[0:SMROWS, W_SM, :], ident[0:SMROWS, 0:SMROWS])\
                .then_inc(w_turned, 1)

            def turn_kv(h, b):
                i = h * B + b
                if i >= 2:
                    pe.wait_ge(kv_copied, i - 1)
                for j in range(4):
                    kv = (heads_raw, heads_agg)[h][1 + j // 2]
                    mm = pe.transpose(bank[2 + i % 2][:, j * 128:(j + 1) * 128],
                                      kv[:, (j % 2) * 8:(j % 2) * 8 + 8, :, b], ident[:, :])
                mm.then_inc(kv_turned, 1)

            def kv_product(h, b):
                i = h * B + b
                pe.wait_ge(kv_copied, i + 1)
                if i >= 2:
                    pe.wait_ge(kv_masked, i - 1)
                if i >= 3:
                    pe.wait_ge(att_out, min(i - 2, B))
                for j in range(2):
                    mm = pe.matmul(bank[4 + i % 2][:, 0:129], kvT[:, i % 2, j, 0:128],
                                   kvT[:, i % 2, 2 + j, 0:129], start=(j == 0), stop=(j == 1))
                mm.then_inc(kv_mm, 1)

            def num_den(h, b):
                i = h * B + b
                pe.wait_ge(kv_masked, i + 1)
                if i in (B + 2, B + 3):
                    pe.wait_ge(conv_copied, len(UNITS))
                elif i >= 2:
                    pe.wait_ge(att_div, i - 1 if i < B + 2 else i - 3)
                n = 128 + NH
                for j in range(2):
                    mm = pe.matmul(bank[nd_bank(i)][:, j * n:(j + 1) * n],
                                   (q_relu, heads_agg[0])[h][:, 8 * j:8 * j + 8, :, b], kvm[:, b, :],
                                   start=True, stop=True)
                mm.then_inc(nd_mm, 1)

            def turn_rows(h, b):
                i = h * B + b
                pe.wait_ge(att_div, i + 1)
                pe.wait_ge(kv_masked, min(i + 2, (h + 1) * B))
                if i >= 2:
                    pe.wait_ge(att_out, i - 1)
                for j in range(2):
                    mm = pe.transpose(bank[4 + (i + 1) % 2][:, S + j * 128:S + (j + 1) * 128],
                                      att_rows[:, i % 2, j, :], ident[:, :])
                mm.then_inc(att_turned, 1)

            stages = (turn_kv, kv_product, num_den, turn_rows)
            pe.wait_ge(head_a, 3 * NCH)
            pe.wait_ge(q_relued, NCH)
            pe.wait_ge(w_ready, 6)
            for s in range(GU * len(UNITS)):
                if s in STEPS:
                    h, n = STEPS[s]
                    if (h, n) == (1, 0):
                        for i in range(2):
                            pe.wait_ge(conv_sent[i], 16 * GU * UPT)
                    for lag, stage in enumerate(stages[0:4 if h == 0 else 2]):
                        if 0 <= n - lag < B:
                            stage(h, n - lag)
                u, i = s // GU, s % GU
                t, v = UNITS[u]
                if i == 0:
                    pe.wait_ge(map_in[u], 16 * GU)
                    if u >= 2:
                        pe.wait_ge(conv_copied, u - 1)
                pe.wait_ge(cw_built[i % 2], 2 * u + i // 2 + 1)
                for k in (2, 1, 3, 0, 4):
                    y0, y1 = max(0, EDGE - k), min(HW, HW + EDGE - k)
                    mm = pe.matmul(bank[u % 2][:, i * 128 + y0 * B:i * 128 + y1 * B], cw[:, u % CWR, i, k, :],
                                   cmap[:, t, v * GU + i, (y0 + k - EDGE) * B:(y1 + k - EDGE) * B],
                                   start=(k == EDGE), stop=(k == 4))
                if i == GU - 1:
                    mm.then_inc(conv_mm, 1)
            for i in range(2):
                pe.wait_ge(conv_sent[i], 16 * GU * len(UNITS) // 2)
            for n in range(B + 3):
                if n < B:
                    num_den(1, n)
                if 2 <= n < B + 2:
                    turn_rows(1, n - 2)
                if n >= 4 and n % 2 == 0:
                    c = (n - 4) // 2
                    pe.wait_ge(att_out, B + 2 * c + 2)
                    if c >= 2:
                        pe.wait_ge(x1_ready, c - 1)
                    for h in range(2):
                        mm = pe.matmul(bank[2 + c % 2][:, :], wT[:, W_P0 + h, :], chunk(att[h], c),
                                       start=(h == 0), stop=(h == 1))
                    mm.then_inc(proj_mm, 1)

            def logits(E, row):
                def product(c):
                    for i in range(4 * c, 4 * c + 4):
                        mm = pe.matmul(bank[0][:, i * E:(i + 1) * E], xn[:, i * 128:(i + 1) * 128],
                                       wT[:, W_SM, row:row + E], start=True, stop=True)
                    mm.then_inc(rt_mm, 1)
                return product

            def token_rows():
                for c in range(NCH):
                    for i in range(4):
                        mm = pe.transpose(bank[4 + c][:, i * 128:(i + 1) * 128],
                                          xn[:, (4 * c + i) * 128:(4 * c + i + 1) * 128], ident[:, :])
                    mm.then_inc(rows_mm, 1)

            def slots(r, E, NB):
                n = TT * E
                pe.wait_ge(rt_mask, r + 1)
                mask = chosen[:, :, 0:E]
                pe.matmul(bank[1][:, 0:n].rearrange("p (t e) -> p t e", e=E), before[:, :], mask,
                          start=True, stop=True)
                pe.matmul(bank[1][:, n:2 * n].rearrange("p (t e) -> p t e", e=E), ones16[:, :], mask,
                          start=True, stop=True).then_inc(rt_prefix, 1)
                pe.wait_ge(rt_ended, r + 1)
                pe.transpose(bank[0][0:1, 0:128], ended[:, 0:1], ident[:, :]).then_inc(rt_expert, 1)
                pe.wait_ge(rt_blocks, r + 1)
                keep_clock(3, 2)
                pe.wait_ge(rt_value, r + 1)
                for i in range(2 * TT):
                    if i % TT == 0:
                        pe.wait_ge(rt_place, 2 * r + i // TT + 1)
                    mm = pe.matmul(bank[2][:, 0:NB], place_hot[:, i, :], block_val[:, i, 0:NB],
                                   start=(i == 0), stop=(i == 2 * TT - 1))
                mm.then_inc(rt_inverse, 1)
                keep_clock(3, 2)

            def moe_tensor(r, E, NB, w_down):
                m = moe[r]
                K = (M0, 2)[r]
                UP = (F0, 2 * F1)[r]
                pe.wait_ge(rt_table, 3 * (r + 1))
                pe.wait_ge(moe_w[r], 16 * (3, 3 * W1_LOADS)[r])
                pe.wait_ge(rows_copied, NCH * (r + 1))
                for n in range(NB + 3):
                    if n < NB:
                        pe.wait_ge(m.gathered[n % RING], 16 * (n // RING) + 16)
                        if n >= 2:
                            pe.wait_ge(m.x_copied, n - 1)
                        pe.transpose(bank[n % 2][:, 0:128], x_rows[:, n % RING, :], ident[:, :]).then_inc(m.turned, 1)
                    if 0 <= n - 1 < NB:
                        j = n - 1
                        pe.wait_ge(m.w, j + 1)
                        pe.wait_ge(m.x_copied, j + 1)
                        if j >= 2:
                            pe.wait_ge(m.h_in, j - 1)
                        for i in range(UP // 128):
                            mm = pe.matmul(bank[2 + j % 2][:, i * 128:(i + 1) * 128],
                                           w_block[:, j % 3, i * 128:(i + 1) * 128], x_cols[:, j % 2, :],
                                           start=True, stop=True)
                        mm.then_inc(m.up, 1)
                    if n >= 3:
                        j = n - 3
                        e = pe.value_load(expert[r][0:1, j:j + 1], min_val=0, max_val=E - 1)
                        pe.wait_ge((m.act, m.h_in)[r], j + 1)
                        if j >= 2:
                            pe.wait_ge(m.y, j - 1)
                        for i in range(K):
                            mm = pe.matmul(bank[6 + j % 2][:, 0:C], h_cols[:, j % 2, i * 128:(i + 1) * 128],
                                           w_down[:, bass.ds(e * (K * C) + i * C, C)],
                                           start=(i == 0), stop=(i == K - 1))
                        mm.then_inc(m.down, 1)

            def y_columns(r):
                def turn(c):
                    if c == 0 and r == 0:
                        pe.wait_ge(y_in[0], 32)
                        keep_clock(7, 2)
                    pe.wait_ge(y_added, TT * r + 4 * c + 4)
                    for i in range(4):
                        mm = pe.transpose(bank[c][:, i * 128:(i + 1) * 128],
                                          xc[:, (4 * c + i) * 128:(4 * c + i + 1) * 128], ident[:, :])
                    mm.then_inc(y_turned, 1)
                return turn

            layer_norm(1, lambda c: (x1_ready, c + 1), after=logits(E0, ROUT0))
            token_rows()
            slots(0, E0, NB0)
            moe_tensor(0, E0, NB0, w_down0)

            def queries_keys(c):
                for j in range(2):
                    if c >= 2:
                        pe.wait_ge(sq_qk_out, 2 * (c - 2) + j + 1)
                    pe.matmul(bank[4 * j + c % 2][:, :], wT[:, W_AQ + j, :], chunk(xn, c),
                              start=True, stop=True).then_inc(sq_qk_mm, 1)

            layer_norm(2, lambda c: (x_moe, c + 1), before=y_columns(0), after=queries_keys)
            for g in range(4):
                for j in range(4):
                    i = 4 * g + j
                    mm = pe.matmul(bank[V_BANKS[g]][:, j * 128:(j + 1) * 128], xn[:, i * 128:(i + 1) * 128],
                                   wT[:, W_AV, :], start=True, stop=True)
                mm.then_inc(sq_v_mm, 1)

            def scores(b):
                if b == 0:
                    pe.wait_ge(sq_qk_out, 2 * NCH)
                if b == 2:
                    pe.wait_ge(sq_v_out, 4)
                if b >= 3:
                    pe.wait_ge(sq_exp, 2 * (b - 2))
                for j in range(2):
                    mm = pe.matmul(bank[b % 3][:, j * S:(j + 1) * S],
                                   sq_q[:, b * S + j * 128:b * S + (j + 1) * 128],
                                   sq_k[:, b * S:(b + 1) * S], start=True, stop=True)
                mm.then_inc(sq_s, 1)

            def turn_p(b):
                pe.wait_ge(sq_norm, 2 * (b + 1))
                if b >= 2:
                    pe.wait_ge(sq_copied, b - 1)
                for j in range(2):
                    for m in range(2):
                        mm = pe.transpose(bank[P_BANKS[b % 2]][:, m * S + j * 128:m * S + (j + 1) * 128],
                                          sq_pn[:, b % 2, j, m * 128:(m + 1) * 128], ident[:, :])
                mm.then_inc(sq_turned, 1)

            def weigh_v(b):
                pe.wait_ge(sq_copied, b + 1)
                if b == 0:
                    pe.wait_ge(sq_v_out, 4)
                if b >= 2:
                    pe.wait_ge(sq_out, b - 1)
                for m in range(2):
                    mm = pe.matmul(bank[4 + b % 2][:, 0:S], sq_vT[:, 2 * b + m, :], sq_pT[:, b % 2, m, :],
                                   start=(m == 0), stop=(m == 1))
                mm.then_inc(sq_mm, 1)

            for i in range(B + 5):
                if i < B:
                    scores(i)
                if 2 <= i < B + 2:
                    turn_p(i - 2)
                if 3 <= i < B + 3:
                    weigh_v(i - 3)
                if i >= 6 and i % 2 == 0:
                    c = (i - 6) // 2
                    pe.wait_ge(sq_out, 2 * c + 2)
                    if c >= 1:
                        pe.wait_ge(x3_ready, c)
                    pe.matmul(bank[7][:, :], wT[:, W_AO, :],
                              sq_o[:, 2 * c:2 * c + 2, :].rearrange("p b s -> p (b s)"), start=True, stop=True)\
                        .then_inc(wo_mm, 1)
            layer_norm(3, lambda c: (x3_ready, c + 1), after=logits(E1, ROUT1))
            token_rows()
            slots(1, E1, NB1)
            moe_tensor(1, E1, NB1, w_down1)
            for c in range(NCH):
                y_columns(1)(c)


_INS = ['x', 'L0_conv_w_qkv', 'L0_conv_w_dw', 'L0_conv_w_pw', 'L0_conv_w_proj', 'L0_conv_bn_gamma',
        'L0_conv_bn_beta', 'L0_conv_bn_mean', 'L0_conv_bn_var', 'L0_ffn_gate_w', 'L0_ffn_w1', 'L0_ffn_b1',
        'L0_ffn_w2', 'L0_ffn_b2', 'L1_conv_wq', 'L1_conv_bq', 'L1_conv_wk', 'L1_conv_bk', 'L1_conv_wv',
        'L1_conv_bv', 'L1_conv_wo', 'L1_conv_bo', 'L1_ffn_router_w', 'L1_ffn_gate_w', 'L1_ffn_up_w',
        'L1_ffn_down_w']


def kernel(**inputs):
    import numpy as _np
    import concourse.bacc as _bacc
    from concourse import mybir as _mybir
    from concourse.bass_utils import run_bass_kernel_spmd as _run

    nc = _bacc.Bacc("TRN2", target_bir_lowering=False, num_devices=1)
    arrays, args = {}, []
    for name in _INS:
        a = _np.ascontiguousarray(inputs[name])
        arrays[f"in_{name}_dram"] = a
        args.append(nc.dram_tensor(f"in_{name}_dram", a.shape, _mybir.dt.from_np(a.dtype), kind="ExternalInput").ap())
    args.append(nc.dram_tensor("out_dram", (B, C, HW, HW), F32, kind="ExternalOutput").ap())
    metaformer(nc, *args)
    r = _run(nc, [arrays], core_ids=[0])
    return r.results[0]["out_dram"]
```
